# Optimizing a Trainium2 kernel written in Bass

```python
import numpy as np
import jax
import jax.numpy as jnp

def _softmax(x, axis=-1):
    return jax.nn.softmax(x, axis=axis)

def _gelu(x):
    return jax.nn.gelu(x, approximate=True)

def _silu(x):
    return jax.nn.silu(x)

def _sigmoid(x):
    return jax.nn.sigmoid(x)

def _layernorm(x, axis=-1, eps=1e-05):
    m = jnp.mean(x, axis=axis, keepdims=True)
    v = jnp.var(x, axis=axis, keepdims=True)
    return (x - m) / jnp.sqrt(v + eps)

def _scatter_add(tgt, idx, src, axis=0):
    return tgt.at[idx].add(src)

def _segment_sum(src, seg, n):
    return jax.ops.segment_sum(src, seg, n)
kernel_name = 'mk_xattn_ffn_d2_seqx_r2_c64dcc'

def setup_inputs(seed: int=0):
    np.random.seed(seed)
    _w = jnp.asarray

    def _rec_inputs():
        import jax
        import jax.numpy as jnp
        _rk = jax.random.key(seed)
        x = -0.0002928 + 1 * jax.random.normal(jax.random.fold_in(_rk, 1), (8, 512, 512), jnp.float32)
        _lenS = 512 - jax.random.randint(jax.random.fold_in(_rk, 7), (8,), 0, max(1, 512 // 4) + 1, jnp.int32)
        _lenS2 = 512 - jax.random.randint(jax.random.fold_in(_rk, 8), (8,), 0, max(1, 512 // 4) + 1, jnp.int32)
        _ctx_1024P = jax.random.normal(jax.random.fold_in(_rk, 11), (8, 16, 512), jnp.float32)
        _ctx_1024c = jax.random.dirichlet(jax.random.fold_in(_rk, 511), 0.3 * jnp.ones((16,), jnp.float32), (8, 512))
        _ctx_1024t = jnp.einsum('bsk,bkd->bsd', _ctx_1024c, _ctx_1024P)
        _ctx_1024t = _ctx_1024t * jax.lax.rsqrt(jnp.mean(jnp.square(_ctx_1024t)) + 1e-12) * 0.953939
        ctx_1024 = -1.39393e-06 + 0.999914 * (_ctx_1024t + 0.3 * jax.random.normal(jax.random.fold_in(_rk, 611), (8, 512, 512), jnp.float32))
        _validS = jnp.arange(512)[None, :] < _lenS[:, None]
        _validS2 = jnp.arange(512)[None, :] < _lenS2[:, None]
        _causal = jnp.tril(jnp.ones((512, 512), dtype=bool))
        mask_BxS2_bk0 = jnp.logical_not(jnp.broadcast_to(_validS2[:, :], (8, 512)))
        return (x, ctx_1024, mask_BxS2_bk0)
    x, ctx_1024, mask_BxS2_bk0 = _rec_inputs()

    def _L0_xattn_setup():
        import jax, jax.numpy as jnp
        import numpy as np
        D_MODEL = 512
        N_HEADS = 16
        D_K = D_MODEL // N_HEADS
        key = jax.random.key(seed)
        ks = jax.random.split(key, 11)
        B, L, S = (2, 1024, 1024)
        scale = 1.0 / np.sqrt(D_MODEL)
        return {'x_q': jax.random.normal(ks[0], (B, L, D_MODEL), jnp.float32), 'x_k': jax.random.normal(ks[1], (B, S, D_MODEL), jnp.float32), 'x_v': jax.random.normal(ks[2], (B, S, D_MODEL), jnp.float32), 'W_Q': jax.random.normal(ks[3], (D_MODEL, D_MODEL), jnp.float32) * scale, 'b_Q': jax.random.normal(ks[4], (D_MODEL,), jnp.float32) * 0.01, 'W_K': jax.random.normal(ks[5], (D_MODEL, D_MODEL), jnp.float32) * scale, 'b_K': jax.random.normal(ks[6], (D_MODEL,), jnp.float32) * 0.01, 'W_V': jax.random.normal(ks[7], (D_MODEL, D_MODEL), jnp.float32) * scale, 'b_V': jax.random.normal(ks[8], (D_MODEL,), jnp.float32) * 0.01, 'W_O': jax.random.normal(ks[9], (D_MODEL, D_MODEL), jnp.float32) * scale, 'b_O': jax.random.normal(ks[10], (D_MODEL,), jnp.float32) * 0.01}
    _L0_xattn_all = _L0_xattn_setup()
    _L0_xattn_in = {k: v for k, v in _L0_xattn_all.items() if k in ('W_Q', 'b_Q', 'W_K', 'b_K', 'W_V', 'b_V', 'W_O', 'b_O')}
    del _L0_xattn_all

    def _L0_ffn_setup():
        import jax, jax.numpy as jnp
        import numpy as np
        EPS = 1e-05

        def rmsnorm(x):
            return x * jax.lax.rsqrt(jnp.mean(x * x, axis=-1, keepdims=True) + EPS)

        def act_quant(x):
            scale = 127.0 / jnp.clip(jnp.max(jnp.abs(x), axis=-1, keepdims=True), 1e-05)
            q = jnp.clip(jnp.round(x * scale), -128.0, 127.0) / scale
            return x + jax.lax.stop_gradient(q - x)

        def weight_quant(w):
            scale = 1.0 / jnp.clip(jnp.mean(jnp.abs(w)), 1e-05)
            q = jnp.clip(jnp.round(w * scale), -1.0, 1.0) / scale
            return w + jax.lax.stop_gradient(q - w)

        def bitlinear(x, w, b):
            xq = act_quant(rmsnorm(x))
            wq = weight_quant(w)
            return jnp.einsum('bsd,fd->bsf', xq, wq) + b
        key = jax.random.key(seed)
        k0, k1, k2 = jax.random.split(key, 3)
        B, S, D, F = (2, 4096, 512, 2048)
        x = jax.random.normal(k0, (B, S, D), dtype=jnp.float32)
        w1 = jax.random.normal(k1, (F, D), dtype=jnp.float32) * (1.0 / np.sqrt(D))
        b1 = jnp.zeros((F,), dtype=jnp.float32)
        w2 = jax.random.normal(k2, (D, F), dtype=jnp.float32) * (1.0 / np.sqrt(F))
        b2 = jnp.zeros((D,), dtype=jnp.float32)
        return {'x': x, 'w1': w1, 'b1': b1, 'w2': w2, 'b2': b2}
    _L0_ffn_all = _L0_ffn_setup()
    _L0_ffn_in = {k: v for k, v in _L0_ffn_all.items() if k in ('w1', 'b1', 'w2', 'b2')}
    del _L0_ffn_all

    def _L1_xattn_setup():
        import jax, jax.numpy as jnp
        import numpy as np
        B, T, D, H = (2, 1024, 512, 16)
        DK = D // H

        def _split_heads(x):
            b, s, _ = x.shape
            return x.reshape(b, s, H, DK).transpose(0, 2, 1, 3)
        key = jax.random.key(seed)
        ks = jax.random.split(key, 12)
        s = 0.02
        return {'query': jax.random.normal(ks[0], (B, T, D), jnp.float32), 'key': jax.random.normal(ks[1], (B, T, D), jnp.float32), 'value': jax.random.normal(ks[2], (B, T, D), jnp.float32), 'mask': jax.random.randint(ks[3], (B, T), 0, 2) != 0, 'Wq': jax.random.normal(ks[4], (D, D), jnp.float32) * s, 'bq': jnp.zeros((D,), jnp.float32), 'Wk': jax.random.normal(ks[5], (D, D), jnp.float32) * s, 'bk': jnp.zeros((D,), jnp.float32), 'Wv': jax.random.normal(ks[6], (D, D), jnp.float32) * s, 'bv': jnp.zeros((D,), jnp.float32), 'Wo': jax.random.normal(ks[7], (D, D), jnp.float32) * s, 'bo': jnp.zeros((D,), jnp.float32)}
    _L1_xattn_all = _L1_xattn_setup()
    _L1_xattn_in = {k: v for k, v in _L1_xattn_all.items() if k in ('Wq', 'bq', 'Wk', 'bk', 'Wv', 'bv', 'Wo', 'bo')}
    del _L1_xattn_all

    def _L1_ffn_setup():
        import jax, jax.numpy as jnp
        import numpy as np
        NUM_EXPERTS = 8
        HIDDEN = 512
        INTER = 512
        BATCH = 2
        SEQ = 512
        TOP_K = 2
        SWIGLU_ALPHA = 1.702
        LIMIT = 7.0

        def _grouped_mm(x, w, expert_ids):
            onehot = jax.nn.one_hot(expert_ids, w.shape[0], dtype=x.dtype)
            y_all = jnp.einsum('tk,ekn->etn', x, w)
            return jnp.einsum('te,etn->tn', onehot, y_all)

        def _gpt_oss_swiglu(x):
            gate = jnp.minimum(x[..., ::2], LIMIT)
            up = jnp.clip(x[..., 1::2], -LIMIT, LIMIT)
            glu = gate * jax.nn.sigmoid(gate * SWIGLU_ALPHA)
            return (up + 1.0) * glu
        key = jax.random.key(seed)
        ks = jax.random.split(key, 7)
        hidden_states = jax.random.normal(ks[0], (BATCH, SEQ, HIDDEN), jnp.float32)
        router_indices = jax.random.randint(ks[1], (BATCH * SEQ, TOP_K), 0, NUM_EXPERTS)
        routing_weights = jax.nn.softmax(jax.random.normal(ks[2], (BATCH * SEQ, NUM_EXPERTS), jnp.float32), axis=-1)
        scale = 0.02
        gate_up_proj = jax.random.normal(ks[3], (NUM_EXPERTS, HIDDEN, 2 * INTER), jnp.float32) * scale
        gate_up_proj_bias = jax.random.normal(ks[4], (NUM_EXPERTS, 2 * INTER), jnp.float32) * scale
        down_proj = jax.random.normal(ks[5], (NUM_EXPERTS, INTER, HIDDEN), jnp.float32) * scale
        down_proj_bias = jax.random.normal(ks[6], (NUM_EXPERTS, HIDDEN), jnp.float32) * scale
        return {'hidden_states': hidden_states, 'router_indices': router_indices, 'routing_weights': routing_weights, 'gate_up_proj': gate_up_proj, 'gate_up_proj_bias': gate_up_proj_bias, 'down_proj': down_proj, 'down_proj_bias': down_proj_bias}
    _L1_ffn_all = _L1_ffn_setup()
    _L1_ffn_in = {k: v for k, v in _L1_ffn_all.items() if k in ('router_indices', 'routing_weights', 'gate_up_proj', 'gate_up_proj_bias', 'down_proj', 'down_proj_bias')}
    del _L1_ffn_all
    return {'x': x, 'ctx_1024': ctx_1024, 'mask_BxS2_bk0': mask_BxS2_bk0, 'L0_xattn_W_Q': _L0_xattn_in['W_Q'], 'L0_xattn_b_Q': _L0_xattn_in['b_Q'], 'L0_xattn_W_K': _L0_xattn_in['W_K'], 'L0_xattn_b_K': _L0_xattn_in['b_K'], 'L0_xattn_W_V': _L0_xattn_in['W_V'], 'L0_xattn_b_V': _L0_xattn_in['b_V'], 'L0_xattn_W_O': _L0_xattn_in['W_O'], 'L0_xattn_b_O': _L0_xattn_in['b_O'], 'L0_ffn_w1': _L0_ffn_in['w1'], 'L0_ffn_b1': _L0_ffn_in['b1'], 'L0_ffn_w2': _L0_ffn_in['w2'], 'L0_ffn_b2': _L0_ffn_in['b2'], 'L1_xattn_Wq': _L1_xattn_in['Wq'], 'L1_xattn_bq': _L1_xattn_in['bq'], 'L1_xattn_Wk': _L1_xattn_in['Wk'], 'L1_xattn_bk': _L1_xattn_in['bk'], 'L1_xattn_Wv': _L1_xattn_in['Wv'], 'L1_xattn_bv': _L1_xattn_in['bv'], 'L1_xattn_Wo': _L1_xattn_in['Wo'], 'L1_xattn_bo': _L1_xattn_in['bo'], 'L1_ffn_router_indices': _L1_ffn_in['router_indices'], 'L1_ffn_routing_weights': _L1_ffn_in['routing_weights'], 'L1_ffn_gate_up_proj': _L1_ffn_in['gate_up_proj'], 'L1_ffn_gate_up_proj_bias': _L1_ffn_in['gate_up_proj_bias'], 'L1_ffn_down_proj': _L1_ffn_in['down_proj'], 'L1_ffn_down_proj_bias': _L1_ffn_in['down_proj_bias']}

def reference(x, ctx_1024, mask_BxS2_bk0, L0_xattn_W_Q, L0_xattn_b_Q, L0_xattn_W_K, L0_xattn_b_K, L0_xattn_W_V, L0_xattn_b_V, L0_xattn_W_O, L0_xattn_b_O, L0_ffn_w1, L0_ffn_b1, L0_ffn_w2, L0_ffn_b2, L1_xattn_Wq, L1_xattn_bq, L1_xattn_Wk, L1_xattn_bk, L1_xattn_Wv, L1_xattn_bv, L1_xattn_Wo, L1_xattn_bo, L1_ffn_router_indices, L1_ffn_routing_weights, L1_ffn_gate_up_proj, L1_ffn_gate_up_proj_bias, L1_ffn_down_proj, L1_ffn_down_proj_bias):
    import jax
    import jax.numpy as jnp

    def _L0_xattn_ref(x_q, x_k, x_v, W_Q, b_Q, W_K, b_K, W_V, b_V, W_O, b_O):
        import jax, jax.numpy as jnp
        import numpy as np
        D_MODEL = 512
        N_HEADS = 16
        D_K = D_MODEL // N_HEADS
        B, L, _ = x_q.shape
        S = x_k.shape[1]
        H, dk = (N_HEADS, D_K)
        Q = (x_q @ W_Q + b_Q).reshape(B, L, H, dk).transpose(0, 2, 1, 3)
        K = (x_k @ W_K + b_K).reshape(B, S, H, dk).transpose(0, 2, 1, 3)
        V = (x_v @ W_V + b_V).reshape(B, S, H, dk).transpose(0, 2, 1, 3)
        scores = jnp.einsum('bhld,bhsd->bhls', Q, K) / jnp.sqrt(jnp.float32(dk))
        attn = jax.nn.softmax(scores, axis=-1)
        ctx = jnp.einsum('bhls,bhsd->bhld', attn, V)
        ctx = ctx.transpose(0, 2, 1, 3).reshape(B, L, H * dk)
        out = ctx @ W_O + b_O
        return out

    def _L0_ffn_ref(x, w1, b1, w2, b2):
        import jax, jax.numpy as jnp
        import numpy as np
        EPS = 1e-05

        def rmsnorm(x):
            return x * jax.lax.rsqrt(jnp.mean(x * x, axis=-1, keepdims=True) + EPS)

        def act_quant(x):
            scale = 127.0 / jnp.clip(jnp.max(jnp.abs(x), axis=-1, keepdims=True), 1e-05)
            q = jnp.clip(jnp.round(x * scale), -128.0, 127.0) / scale
            return x + jax.lax.stop_gradient(q - x)

        def weight_quant(w):
            scale = 1.0 / jnp.clip(jnp.mean(jnp.abs(w)), 1e-05)
            q = jnp.clip(jnp.round(w * scale), -1.0, 1.0) / scale
            return w + jax.lax.stop_gradient(q - w)

        def bitlinear(x, w, b):
            xq = act_quant(rmsnorm(x))
            wq = weight_quant(w)
            return jnp.einsum('bsd,fd->bsf', xq, wq) + b
        h = bitlinear(x, w1, b1)
        h = jax.nn.gelu(h, approximate=False)
        return bitlinear(h, w2, b2)

    def _L1_xattn_ref(query, key, value, mask, Wq, bq, Wk, bk, Wv, bv, Wo, bo):
        import jax, jax.numpy as jnp
        import numpy as np
        B, T, D, H = (2, 1024, 512, 16)
        DK = D // H

        def _split_heads(x):
            b, s, _ = x.shape
            return x.reshape(b, s, H, DK).transpose(0, 2, 1, 3)
        q = _split_heads(query @ Wq.T + bq)
        k = _split_heads(key @ Wk.T + bk)
        v = _split_heads(value @ Wv.T + bv)
        scale = 1.0 / np.sqrt(DK).astype(np.float32)
        scores = jnp.einsum('bhtd,bhsd->bhts', q, k) * scale
        scores = jnp.where(mask[:, None, None, :], scores, -jnp.inf)
        attn = jax.nn.softmax(scores, axis=-1)
        out = jnp.einsum('bhts,bhsd->bhtd', attn, v)
        out = out.transpose(0, 2, 1, 3).reshape(query.shape[0], -1, D)
        return out @ Wo.T + bo

    def _L1_ffn_ref(hidden_states, router_indices, routing_weights, gate_up_proj, gate_up_proj_bias, down_proj, down_proj_bias):
        import jax, jax.numpy as jnp
        import numpy as np
        NUM_EXPERTS = 8
        HIDDEN = 512
        INTER = 512
        BATCH = 2
        SEQ = 512
        TOP_K = 2
        SWIGLU_ALPHA = 1.702
        LIMIT = 7.0

        def _grouped_mm(x, w, expert_ids):
            onehot = jax.nn.one_hot(expert_ids, w.shape[0], dtype=x.dtype)
            y_all = jnp.einsum('tk,ekn->etn', x, w)
            return jnp.einsum('te,etn->tn', onehot, y_all)

        def _gpt_oss_swiglu(x):
            gate = jnp.minimum(x[..., ::2], LIMIT)
            up = jnp.clip(x[..., 1::2], -LIMIT, LIMIT)
            glu = gate * jax.nn.sigmoid(gate * SWIGLU_ALPHA)
            return (up + 1.0) * glu
        B = hidden_states.shape[0]
        H = hidden_states.shape[-1]
        x = hidden_states.reshape(-1, H)
        M = x.shape[0]
        top_k = router_indices.shape[1]
        num_experts = gate_up_proj.shape[0]
        topk_weights = jnp.take_along_axis(routing_weights, router_indices, axis=1)
        flat_experts = router_indices.reshape(-1)
        sort_idx = jnp.argsort(flat_experts)
        sorted_pos = sort_idx // top_k
        expert_sorted = flat_experts[sort_idx]
        grouped = x[sorted_pos]
        gate_up = _grouped_mm(grouped, gate_up_proj, expert_sorted)
        gate_up = gate_up + gate_up_proj_bias[expert_sorted]
        inter = _gpt_oss_swiglu(gate_up)
        down = _grouped_mm(inter, down_proj, expert_sorted)
        down = down + down_proj_bias[expert_sorted]
        down = down * topk_weights.reshape(-1)[sort_idx][:, None]
        out = jnp.zeros((M, H), x.dtype).at[sorted_pos].add(down)
        return out.reshape(B, -1, H)
    x = x + _L0_xattn_ref(_layernorm(x, axis=-1), ctx_1024, ctx_1024, L0_xattn_W_Q, L0_xattn_b_Q, L0_xattn_W_K, L0_xattn_b_K, L0_xattn_W_V, L0_xattn_b_V, L0_xattn_W_O, L0_xattn_b_O)
    x = x + _L0_ffn_ref(_layernorm(x, axis=-1), L0_ffn_w1, L0_ffn_b1, L0_ffn_w2, L0_ffn_b2)
    x = x + _L1_xattn_ref(_layernorm(x, axis=-1), ctx_1024, ctx_1024, mask_BxS2_bk0, L1_xattn_Wq, L1_xattn_bq, L1_xattn_Wk, L1_xattn_bk, L1_xattn_Wv, L1_xattn_bv, L1_xattn_Wo, L1_xattn_bo)
    x = x + _L1_ffn_ref(_layernorm(x, axis=-1), L1_ffn_router_indices, L1_ffn_routing_weights, L1_ffn_gate_up_proj, L1_ffn_gate_up_proj_bias, L1_ffn_down_proj, L1_ffn_down_proj_bias)
    return x

_drawn_inputs = setup_inputs


def setup_inputs(seed=0):
    import zlib

    import numpy as np

    out = dict(_drawn_inputs(seed))
    spreads = {'L0_ffn_b1': (0.0, 0.1),
     'L0_ffn_b2': (0.0, 0.1),
     'L1_xattn_bq': (0.0, 0.8),
     'L1_xattn_bk': (0.0, 2.0),
     'L1_xattn_bv': (0.0, 0.1),
     'L1_xattn_bo': (0.0, 0.1)}
    factors = {'L0_xattn_b_Q': 7.025,
     'L0_xattn_b_K': 64.0,
     'L0_xattn_b_V': 4.132,
     'L0_xattn_b_O': 3.934,
     'L1_xattn_Wq': 8.0,
     'L1_xattn_Wk': 8.0,
     'L1_ffn_routing_weights': 6.904,
     'L1_ffn_gate_up_proj': 4.947,
     'L1_ffn_gate_up_proj_bias': 8.0,
     'L1_ffn_down_proj': 4.763,
     'L1_ffn_down_proj_bias': 23.563}
    for name, (base, spread) in spreads.items():
        noise = np.random.default_rng([zlib.crc32(name.encode()), seed]).standard_normal(out[name].shape)
        drawn = base * np.exp(spread * noise) if base else spread * noise
        out[name] = jnp.asarray(drawn.astype(out[name].dtype))
    for name, factor in factors.items():
        out[name] = (out[name] * factor).astype(out[name].dtype)
    return out
```

```python
from contextlib import ExitStack

import concourse.bass as bass
from concourse import mybir

F32 = mybir.dt.float32
F16 = mybir.dt.float16
BF16 = mybir.dt.bfloat16
U8 = mybir.dt.uint8
I32 = mybir.dt.int32
ALU = mybir.AluOpType
ACT = mybir.ActivationFunctionType
AX = mybir.AxisListType.X

P = 128
D = 512
T = 512
B = 8
H = 16
DK = D // H
KC = D // P
TT = T // P
HG = P // DK
NG = H // HG
F = 2048
FC = F // P
FB = F // 512
E = 8
MT = 1024
MI = 512
UNITS = NG * TT

LN_EPS = 1e-5
RMS_EPS = 1e-5
QUANT_MIN = 1e-5
ROUND = 12582912.0
WS = 16.0
MS = 512.0
MASKED = 32768.0
ROWS_MAX = 3 * DK + 1
ROWS = ROWS_MAX + 2
NSPLIT = 3 * KC
STK = 16 * 3 * HG


def wait(eng, sem, value):
    if isinstance(value, int) and value <= 0:
        return
    eng.wait_ge(sem, value)


def encoder_phase(nc, layer, x_in, ctxT_in, x_out, w_in, bias_in, bo_in, mask_in, ffn_in):
    ffn = layer == 0
    tag = f"L{layer}_"
    sems = []
    with ExitStack() as ctx:
        def sb(name, shape, dt):
            return ctx.enter_context(nc.sbuf_tensor(tag + name, shape, dt))

        def sem(name):
            sems.append(nc.alloc_semaphore(tag + name))
            return sems[-1]

        w_hi = sb("w_hi", [P, 4, KC, D], F16)
        w_lo = sb("w_lo", [P, 4, KC, D], F16)
        qkv_bias = sb("qkv_bias", [P, 3, KC], F32)
        bo_rows = sb("bo_rows", [P, D], F32)
        ctx_raw = sb("ctx_raw", [P, KC, T], F32)
        ctx_hi = sb("ctx_hi", [P, KC, T], F16)
        ctx_lo = sb("ctx_lo", [P, KC, T], F16)
        xz = sb("xz", [P, TT, D], F32)
        xres = sb("xres", [P, TT, D], F32)
        xout = sb("xout", [P, TT, D], F32)
        xT_hi = sb("xT_hi", [P, KC, T], F16)
        xT_lo = sb("xT_lo", [P, KC, T], F16)
        stage_hi = sb("stage_hi", [P, KC, T], F16)
        stage_lo = sb("stage_lo", [P, KC, T], F16)
        v = sb("v", [P, TT, D], F32)
        q_stack = sb("q_stack", [ROWS, H, T], F16)
        k_stack = sb("k_stack", [ROWS, H, T], F16)
        probs = sb("probs", [P, 2, HG, T], F32)
        oT = sb("oT", [P, 2, NG, T], F16)
        o_sb = sb("o_sb", [P, T], F32)
        sum_sb = sb("sum_sb", [P, T], F32)
        ident = sb("ident", [P, P], F32)
        ones = sb("ones", [P, P], F32)
        stats = sb("stats", [P, TT, 6], F32)
        meanvar = sb("meanvar", [P, TT, 2], F32)
        half = sb("half", [P, TT], F32)
        eps = sb("eps", [P, TT], F32)
        var_eps = sb("var_eps", [P, TT], F32)
        rstd = sb("rstd", [P, TT], F32)
        maxima = sb("maxima", [P, 2, HG, TT], F32)
        m_parts = sb("m_parts", [P, 2 * HG * TT], F16)
        m_rows = sb("m_rows", [P, 2 * HG * TT], F16)
        if ffn:
            w1 = sb("w1", [P, KC, F], BF16)
            w2 = sb("w2", [P, FC, D], BF16)
            b1_rows = sb("b1_rows", [P, F], F32)
            b2_rows = sb("b2_rows", [P, D], F32)
            ident_bf = sb("ident_bf", [P, P], BF16)
            gT = sb("gT", [P, 2, FC, P], BF16)
            gq = sb("gq", [P, F], BF16)
            junk = sb("junk", [P, F], BF16)
            wabs = sb("wabs", [P, 2, 4], F32)
            wtot = sb("wtot", [P, 2], F32)
            wmean = sb("wmean", [P, 2], F32)
            wscale = sb("wscale", [P, 2], F32)
            rms = sb("rms", [P, TT], F32)
            zmax = sb("zmax", [P, TT], F32)
            zclip = sb("zclip", [P, TT], F32)
            zrec = sb("zrec", [P, TT], F32)
            zmul = sb("zmul", [P, TT], F32)
            zback = sb("zback", [P, TT], F32)
            gsum = sb("gsum", [P, TT], F32)
            grms = sb("grms", [P, TT], F32)
            inv_f = sb("inv_f", [P, 1], F32)
            gmax = sb("gmax", [P, TT], F32)
            gclip = sb("gclip", [P, TT], F32)
            grec = sb("grec", [P, TT], F32)
            gmul = sb("gmul", [P, TT], F32)
            gback = sb("gback", [P, TT], F32)
            zq = oT[:, 0, :, :].bitcast(BF16)
            qT = oT[:, 1, :, :].bitcast(BF16)
            g = probs[:, :, :, :].rearrange("p s h t -> p s (h t)")
        else:
            mask_u8 = sb("mask_u8", [1, B * T], U8)
            mask_row = sb("mask_row", [1, B * T], F16)
            kept = sb("kept", [1, B], F32)

        bank = [ctx.enter_context(nc.psum_tensor(f"{tag}bank{i}", [P, 512], F32)) for i in range(8)]
        bf_bank = {i: bank[i][:, :].bitcast(BF16) for i in (4, 5)}

        w_landed = [sem(f"w_landed{i}") for i in range(2)]
        small_landed = sem("small_landed")
        w_hi_made = sem("w_hi_made")
        w_lo_made = sem("w_lo_made")
        consts = sem("consts")
        consts2 = sem("consts2")
        bias_scaled = sem("bias_scaled")
        abs_made = sem("abs_made")
        mask_step = sem("mask_step")
        tot_made = sem("tot_made")
        tot_psum = sem("tot_psum")
        mean_made = sem("mean_made")
        tern_step = sem("tern_step")
        tern_made = sem("tern_made")
        stage = probs[:, :, :, :].rearrange("p s h t -> p s (h t)")

        jobs = [(w_in[i].rearrange("(c p) n -> p c n", p=P), "split", i) for i in range(4)]
        if ffn:
            w1T, w2T, b1, b2 = ffn_in
            w_views = [
                [w1T.rearrange("(c p) f -> p c f", p=P)[:, :, 512 * q:512 * q + 512] for q in range(4)],
                [w2T.rearrange("(c p) d -> p c d", p=P)[:, 4 * q:4 * q + 4, :] for q in range(4)],
            ]
            for m in range(2):
                jobs += [(w_views[m][q], "abs", (m, q)) for q in range(4)]
            for m in range(2):
                jobs += [(w_views[m][q], "tern", (m, q)) for q in range(4)]
        n_small = 4 if ffn else 3

        with nc.Block() as block:
            @block.sync
            def _(sp):
                sp.dma_start(qkv_bias[:, :, :], bias_in).then_inc(small_landed, 16)
                sp.dma_start(bo_rows[:, :], bo_in.partition_broadcast(P)).then_inc(small_landed, 16)
                if ffn:
                    sp.dma_start(b1_rows[:, :], b1.partition_broadcast(P)).then_inc(small_landed, 16)
                    sp.dma_start(b2_rows[:, :], b2.partition_broadcast(P)).then_inc(small_landed, 16)
                else:
                    sp.dma_start(mask_u8[:, :], mask_in).then_inc(small_landed, 16)
                for n, (src, kind, i) in enumerate(jobs):
                    if n >= 2:
                        _, kind2, i2 = jobs[n - 2]
                        if kind2 == "split":
                            sp.wait_ge(w_lo_made, n - 1)
                        elif kind2 == "abs":
                            sp.wait_ge(abs_made, 4 * i2[0] + i2[1] + 1)
                        else:
                            sp.wait_ge(tern_made, 4 * i2[0] + i2[1] + 1)
                    sp.dma_start(stage[:, n % 2, :].rearrange("p (c n) -> p c n", c=4), src)\
                      .then_inc(w_landed[n % 2], 16)

            @block.gpsimd
            def _(pool):
                nc.gpsimd.memset(ident[:, :], 0.0).then_inc(consts, 1)
                nc.gpsimd.memset(ones[:, :], 1.0).then_inc(consts, 1)
                nc.gpsimd.memset(half[:, :], -0.5).then_inc(consts, 1)
                nc.gpsimd.memset(eps[:, :], LN_EPS).then_inc(consts, 1)
                pool.wait_ge(consts, 4)
                nc.gpsimd.affine_select(out=ident[:, :], in_=ident[:, :], compare_op=ALU.not_equal,
                                        fill=1.0, base=0, pattern=[[-1, P]], channel_multiplier=1)\
                    .then_inc(consts, 1)
                if ffn:
                    pool.wait_ge(consts, 5)
                    nc.gpsimd.tensor_copy(ident_bf[:, :], ident[:, :]).then_inc(consts, 1)
                    nc.gpsimd.memset(inv_f[:, :], 1.0 / F).then_inc(consts, 1)

            @block.scalar
            def _(act):
                for n in range(4):
                    act.wait_ge(w_landed[n % 2], 16 * (n // 2 + 1))
                    nc.scalar.activation(w_hi[:, n, :, :], stage[:, n % 2, :].rearrange("p (c n) -> p c n", c=4),
                                         ACT.Copy, scale=WS).then_inc(w_hi_made, 1)
                act.wait_ge(small_landed, 16 * n_small)
                nc.scalar.activation(qkv_bias[:, :, :], qkv_bias[:, :, :], ACT.Copy, scale=WS)\
                    .then_inc(bias_scaled, 1)

            @block.tensor
            def _(pe):
                if ffn:
                    pe.wait_ge(consts, 5)
                    pe.wait_ge(tot_made, 1)
                    nc.tensor.matmul(bank[0][:, 0:2], ones[:, :], wtot[:, :], start=True, stop=True)\
                        .then_inc(tot_psum, 1)

            @block.vector
            def _(dve):
                nc.vector.memset(q_stack[96:ROWS, :, :], MASKED).then_inc(consts2, 1)
                nc.vector.memset(k_stack[96:ROWS, :, :], -MS).then_inc(consts2, 1)
                if ffn:
                    dve.wait_ge(consts2, 2)
                    nc.vector.memset(k_stack[96:97, :, :], 0.0).then_inc(consts2, 1)
                else:
                    rows = mask_row[:, :].rearrange("o (b t) -> o b t", b=B)
                    dve.wait_ge(small_landed, 16 * n_small)
                    nc.vector.tensor_scalar(mask_row[:, :], mask_u8[:, :], MASKED, -MASKED, ALU.mult, ALU.add)\
                        .then_inc(mask_step, 1)
                    nc.vector.tensor_reduce(kept[:, :], mask_u8[:, :].rearrange("o (b t) -> o b t", b=B), AX, ALU.add)\
                        .then_inc(mask_step, 1)
                    dve.wait_ge(mask_step, 2)
                    nc.vector.reciprocal(kept[:, :], kept[:, :]).then_inc(mask_step, 1)
                    dve.wait_ge(mask_step, 3)
                    nc.vector.tensor_scalar(kept[:, :], kept[:, :], 0.0, None, ALU.mult).then_inc(mask_step, 1)
                    dve.wait_ge(mask_step, 4)
                    nc.vector.tensor_tensor(rows, rows, kept[:, :].unsqueeze(2).to_broadcast([1, B, T]), ALU.add)\
                        .then_inc(mask_step, 1)
                for n, (src, kind, i) in enumerate(jobs):
                    half_n = stage[:, n % 2, :]
                    dve.wait_ge(w_landed[n % 2], 16 * (n // 2 + 1))
                    if kind == "split":
                        dve.wait_ge(w_hi_made, n + 1)
                        nc.vector.scalar_tensor_tensor(
                            w_lo[:, n, :, :].rearrange("p c n -> p (c n)"), half_n, WS,
                            w_hi[:, n, :, :].rearrange("p c n -> p (c n)"), ALU.mult, ALU.subtract)\
                            .then_inc(w_lo_made, 1)
                    elif kind == "abs":
                        m, q = i
                        nc.vector.tensor_reduce(wabs[:, m, q:q + 1], half_n, AX, ALU.add,
                                                apply_absolute_value=True).then_inc(abs_made, 1)
                        if i == (1, 3):
                            dve.wait_ge(abs_made, 8)
                            nc.vector.tensor_reduce(wtot[:, :], wabs[:, :, :], AX, ALU.add)\
                                .then_inc(tot_made, 1)
                            dve.wait_ge(tot_psum, 1)
                            nc.vector.tensor_scalar(wmean[:, :], bank[0][:, 0:2], 1.0 / (D * F), QUANT_MIN,
                                                    ALU.mult, ALU.max).then_inc(mean_made, 1)
                            dve.wait_ge(mean_made, 1)
                            nc.vector.reciprocal(wscale[:, :], wmean[:, :]).then_inc(mean_made, 1)
                            dve.wait_ge(mean_made, 2)
                    else:
                        m, q = i
                        k = 2 * (4 * m + q)
                        nc.vector.tensor_scalar(half_n, half_n, wscale[:, m:m + 1], ROUND, ALU.mult, ALU.add)\
                            .then_inc(tern_step, 1)
                        dve.wait_ge(tern_step, k + 1)
                        nc.vector.tensor_scalar(half_n, half_n, ROUND + 1.0, ROUND - 1.0, ALU.min, ALU.max)\
                            .then_inc(tern_step, 1)
                        dve.wait_ge(tern_step, k + 2)
                        out = w1[:, :, 512 * q:512 * q + 512] if m == 0 else w2[:, 4 * q:4 * q + 4, :]
                        nc.vector.tensor_scalar(out, half_n.rearrange("p (c n) -> p c n", c=4), -ROUND, None,
                                                ALU.add).then_inc(tern_made, 1)

        xz_landed, xres_landed, ctx_landed = sem("xz_landed"), sem("xres_landed"), sem("ctx_landed")
        stack_landed = [[sem(f"{s}_stack_landed{i}") for i in range(2)] for s in "qk"]
        mask_landed, mrows_landed, out_landed = sem("mask_landed"), sem("mrows_landed"), sem("out_landed")
        scores_done, maxmm_done, pv_done = sem("scores_done"), sem("maxmm_done"), sem("pv_done")
        split_job, v_job, o_job = sem("split_job"), sem("v_job"), sem("o_job")
        exp_done, hi_made, v_made, o_copied = sem("exp_done"), sem("hi_made"), sem("v_made"), sem("o_copied")
        max_made, lo_made, z_made, o_normed = sem("max_made"), sem("lo_made"), sem("z_made"), sem("o_normed")
        x1_made, mhi_made, mlo_made, mrows_made = sem("x1_made"), sem("mhi_made"), sem("mlo_made"), sem("mrows_made")
        stats_made, meanvar_made, sum_inverted = sem("stats_made"), sem("meanvar_made"), sem("sum_inverted")
        ve_made, rstd_made, ctxhi_made, ctx_made = sem("ve_made"), sem("rstd_made"), sem("ctxhi_made"), sem("ctx_made")
        ob_made, ohi_made, o_made, xres_made = sem("ob_made"), sem("ohi_made"), sem("o_made"), sem("xres_made")
        if ffn:
            tr_done, f1_done, f2_done = sem("tr_done"), sem("f1_done"), sem("f2_done")
            tr_copied, gelu_made, gsum_made = sem("tr_copied"), sem("gelu_made"), sem("gsum_made")
            stats2_made, meanvar2_made, z2_made = sem("stats2_made"), sem("meanvar2_made"), sem("z2_made")
            zscale_made, zround_made, zq_made = sem("zscale_made"), sem("zround_made"), sem("zq_made")
            u_made, gscale_made, ground_made, gq_made = sem("u_made"), sem("gscale_made"), sem("ground_made"), sem("gq_made")
            x2_made, xout_made = sem("x2_made"), sem("xout_made")
            rms_step, rms_made, grms_step, grms_made = sem("rms_step"), sem("rms_made"), sem("grms_step"), sem("grms_made")

        gated = sem("gated")
        gate = sb("gate", [P, 1], F32)

        x_dst = xres if ffn else xout
        TR = ["q0", "q1", "g0a", "g0b", "q2", "g1a", "g1b", "q3", "g2a", "g2b", "g3a", "g3b"]
        N_TR = len(TR)
        N_ZS, N_GS = 5, 5

        x_view = x_in.rearrange("b (t p) d -> b p t d", p=P)
        out_view = x_out.rearrange("b (t p) d -> b p t d", p=P)
        ctx_view = ctxT_in.rearrange("b (c p) t -> b p c t", p=P)

        def all_batches(eng, prologue, body, epilogue=None):
            prologue()
            body(0, 1)
            with eng.Fori(1, B - 1) as b:
                body(b, b + 1)
            body(B - 1, None)
            if epilogue is not None:
                epilogue()

        with nc.Block() as block:
            @block.sync
            def _(sp):
                def load_for_next(n):
                    if ffn:
                        wait(sp, zq_made, TT * (n - 1))
                    wait(sp, split_job, NSPLIT * (n - 1) + KC)
                    sp.dma_start(xz[:, :, :], x_view[n, :, :, :]).then_inc(xz_landed, 16)
                    wait(sp, ctx_made, KC * n)
                    sp.dma_start(ctx_raw[:, :, :], ctx_view[n, :, :, :]).then_inc(ctx_landed, 16)

                def stacks(n):
                    for which in range(2):
                        stack = (q_stack, k_stack)[which]
                        parts = (stage_hi, stage_lo, stage_hi) if which == 0 else (stage_hi, stage_hi, stage_lo)
                        for pair in range(2):
                            sp.wait_ge(lo_made, NSPLIT * n + KC * (1 + which) + 2 * (pair + 1))
                            for r, part in enumerate(parts):
                                for j in range(HG):
                                    h0 = 2 * pair * HG + j
                                    sp.dma_start(stack[DK * r:DK * r + DK, h0:h0 + HG + 1:HG, :],
                                                 part[DK * j:DK * j + DK, 2 * pair:2 * pair + 2, :])\
                                      .then_inc(stack_landed[which][pair], 16)
                    if not ffn:
                        sp.dma_start(k_stack[96:97, :, :], mask_row[0:1, bass.ds(n * T, T)].unsqueeze(1)
                                     .to_broadcast([1, H, T])).then_inc(mask_landed, 16)

                def m_row_dmas(G, g_):
                    sp.wait_ge(mrows_made, G + 1)
                    for q in range(4):
                        for part in range(2):
                            dst = q_stack[97 + part:98 + part, HG * g_:HG * g_ + HG, :]\
                                .rearrange("o h (t i) -> o h t i", i=P)[:, :, :, 32 * q:32 * q + 32]
                            src = m_rows[32 * q + 16 * part:32 * q + 16 * part + 16, 0:32]
                            sp.dma_start(dst, src).then_inc(mrows_landed, 16)

                def prologue():
                    load_for_next(0)
                    stacks(0)
                    m_row_dmas(0, 0)

                def store(b):
                    sp.wait_ge(x2_made if ffn else x1_made, TT * (b + 1))
                    sp.dma_start(out_view[b, :, :, :], xout[:, :, :]).then_inc(out_landed, 16)

                def body(b, n):
                    if n is not None:
                        load_for_next(n)
                    if ffn:
                        wait(sp, xout_made, b)
                        wait(sp, z2_made, TT * b)
                    wait(sp, x1_made, TT * b)
                    sp.dma_start(xres[:, :, :], x_view[b, :, :, :]).then_inc(xres_landed, 16)
                    if not (isinstance(b, int) and b == 0):
                        store(b - 1)
                    for g_ in range(1, NG):
                        m_row_dmas(NG * b + g_, g_)
                    if n is not None:
                        stacks(n)
                        m_row_dmas(NG * n, 0)

                def epilogue():
                    store(B - 1)
                    sp.wait_ge(out_landed, 16 * B)

                all_batches(sp, prologue, body, epilogue)

            @block.tensor
            def _(pe):
                def product(out, lhs_hi, lhs_lo, rhs_hi, rhs_lo):
                    for c in range(KC):
                        nc.tensor.matmul(out, lhs_hi(c), rhs_hi(c), start=(c == 0), stop=False)
                        nc.tensor.matmul(out, lhs_hi(c), rhs_lo(c), start=False, stop=False)
                        last = nc.tensor.matmul(out, lhs_lo(c), rhs_hi(c), start=False, stop=(c == KC - 1))
                    return last

                def prep_xqk(n):
                    wait(pe, exp_done, 2 * UNITS * n)
                    pe.wait_ge(z_made, TT * (n + 1))
                    for c in range(KC):
                        for t in range(TT):
                            last = nc.tensor.matmul(bank[c][:, P * t:P * t + P], xz[:, t, P * c:P * c + P], ident[:, :],
                                                    is_transpose=True, start=True, stop=True)
                        last.then_inc(split_job, 1)
                    for j in range(KC, NSPLIT):
                        c, which = j % KC, j // KC - 1
                        if j == KC:
                            pe.wait_ge(lo_made, NSPLIT * n + KC)
                        else:
                            pe.wait_ge(lo_made, NSPLIT * n + j - 3)
                        if j == 2 * KC:
                            pe.wait_ge(ctx_made, KC * (n + 1))
                        src_hi, src_lo = (xT_hi, xT_lo) if which == 0 else (ctx_hi, ctx_lo)
                        cols = slice(P * c, P * c + P)
                        product(bank[j % 4][:, :],
                                lambda k: w_hi[:, which, k, cols], lambda k: w_lo[:, which, k, cols],
                                lambda k: src_hi[:, k, :], lambda k: src_lo[:, k, :]).then_inc(split_job, 1)

                def max_mms(n, g_, t):
                    for i in range(HG):
                        h = HG * g_ + i
                        M = UNITS * HG * n + (g_ * TT + t) * HG + i
                        wait(pe, max_made, M - 1)
                        nc.tensor.matmul(bank[4 + i % 2][:, :], q_stack[0:ROWS_MAX, h, P * t:P * t + P],
                                         k_stack[0:ROWS_MAX, h, :], start=True, stop=True).then_inc(maxmm_done, 1)

                def prep_v_max0(n):
                    pe.wait_ge(ctx_made, KC * (n + 1))
                    for s in range(TT):
                        if s == 0:
                            for landed in stack_landed[0] + stack_landed[1]:
                                pe.wait_ge(landed, STK * (n + 1))
                            if not ffn:
                                pe.wait_ge(mask_landed, 16 * (n + 1))
                            if ffn:
                                wait(pe, tr_copied, N_TR * (n - 1))
                        max_mms(n, 0, s)
                        pe.wait_ge(lo_made, NSPLIT * n + 2 * KC + s + 1)
                        product(bank[s][:, :],
                                lambda k: ctx_hi[:, k, P * s:P * s + P], lambda k: ctx_lo[:, k, P * s:P * s + P],
                                lambda k: w_hi[:, 2, k, :], lambda k: w_lo[:, 2, k, :]).then_inc(v_job, 1)

                def scores(b, k):
                    g_, s = divmod(k, TT)
                    if s == 0:
                        pe.wait_ge(mrows_landed, 128 * (NG * b + g_ + 1))
                    for i in range(HG):
                        h = HG * g_ + i
                        if i % 2 == 0:
                            if k == 0:
                                pe.wait_ge(v_made, TT * (b + 1))
                                if ffn:
                                    wait(pe, u_made, FB * TT * b)
                            else:
                                pe.wait_ge(exp_done, 2 * (UNITS * b + k - 1) + i // 2 + 1)
                        mm = nc.tensor.matmul(bank[i][:, :], k_stack[0:ROWS, h, P * s:P * s + P],
                                              q_stack[0:ROWS, h, :], start=True, stop=True)
                        if i % 2 == 1:
                            mm.then_inc(scores_done, 1)

                def weighted_values(b, k):
                    g_, s = divmod(k, TT)
                    pe.wait_ge(exp_done, 2 * (UNITS * b + k) + 2)
                    if s == 0:
                        wait(pe, o_copied, NG * b + g_)
                        if g_ == 0:
                            wait(pe, x1_made, TT * b)
                            if ffn:
                                wait(pe, x2_made, TT * b)
                    for i in range(HG):
                        rows = slice(DK * i, DK * i + DK)
                        h = HG * g_ + i
                        nc.tensor.matmul(bank[6][rows, :], v[:, s, DK * h:DK * h + DK], probs[:, k % 2, i, :],
                                         start=(s == 0), stop=(s == TT - 1))

                def summed_probs(k):
                    s = k % TT
                    for i in range(HG):
                        rows = slice(DK * i, DK * i + DK)
                        last = nc.tensor.matmul(bank[7][rows, :], ones[:, rows], probs[:, k % 2, i, :],
                                                start=(s == 0), stop=(s == TT - 1))
                    last.then_inc(pv_done, 1)

                def project_out(b):
                    pe.wait_ge(o_made, NG * (b + 1))
                    pe.wait_ge(o_copied, NG * (b + 1))
                    for t in range(TT):
                        if t >= 2:
                            pe.wait_ge(x1_made, TT * b + t - 1)
                        product(bank[6 + t % 2][:, :],
                                lambda k: oT[:, 0, k, P * t:P * t + P], lambda k: oT[:, 1, k, P * t:P * t + P],
                                lambda k: w_hi[:, 3, k, :], lambda k: w_lo[:, 3, k, :]).then_inc(o_job, 1)

                def transposes(b, name):
                    i = TR.index(name)
                    kind, t = name[0], int(name[1])
                    dst = bf_bank[4 + i % 2]
                    wait(pe, tr_copied, N_TR * b + i - 1)
                    if kind == "q":
                        pe.wait_ge(zq_made, TT * b + t + 1)
                        for c in range(KC):
                            last = nc.tensor.matmul(dst[:, P * c:P * c + P], zq[:, t, P * c:P * c + P], ident_bf[:, :],
                                                    is_transpose=True, start=True, stop=True)
                    else:
                        pe.wait_ge(gq_made, TT * b + t + 1)
                        first = 0 if name[2] == "a" else 8
                        for c in range(8):
                            cols = slice(P * (first + c), P * (first + c) + P)
                            last = nc.tensor.matmul(dst[:, P * c:P * c + P], gq[:, cols], ident_bf[:, :],
                                                    is_transpose=True, start=True, stop=True)
                    last.then_inc(tr_done, 1)

                def ffn_up(b, t):
                    pe.wait_ge(tr_copied, N_TR * b + TR.index(f"q{t}") + 1)
                    for j in range(FB):
                        if t > 0:
                            pe.wait_ge(u_made, FB * (TT * b + t - 1) + j + 1)
                        for c in range(KC):
                            last = nc.tensor.matmul(bank[j][:, :], qT[:, c, P * t:P * t + P],
                                                    w1[:, c, 512 * j:512 * j + 512], start=(c == 0), stop=(c == KC - 1))
                        last.then_inc(f1_done, 1)

                def ffn_down(b, t):
                    pe.wait_ge(tr_copied, N_TR * b + TR.index(f"g{t}b") + 1)
                    if t >= 2:
                        pe.wait_ge(x2_made, TT * b + t - 1)
                    for c in range(FC):
                        last = nc.tensor.matmul(bank[6 + t % 2][:, :], gT[:, t % 2, c, :], w2[:, c, :],
                                                start=(c == 0), stop=(c == FC - 1))
                    last.then_inc(f2_done, 1)

                def feed_forward(b, n):
                    pe.wait_ge(x1_made, TT * (b + 1))
                    pe.wait_ge(v_made, TT * (b + 1) if n is None else TT * (n + 1))
                    pe.wait_ge(exp_done, 2 * UNITS * (b + 1))
                    last_max = UNITS * HG * (b + 1) if n is None else UNITS * HG * n + TT * HG
                    pe.wait_ge(max_made, last_max)
                    transposes(b, "q0")
                    ffn_up(b, 0)
                    transposes(b, "q1")
                    ffn_up(b, 1)
                    for t in range(TT):
                        transposes(b, f"g{t}a")
                        transposes(b, f"g{t}b")
                        if t + 2 < TT:
                            transposes(b, f"q{t + 2}")
                        ffn_down(b, t)
                        if t + 2 < TT:
                            ffn_up(b, t + 2)

                def prologue():
                    prep_xqk(0)
                    prep_v_max0(0)

                def body(b, n):
                    scores(b, 0)
                    for k in range(UNITS):
                        if k + 1 < UNITS:
                            scores(b, k + 1)
                        g_, s = divmod(k, TT)
                        ahead = g_ + 1 < NG and s < 2
                        if ahead:
                            if ffn and k == 0:
                                wait(pe, tr_copied, N_TR * b)
                            max_mms(b, g_ + 1, 2 * s)
                        weighted_values(b, k)
                        if ahead:
                            max_mms(b, g_ + 1, 2 * s + 1)
                        summed_probs(k)
                    if n is not None:
                        prep_xqk(n)
                    project_out(b)
                    if n is not None:
                        prep_v_max0(n)
                    if ffn:
                        feed_forward(b, n)

                all_batches(pe, prologue, body)

            @block.scalar
            def _(act):
                def hi_parts(n):
                    for j in range(NSPLIT):
                        c = j % KC
                        act.wait_ge(split_job, NSPLIT * n + j + 1)
                        if j < KC:
                            nc.scalar.activation(xT_hi[:, c, :], bank[c][:, :], ACT.Copy).then_inc(hi_made, 1)
                        else:
                            which = j // KC - 1
                            wait(act, stack_landed[1 - which][c // 2], STK * (n + which))
                            nc.scalar.activation(stage_hi[:, c, :], bank[c][:, :], ACT.Identity,
                                                 bias=qkv_bias[:, which, c:c + 1]).then_inc(hi_made, 1)

                def v_copies(n):
                    for s in range(TT):
                        act.wait_ge(v_job, TT * n + s + 1)
                        nc.scalar.activation(v[:, s, :], bank[s][:, :], ACT.Copy).then_inc(v_made, 1)

                def o_copies(b, g_):
                    act.wait_ge(pv_done, UNITS * b + TT * (g_ + 1))
                    wait(act, o_made, NG * b + g_)
                    nc.scalar.activation(sum_sb[:, :], bank[7][:, :], ACT.Copy)
                    nc.scalar.activation(o_sb[:, :], bank[6][:, :], ACT.Copy).then_inc(o_copied, 1)

                def body(b, n):
                    if ffn:
                        wait(act, gq_made, TT * b)
                    for k in range(UNITS):
                        g_, s = divmod(k, TT)
                        wait(act, pv_done, UNITS * b + k - 1)
                        for pair in range(2):
                            act.wait_ge(scores_done, 2 * (UNITS * b + k) + pair + 1)
                            for i in (2 * pair, 2 * pair + 1):
                                e = nc.scalar.activation(probs[:, k % 2, i, :], bank[i][:, :], ACT.Exp,
                                                         scale=float(DK) ** -0.5 / WS ** 2)
                            e.then_inc(exp_done, 1)
                        if s == 0 and g_ > 0:
                            o_copies(b, g_ - 1)
                    o_copies(b, NG - 1)
                    if n is not None:
                        hi_parts(n)
                        v_copies(n)
                    if ffn:
                        feed_forward(b)

                def feed_forward(b):
                    def copy(name):
                        i = TR.index(name)
                        t = int(name[1])
                        act.wait_ge(tr_done, N_TR * b + i + 1)
                        src = bf_bank[4 + i % 2]
                        if name[0] == "q":
                            dst = qT[:, :, P * t:P * t + P]
                            src = src[:, 0:KC * P]
                        else:
                            wait(act, f2_done, TT * b + t - 1)
                            dst = gT[:, t % 2, 0:8, :] if name[2] == "a" else gT[:, t % 2, 8:16, :]
                        nc.scalar.activation(dst, src.rearrange("p (c t) -> p c t", t=P), ACT.Copy)\
                            .then_inc(tr_copied, 1)

                    def gelu(t):
                        act.wait_ge(u_made, FB * (TT * b + t + 1))
                        nc.scalar.activation(g[:, t % 2, :], g[:, t % 2, :], ACT.Gelu).then_inc(gelu_made, 1)
                        act.wait_ge(gelu_made, TT * b + t + 1)
                        wait(act, gsum_made, TT * b + t)
                        nc.scalar.activation(junk[:, :], g[:, t % 2, :], ACT.Square,
                                             accum_out=gsum[:, t:t + 1]).then_inc(gsum_made, 1)

                    copy("q0")
                    copy("q1")
                    gelu(0)
                    gelu(1)
                    for t in range(TT):
                        copy(f"g{t}a")
                        copy(f"g{t}b")
                        if t + 2 < TT:
                            copy(f"q{t + 2}")
                            gelu(t + 2)

                def prologue():
                    hi_parts(0)
                    v_copies(0)

                all_batches(act, prologue, body)

            @block.vector
            def _(dve):
                def aggregate_gate(done):
                    wait(dve, gated, done)
                    nc.vector.memset(gate[:, :], 0.0).then_inc(gated, 1)

                def ln_stats(n):
                    dve.wait_ge(xz_landed, 16 * (n + 1))
                    wait(dve, rstd_made, n)
                    wait(dve, z_made, TT * n)
                    for t in range(TT):
                        nc.vector.bn_stats(stats[:, t, :], xz[:, t, :]).then_inc(stats_made, 1)
                    dve.wait_ge(stats_made, TT * (n + 1))
                    if ffn:
                        wait(dve, z2_made, TT * (n - 1))
                        wait(dve, rms_made, n - 1)
                    aggregate_gate(2 * n - 1 if ffn else n)
                    for t in range(TT):
                        nc.vector.bn_aggr(meanvar[:, t, :], stats[:, t, :]).then_inc(meanvar_made, 1)

                def ln_apply(n, t):
                    dve.wait_ge(rstd_made, n + 1)
                    dve.wait_ge(meanvar_made, TT * (n + 1))
                    nc.vector.tensor_scalar(xz[:, t, :], xz[:, t, :], meanvar[:, t, 0:1], rstd[:, t:t + 1],
                                            ALU.subtract, ALU.mult).then_inc(z_made, 1)

                def lo_parts(n):
                    for j in range(NSPLIT):
                        c = j % KC
                        dve.wait_ge(hi_made, NSPLIT * n + j + 1)
                        if j < KC:
                            nc.vector.tensor_tensor(xT_lo[:, c, :], bank[c][:, :], xT_hi[:, c, :], ALU.subtract)\
                                .then_inc(lo_made, 1)
                        else:
                            which = j // KC - 1
                            nc.vector.scalar_tensor_tensor(stage_lo[:, c, :], bank[c][:, :],
                                                           qkv_bias[:, which, c:c + 1], stage_hi[:, c, :],
                                                           ALU.add, ALU.subtract).then_inc(lo_made, 1)

                def maxima_of(n, g_, t):
                    for i in range(HG):
                        M = UNITS * HG * n + (g_ * TT + t) * HG + i
                        dve.wait_ge(maxmm_done, M + 1)
                        nc.vector.tensor_reduce(maxima[:, g_ % 2, i, t:t + 1], bank[4 + i % 2][:, :], AX, ALU.max)\
                            .then_inc(max_made, 1)

                def max_rows(n, g_):
                    G = NG * n + g_
                    half_n = HG * TT
                    dve.wait_ge(max_made, HG * TT * (G + 1))
                    wait(dve, mrows_made, G)
                    src = maxima[:, g_ % 2, :, :].rearrange("p h t -> p (h t)")
                    nc.vector.tensor_scalar(m_parts[:, 0:half_n], src, 1.0 / MS, None, ALU.mult).then_inc(mhi_made, 1)
                    dve.wait_ge(mhi_made, G + 1)
                    nc.vector.scalar_tensor_tensor(m_parts[:, half_n:2 * half_n], src, 1.0 / MS, m_parts[:, 0:half_n],
                                                   ALU.mult, ALU.subtract).then_inc(mlo_made, 1)
                    dve.wait_ge(mlo_made, G + 1)
                    wait(dve, mrows_landed, 128 * G)
                    nc.vector.transpose(m_rows[:, :], m_parts[:, :]).then_inc(mrows_made, 1)

                def normalise(b, g_):
                    G = NG * b + g_
                    dve.wait_ge(o_copied, G + 1)
                    nc.vector.reciprocal(sum_sb[:, :], sum_sb[:, :]).then_inc(sum_inverted, 1)
                    dve.wait_ge(sum_inverted, G + 1)
                    nc.vector.tensor_tensor(o_sb[:, :], o_sb[:, :], sum_sb[:, :], ALU.mult).then_inc(o_normed, 1)

                def residual(b):
                    dve.wait_ge(xres_made, b + 1)
                    if not ffn:
                        wait(dve, out_landed, 16 * b)
                    for t in range(TT):
                        dve.wait_ge(o_job, TT * b + t + 1)
                        nc.vector.scalar_tensor_tensor(x_dst[:, t, :], bank[6 + t % 2][:, :], 1.0 / WS ** 2,
                                                       xres[:, t, :], ALU.mult, ALU.add).then_inc(x1_made, 1)

                def quantise_x(b, n):
                    dve.wait_ge(x1_made, TT * (b + 1))
                    for t in range(TT):
                        nc.vector.bn_stats(stats[:, t, :], xres[:, t, :]).then_inc(stats2_made, 1)
                    dve.wait_ge(stats2_made, TT * (b + 1))
                    dve.wait_ge(z_made, TT * (b + 1 if n is None else n + 1))
                    aggregate_gate(2 * b + 1 if n is None else 2 * b + 2)
                    for t in range(TT):
                        nc.vector.bn_aggr(meanvar[:, t, :], stats[:, t, :]).then_inc(meanvar2_made, 1)
                    dve.wait_ge(split_job, NSPLIT * (b + 1 if n is None else n + 1))
                    dve.wait_ge(rms_step, 5 * b + 2)
                    dve.wait_ge(meanvar2_made, TT * (b + 1))
                    for t in range(TT):
                        nc.vector.tensor_scalar(xz[:, t, :], xres[:, t, :], meanvar[:, t, 0:1], rstd[:, t:t + 1],
                                                ALU.subtract, ALU.mult).then_inc(z2_made, 1)
                    dve.wait_ge(z2_made, TT * (b + 1))
                    zs = N_ZS * b
                    wait(dve, u_made, FB * TT * b)
                    nc.vector.tensor_reduce(zmax[:, :], xz[:, :, :], AX, ALU.max, apply_absolute_value=True)\
                        .then_inc(zscale_made, 1)
                    dve.wait_ge(rms_made, b + 1)
                    dve.wait_ge(zscale_made, zs + 1)
                    nc.vector.tensor_tensor(zclip[:, :], zmax[:, :], rms[:, :], ALU.mult).then_inc(zscale_made, 1)
                    dve.wait_ge(zscale_made, zs + 2)
                    nc.vector.tensor_scalar(zclip[:, :], zclip[:, :], QUANT_MIN, None, ALU.max).then_inc(zscale_made, 1)
                    dve.wait_ge(zscale_made, zs + 3)
                    nc.vector.reciprocal(zrec[:, :], zclip[:, :]).then_inc(zscale_made, 1)
                    nc.vector.tensor_scalar(zback[:, :], zclip[:, :], 1.0 / 127.0, wmean[:, 0:1], ALU.mult, ALU.mult)\
                        .then_inc(zscale_made, 1)
                    dve.wait_ge(zscale_made, zs + 5)
                    nc.vector.scalar_tensor_tensor(zmul[:, :], zrec[:, :], 127.0, rms[:, :], ALU.mult, ALU.mult)\
                        .then_inc(zround_made, 1)
                    dve.wait_ge(zround_made, 5 * b + 1)
                    for t in range(TT):
                        nc.vector.tensor_scalar(xz[:, t, :], xz[:, t, :], zmul[:, t:t + 1], ROUND, ALU.mult, ALU.add)\
                            .then_inc(zround_made, 1)
                        dve.wait_ge(zround_made, 5 * b + t + 2)
                        nc.vector.tensor_scalar(zq[:, t, :], xz[:, t, :], ROUND + 127.0, -ROUND, ALU.min, ALU.add)\
                            .then_inc(zq_made, 1)

                def ffn_hidden(b, t):
                    for j in range(FB):
                        dve.wait_ge(f1_done, FB * (TT * b + t) + j + 1)
                        if j == 0:
                            if t >= 2:
                                dve.wait_ge(gq_made, TT * b + t - 1)
                            else:
                                dve.wait_ge(pv_done, UNITS * (b + 1))
                        nc.vector.scalar_tensor_tensor(g[:, t % 2, 512 * j:512 * j + 512], bank[j][:, :],
                                                       zback[:, t:t + 1], b1_rows[:, 512 * j:512 * j + 512],
                                                       ALU.mult, ALU.add).then_inc(u_made, 1)

                def quantise_g(b, t):
                    gs = N_GS * (TT * b + t)
                    col = slice(t, t + 1)
                    dve.wait_ge(gelu_made, TT * b + t + 1)
                    if t == 0:
                        wait(dve, x2_made, TT * b)
                    nc.vector.tensor_reduce(gmax[:, col], g[:, t % 2, :], AX, ALU.max, apply_absolute_value=True)\
                        .then_inc(gscale_made, 1)
                    dve.wait_ge(grms_made, TT * b + t + 1)
                    dve.wait_ge(gscale_made, gs + 1)
                    nc.vector.tensor_tensor(gclip[:, col], gmax[:, col], grms[:, col], ALU.mult).then_inc(gscale_made, 1)
                    dve.wait_ge(gscale_made, gs + 2)
                    nc.vector.tensor_scalar(gclip[:, col], gclip[:, col], QUANT_MIN, None, ALU.max).then_inc(gscale_made, 1)
                    dve.wait_ge(gscale_made, gs + 3)
                    nc.vector.reciprocal(grec[:, col], gclip[:, col]).then_inc(gscale_made, 1)
                    nc.vector.tensor_scalar(gback[:, col], gclip[:, col], 1.0 / 127.0, wmean[:, 1:2], ALU.mult, ALU.mult)\
                        .then_inc(gscale_made, 1)
                    dve.wait_ge(gscale_made, gs + 5)
                    nc.vector.scalar_tensor_tensor(gmul[:, col], grec[:, col], 127.0, grms[:, col], ALU.mult, ALU.mult)\
                        .then_inc(ground_made, 1)
                    dve.wait_ge(ground_made, 2 * (TT * b + t) + 1)
                    dve.wait_ge(gsum_made, TT * b + t + 1)
                    nc.vector.tensor_scalar(g[:, t % 2, :], g[:, t % 2, :], gmul[:, col], ROUND, ALU.mult, ALU.add)\
                        .then_inc(ground_made, 1)
                    dve.wait_ge(ground_made, 2 * (TT * b + t) + 2)
                    if t > 0:
                        dve.wait_ge(tr_done, N_TR * b + TR.index(f"g{t - 1}b") + 1)
                    nc.vector.tensor_scalar(gq[:, :], g[:, t % 2, :], ROUND + 127.0, -ROUND, ALU.min, ALU.add)\
                        .then_inc(gq_made, 1)

                def ffn_residual(b, t):
                    if t == 0:
                        dve.wait_ge(xout_made, b + 1)
                    dve.wait_ge(f2_done, TT * b + t + 1)
                    nc.vector.scalar_tensor_tensor(xout[:, t, :], bank[6 + t % 2][:, :], gback[:, t:t + 1],
                                                   xout[:, t, :], ALU.mult, ALU.add).then_inc(x2_made, 1)

                def body(b, n):
                    for k in range(UNITS):
                        g_, s = divmod(k, TT)
                        if g_ + 1 < NG and s < 2:
                            maxima_of(b, g_ + 1, 2 * s)
                            maxima_of(b, g_ + 1, 2 * s + 1)
                            if s == 1:
                                max_rows(b, g_ + 1)
                        if n is not None:
                            if k == 3:
                                ln_stats(n)
                            if g_ > 0 and s == 3:
                                ln_apply(n, g_ - 1)
                                if g_ == NG - 1:
                                    ln_apply(n, g_)
                        if s == 2 and g_ > 0:
                            normalise(b, g_ - 1)
                    normalise(b, NG - 1)
                    if n is not None:
                        lo_parts(n)
                    residual(b)
                    if n is not None:
                        for s in range(TT):
                            maxima_of(n, 0, s)
                        max_rows(n, 0)
                    if ffn:
                        quantise_x(b, n)
                        ffn_hidden(b, 0)
                        ffn_hidden(b, 1)
                        quantise_g(b, 0)
                        quantise_g(b, 1)
                        ffn_residual(b, 0)
                        ffn_hidden(b, 2)
                        ffn_residual(b, 1)
                        ffn_hidden(b, 3)
                        quantise_g(b, 2)
                        quantise_g(b, 3)
                        ffn_residual(b, 2)
                        ffn_residual(b, 3)

                def prologue():
                    ln_stats(0)
                    for t in range(TT):
                        ln_apply(0, t)
                    lo_parts(0)
                    for s in range(TT):
                        maxima_of(0, 0, s)
                    max_rows(0, 0)

                all_batches(dve, prologue, body)

            @block.gpsimd
            def _(pool):
                def inverse_std(n):
                    pool.wait_ge(meanvar_made, TT * (n + 1))
                    if ffn:
                        wait(pool, z2_made, TT * (n - 1))
                    wait(pool, z_made, TT * n)
                    nc.gpsimd.tensor_tensor(var_eps[:, :], meanvar[:, :, 1], eps[:, :], ALU.add).then_inc(ve_made, 1)
                    pool.wait_ge(ve_made, n + 1)
                    nc.gpsimd.tensor_tensor(rstd[:, :], var_eps[:, :], half[:, :], ALU.pow).then_inc(rstd_made, 1)

                def split_context(n):
                    pool.wait_ge(ctx_landed, 16 * (n + 1))
                    wait(pool, v_job, TT * n)
                    for c in range(KC):
                        nc.gpsimd.tensor_tensor(ctx_hi[:, c, :], ctx_raw[:, c, :], ones[:, 0:1].to_broadcast([P, T]),
                                                ALU.mult).then_inc(ctxhi_made, 1)
                        pool.wait_ge(ctxhi_made, KC * n + c + 1)
                        nc.gpsimd.tensor_tensor(ctx_lo[:, c, :], ctx_raw[:, c, :], ctx_hi[:, c, :], ALU.subtract)\
                            .then_inc(ctx_made, 1)

                def split_output(b, g_):
                    G = NG * b + g_
                    pool.wait_ge(o_normed, G + 1)
                    if g_ == 0:
                        wait(pool, o_job, TT * b)
                        if ffn:
                            wait(pool, f1_done, FB * TT * b)
                    nc.gpsimd.tensor_tensor(o_sb[:, :], o_sb[:, :], qkv_bias[:, 2, g_:g_ + 1].to_broadcast([P, T]),
                                            ALU.add).then_inc(ob_made, 1)
                    pool.wait_ge(ob_made, G + 1)
                    nc.gpsimd.tensor_tensor(oT[:, 0, g_, :], o_sb[:, :], ones[:, 0:1].to_broadcast([P, T]),
                                            ALU.mult).then_inc(ohi_made, 1)
                    pool.wait_ge(ohi_made, G + 1)
                    nc.gpsimd.tensor_tensor(oT[:, 1, g_, :], o_sb[:, :], oT[:, 0, g_, :], ALU.subtract)\
                        .then_inc(o_made, 1)

                def residual_bias(b):
                    pool.wait_ge(xres_landed, 16 * (b + 1))
                    nc.gpsimd.tensor_tensor(xres[:, :, :], xres[:, :, :],
                                            bo_rows[:, :].unsqueeze(1).to_broadcast([P, TT, D]), ALU.add)\
                        .then_inc(xres_made, 1)

                def ffn_norms(b):
                    k = 5 * b
                    wait(pool, zround_made, 5 * (b - 1) + 1)
                    pool.wait_ge(meanvar2_made, TT * (b + 1))
                    var = meanvar[:, :, 1]
                    nc.gpsimd.tensor_tensor(var_eps[:, :], var, eps[:, :], ALU.add).then_inc(rms_step, 1)
                    pool.wait_ge(rms_step, k + 1)
                    nc.gpsimd.tensor_tensor(rstd[:, :], var_eps[:, :], half[:, :], ALU.pow).then_inc(rms_step, 1)
                    pool.wait_ge(rms_step, k + 2)
                    nc.gpsimd.tensor_tensor(rms[:, :], var, rstd[:, :], ALU.mult).then_inc(rms_step, 1)
                    pool.wait_ge(rms_step, k + 3)
                    nc.gpsimd.tensor_tensor(rms[:, :], rms[:, :], rstd[:, :], ALU.mult).then_inc(rms_step, 1)
                    pool.wait_ge(rms_step, k + 4)
                    nc.gpsimd.tensor_tensor(rms[:, :], rms[:, :], eps[:, :], ALU.add).then_inc(rms_step, 1)
                    pool.wait_ge(rms_step, k + 5)
                    nc.gpsimd.tensor_tensor(rms[:, :], rms[:, :], half[:, :], ALU.pow).then_inc(rms_made, 1)
                    wait(pool, out_landed, 16 * b)
                    pool.wait_ge(x1_made, TT * (b + 1))
                    nc.gpsimd.tensor_tensor(xout[:, :, :], xres[:, :, :],
                                            b2_rows[:, :].unsqueeze(1).to_broadcast([P, TT, D]), ALU.add)\
                        .then_inc(xout_made, 1)
                    for t in range(TT):
                        col = slice(t, t + 1)
                        pool.wait_ge(gsum_made, TT * b + t + 1)
                        wait(pool, ground_made, 2 * (TT * b + t - 3) - 1)
                        nc.gpsimd.tensor_tensor(grms[:, col], gsum[:, col], inv_f[:, :], ALU.mult).then_inc(grms_step, 1)
                        pool.wait_ge(grms_step, 2 * (TT * b + t) + 1)
                        nc.gpsimd.tensor_tensor(grms[:, col], grms[:, col], eps[:, col], ALU.add).then_inc(grms_step, 1)
                        pool.wait_ge(grms_step, 2 * (TT * b + t) + 2)
                        nc.gpsimd.tensor_tensor(grms[:, col], grms[:, col], half[:, col], ALU.pow).then_inc(grms_made, 1)

                def body(b, n):
                    residual_bias(b)
                    if n is not None:
                        split_context(n)
                        inverse_std(n)
                    for g_ in range(NG):
                        split_output(b, g_)
                    if ffn:
                        ffn_norms(b)

                def prologue():
                    inverse_std(0)
                    split_context(0)

                all_batches(pool, prologue, body)

        nc.clear_and_free_semaphores(sems)
        nc.all_engine_barrier()


def experts_phase(nc, x_io, idx_in, rw_in, gu_in, gub_in, dw_in, db_in):
    tag = "M_"
    sems = []
    NT = MT // P
    NB = MT // T
    GC = MI // P
    with ExitStack() as ctx:
        def sb(name, shape, dt):
            return ctx.enter_context(nc.sbuf_tensor(tag + name, shape, dt))

        def sem(name):
            sems.append(nc.alloc_semaphore(tag + name))
            return sems[-1]

        acc = sb("acc", [P, NT, D], F32)
        z = sb("z", [P, NT, D], F32)
        xT_hi = sb("xT_hi", [P, KC, MT], F16)
        xT_lo = sb("xT_lo", [P, KC, MT], F16)
        gu_raw = sb("gu_raw", [P, KC, 2 * MI], F32)
        dw_raw = sb("dw_raw", [P, GC, D], F32)
        gu_hi = sb("gu_hi", [P, 2, KC, 2 * MI], F16)
        gu_lo = sb("gu_lo", [P, 2, KC, 2 * MI], F16)
        dw_hi = sb("dw_hi", [P, 2, GC, D], F16)
        dw_lo = sb("dw_lo", [P, 2, GC, D], F16)
        gub = sb("gub", [P, E, 2, GC], F32)
        db = sb("db", [E, D], F32)
        gate = sb("gate", [P, 2, T], F32)
        up = sb("up", [P, 2, T], F32)
        inter = sb("inter", [P, 2, T], F32)
        int_hi = sb("int_hi", [P, 2, GC, T], F16)
        int_lo = sb("int_lo", [P, 2, GC, T], F16)
        idx_i = sb("idx_i", [P, NT, 2], I32)
        idx_f = sb("idx_f", [P, NT, 2], F32)
        rw = sb("rw", [P, NT, E], F32)
        number = sb("number", [P, E], F32)
        named = sb("named", [P, NT, E], F32)
        cw = sb("cw", [P, NT, E], F32)
        cws = sb("cws", [P, NT, E], F32)
        cwT = sb("cwT", [E, MT], F32)
        ident = sb("ident", [P, P], F32)
        half = sb("half", [P, NT], F32)
        eps = sb("eps", [P, NT], F32)
        stats = sb("stats", [P, NT, 6], F32)
        meanvar = sb("meanvar", [P, NT, 2], F32)
        rstd = sb("rstd", [P, NT], F32)
        bank = [ctx.enter_context(nc.psum_tensor(f"{tag}bank{i}", [P, 512], F32)) for i in range(8)]

        x_landed, small_landed = sem("x_landed"), sem("small_landed")
        gu_landed, dw_landed, out_landed = sem("gu_landed"), sem("dw_landed"), sem("out_landed")
        consts, stats_made, meanvar_made, z_made = sem("consts"), sem("stats_made"), sem("meanvar_made"), sem("z_made")
        rstd_step = sem("rstd_step")
        xT_job, xhi_made, xlo_made = sem("xT_job"), sem("xhi_made"), sem("xlo_made")
        cw_step, cwT_job, cwT_made, bias_job, acc_made = sem("cw_step"), sem("cwT_job"), sem("cwT_made"), sem("bias_job"), sem("acc_made")
        guhi_made, gulo_made, dwhi_made, dwlo_made = sem("guhi_made"), sem("gulo_made"), sem("dwhi_made"), sem("dwlo_made")
        gu_job, down_job = sem("gu_job"), sem("down_job")
        gate_made, glu_made, upa_made, up_made = sem("gate_made"), sem("glu_made"), sem("upa_made"), sem("up_made")
        inter_made, ihi_made, ilo_made, gub_made = sem("inter_made"), sem("ihi_made"), sem("ilo_made"), sem("gub_made")
        x_view = x_io[0:NB, :, :].rearrange("b (t p) d -> p (b t) d", p=P)
        STEPS = E * NB * GC

        with nc.Block() as block:
            @block.sync
            def _(sp):
                sp.dma_start(acc[:, :, :], x_view).then_inc(x_landed, 16)
                sp.dma_start(idx_i[:, :, :], idx_in.rearrange("(t p) k -> p t k", p=P)).then_inc(small_landed, 16)
                sp.dma_start(rw[:, :, :], rw_in.rearrange("(t p) e -> p t e", p=P)).then_inc(small_landed, 16)
                sp.dma_start(gub[:, :, :, :], gub_in).then_inc(small_landed, 16)
                sp.dma_start(db[:, :], db_in).then_inc(small_landed, 16)
                for e in range(E):
                    wait(sp, gulo_made, e)
                    sp.dma_start(gu_raw[:, :, :], gu_in[e].rearrange("(c p) n -> p c n", p=P)).then_inc(gu_landed, 16)
                    wait(sp, dwlo_made, e)
                    sp.dma_start(dw_raw[:, :, :], dw_in[e].rearrange("(c p) n -> p c n", p=P)).then_inc(dw_landed, 16)
                for t in range(NT):
                    sp.wait_ge(acc_made, NT + NT * (E - 1) + t + 1)
                    sp.dma_start(x_view[:, t, :], acc[:, t, :]).then_inc(out_landed, 16)
                sp.wait_ge(out_landed, 16 * NT)

            @block.gpsimd
            def _(pool):
                nc.gpsimd.memset(ident[:, :], 0.0).then_inc(consts, 1)
                nc.gpsimd.memset(half[:, :], -0.5).then_inc(consts, 1)
                nc.gpsimd.memset(eps[:, :], LN_EPS).then_inc(consts, 1)
                for e in range(E):
                    nc.gpsimd.memset(number[:, e:e + 1], float(e)).then_inc(consts, 1)
                pool.wait_ge(consts, 3 + E)
                nc.gpsimd.affine_select(out=ident[:, :], in_=ident[:, :], compare_op=ALU.not_equal, fill=1.0, base=0,
                                        pattern=[[-1, P]], channel_multiplier=1).then_inc(consts, 1)
                pool.wait_ge(meanvar_made, NT)
                nc.gpsimd.tensor_tensor(rstd[:, :], meanvar[:, :, 1], eps[:, :], ALU.add).then_inc(rstd_step, 1)
                pool.wait_ge(rstd_step, 1)
                nc.gpsimd.tensor_tensor(rstd[:, :], rstd[:, :], half[:, :], ALU.pow).then_inc(rstd_step, 1)

            @block.tensor
            def _(pe):
                pe.wait_ge(consts, 4 + E)
                for j in range(NB * KC):
                    nb, c = divmod(j, KC)
                    pe.wait_ge(z_made, TT * (nb + 1))
                    wait(pe, xlo_made, j - 3)
                    for t in range(TT):
                        last = nc.tensor.matmul(bank[j % 4][:, P * t:P * t + P], z[:, TT * nb + t, P * c:P * c + P],
                                                ident[:, :], is_transpose=True, start=True, stop=True)
                    last.then_inc(xT_job, 1)
                pe.wait_ge(cw_step, 5)
                for t in range(NT):
                    last = nc.tensor.matmul(bank[4 + t // 4][0:E, P * (t % 4):P * (t % 4) + P], cw[:, t, :], ident[:, :],
                                            is_transpose=True, start=True, stop=True)
                last.then_inc(cwT_job, 1)
                pe.wait_ge(cwT_made, 2)
                for t in range(NT):
                    wait(pe, acc_made, t - 1)
                    nc.tensor.matmul(bank[6 + t % 2][:, :], cwT[:, P * t:P * t + P], db[:, :], start=True, stop=True)\
                        .then_inc(bias_job, 1)

                def product(out, lhs_hi, lhs_lo, rhs_hi, rhs_lo):
                    for c in range(KC):
                        nc.tensor.matmul(out, lhs_hi(c), rhs_hi(c), start=(c == 0), stop=False)
                        nc.tensor.matmul(out, lhs_hi(c), rhs_lo(c), start=False, stop=False)
                        last = nc.tensor.matmul(out, lhs_lo(c), rhs_hi(c), start=False, stop=(c == KC - 1))
                    return last

                def down(e, nb):
                    pe.wait_ge(ilo_made, (e * NB + nb + 1) * GC)
                    pe.wait_ge(dwlo_made, e + 1)
                    for t in range(TT):
                        job = (e * NB + nb) * TT + t
                        pe.wait_ge(acc_made, NT + job - 1)
                        product(bank[6 + t % 2][:, :],
                                lambda k: int_hi[:, nb, k, P * t:P * t + P], lambda k: int_lo[:, nb, k, P * t:P * t + P],
                                lambda k: dw_hi[:, e % 2, k, :], lambda k: dw_lo[:, e % 2, k, :]).then_inc(down_job, 1)

                pe.wait_ge(xlo_made, NB * KC)
                for e in range(E):
                    pe.wait_ge(gulo_made, e + 1)
                    for nb in range(NB):
                        for f in range(GC):
                            step = (e * NB + nb) * GC + f
                            for u in range(2):
                                if u == 0:
                                    wait(pe, gate_made, step - 1)
                                else:
                                    wait(pe, upa_made, step - 1)
                                cols = slice(MI * u + P * f, MI * u + P * f + P)
                                toks = slice(T * nb, T * nb + T)
                                product(bank[2 * (step % 2) + u][:, :],
                                        lambda k: gu_hi[:, e % 2, k, cols], lambda k: gu_lo[:, e % 2, k, cols],
                                        lambda k: xT_hi[:, k, toks], lambda k: xT_lo[:, k, toks]).then_inc(gu_job, 1)
                        if (e, nb) != (0, 0):
                            down(*divmod(e * NB + nb - 1, NB))
                down(E - 1, NB - 1)

            def split_weights_hi(e):
                wait(nc.scalar, down_job, NT * (e - 1))
                nc.scalar.wait_ge(gu_landed, 16 * (e + 1))
                nc.scalar.activation(gu_hi[:, e % 2, :, :], gu_raw[:, :, :], ACT.Copy, scale=WS).then_inc(guhi_made, 1)
                nc.scalar.wait_ge(dw_landed, 16 * (e + 1))
                nc.scalar.activation(dw_hi[:, e % 2, :, :], dw_raw[:, :, :], ACT.Copy, scale=WS).then_inc(dwhi_made, 1)

            @block.scalar
            def _(act):
                for j in range(NB * KC):
                    nb, c = divmod(j, KC)
                    act.wait_ge(xT_job, j + 1)
                    nc.scalar.activation(xT_hi[:, c, T * nb:T * nb + T], bank[j % 4][:, :], ACT.Copy).then_inc(xhi_made, 1)
                act.wait_ge(small_landed, 64)
                nc.scalar.activation(gub[:, :, :, :], gub[:, :, :, :], ACT.Copy, scale=WS).then_inc(gub_made, 1)
                split_weights_hi(0)
                act.wait_ge(cwT_job, 1)
                for i in range(2):
                    nc.scalar.activation(cwT[:, T * i:T * i + T], bank[4 + i][0:E, :], ACT.Copy).then_inc(cwT_made, 1)
                for step in range(STEPS):
                    e, r = divmod(step, NB * GC)
                    nb, f = divmod(r, GC)
                    act.wait_ge(gate_made, step + 1)
                    nc.scalar.activation(gate[:, step % 2, :], gate[:, step % 2, :], ACT.Gelu_apprx_sigmoid,
                                         scale=1.0 / WS).then_inc(glu_made, 1)
                    if step % (NB * GC) == GC and e + 1 < E:
                        split_weights_hi(e + 1)
                    act.wait_ge(inter_made, step + 1)
                    if f == 0:
                        wait(act, down_job, TT * (e * NB + nb - 1))
                    nc.scalar.activation(int_hi[:, nb, f, :], inter[:, step % 2, :], ACT.Copy).then_inc(ihi_made, 1)

            @block.vector
            def _(dve):
                dve.wait_ge(x_landed, 16)
                for t in range(NT):
                    nc.vector.bn_stats(stats[:, t, :], acc[:, t, :]).then_inc(stats_made, 1)
                dve.wait_ge(stats_made, NT)
                for t in range(NT):
                    nc.vector.bn_aggr(meanvar[:, t, :], stats[:, t, :]).then_inc(meanvar_made, 1)
                dve.wait_ge(meanvar_made, NT)
                dve.wait_ge(rstd_step, 2)
                for t in range(NT):
                    nc.vector.tensor_scalar(z[:, t, :], acc[:, t, :], meanvar[:, t, 0:1], rstd[:, t:t + 1],
                                            ALU.subtract, ALU.mult).then_inc(z_made, 1)
                for j in range(NB * KC):
                    nb, c = divmod(j, KC)
                    dve.wait_ge(xhi_made, j + 1)
                    nc.vector.tensor_tensor(xT_lo[:, c, T * nb:T * nb + T], bank[j % 4][:, :],
                                            xT_hi[:, c, T * nb:T * nb + T], ALU.subtract).then_inc(xlo_made, 1)
                dve.wait_ge(small_landed, 64)
                dve.wait_ge(consts, 3 + E)
                nc.vector.tensor_copy(idx_f[:, :, :], idx_i[:, :, :]).then_inc(cw_step, 1)
                dve.wait_ge(cw_step, 1)
                every = number[:, :].unsqueeze(1).to_broadcast([P, NT, E])
                nc.vector.tensor_tensor(named[:, :, :], every, idx_f[:, :, 0:1].to_broadcast([P, NT, E]), ALU.is_equal)\
                    .then_inc(cw_step, 1)
                nc.vector.tensor_tensor(cw[:, :, :], every, idx_f[:, :, 1:2].to_broadcast([P, NT, E]), ALU.is_equal)\
                    .then_inc(cw_step, 1)
                dve.wait_ge(cw_step, 3)
                nc.vector.tensor_tensor(named[:, :, :], named[:, :, :], cw[:, :, :], ALU.add).then_inc(cw_step, 1)
                dve.wait_ge(cw_step, 4)
                nc.vector.tensor_tensor(cw[:, :, :], named[:, :, :], rw[:, :, :], ALU.mult).then_inc(cw_step, 1)
                dve.wait_ge(cw_step, 5)
                nc.vector.tensor_scalar(cws[:, :, :], cw[:, :, :], 1.0 / WS ** 2, None, ALU.mult).then_inc(cw_step, 1)
                dve.wait_ge(cw_step, 6)

                def split_weights_lo(e):
                    dve.wait_ge(guhi_made, e + 1)
                    nc.vector.scalar_tensor_tensor(gu_lo[:, e % 2, :, :].rearrange("p c n -> p (c n)"),
                                                   gu_raw[:, :, :].rearrange("p c n -> p (c n)"), WS,
                                                   gu_hi[:, e % 2, :, :].rearrange("p c n -> p (c n)"),
                                                   ALU.mult, ALU.subtract).then_inc(gulo_made, 1)
                    dve.wait_ge(dwhi_made, e + 1)
                    nc.vector.scalar_tensor_tensor(dw_lo[:, e % 2, :, :].rearrange("p c n -> p (c n)"),
                                                   dw_raw[:, :, :].rearrange("p c n -> p (c n)"), WS,
                                                   dw_hi[:, e % 2, :, :].rearrange("p c n -> p (c n)"),
                                                   ALU.mult, ALU.subtract).then_inc(dwlo_made, 1)

                split_weights_lo(0)
                for t in range(NT):
                    dve.wait_ge(bias_job, t + 1)
                    nc.vector.tensor_tensor(acc[:, t, :], bank[6 + t % 2][:, :], acc[:, t, :], ALU.add)\
                        .then_inc(acc_made, 1)
                dve.wait_ge(gub_made, 1)

                def accumulate(e, nb):
                    for t in range(TT):
                        job = (e * NB + nb) * TT + t
                        tile = TT * nb + t
                        dve.wait_ge(down_job, job + 1)
                        dve.wait_ge(acc_made, NT + job - NT + 1)
                        nc.vector.scalar_tensor_tensor(acc[:, tile, :], bank[6 + t % 2][:, :], cws[:, tile, e:e + 1],
                                                       acc[:, tile, :], ALU.mult, ALU.add).then_inc(acc_made, 1)

                for step in range(STEPS):
                    e, r = divmod(step, NB * GC)
                    nb, f = divmod(r, GC)
                    s = step % 2
                    dve.wait_ge(gu_job, 2 * step + 1)
                    wait(dve, inter_made, step - 1)
                    nc.vector.tensor_scalar(gate[:, s, :], bank[2 * s][:, :], gub[:, e, 0, f:f + 1], 7.0 * WS,
                                            ALU.add, ALU.min).then_inc(gate_made, 1)
                    dve.wait_ge(gu_job, 2 * step + 2)
                    nc.vector.tensor_scalar(up[:, s, :], bank[2 * s + 1][:, :], gub[:, e, 1, f:f + 1], 7.0 * WS,
                                            ALU.add, ALU.min).then_inc(upa_made, 1)
                    dve.wait_ge(upa_made, step + 1)
                    nc.vector.tensor_scalar(up[:, s, :], up[:, s, :], -7.0 * WS, WS, ALU.max, ALU.add)\
                        .then_inc(up_made, 1)
                    dve.wait_ge(up_made, step + 1)
                    dve.wait_ge(glu_made, step + 1)
                    wait(dve, ihi_made, step - 1)
                    wait(dve, ilo_made, step - 1)
                    nc.vector.tensor_tensor(inter[:, s, :], up[:, s, :], gate[:, s, :], ALU.mult).then_inc(inter_made, 1)
                    dve.wait_ge(ihi_made, step + 1)
                    nc.vector.tensor_tensor(int_lo[:, nb, f, :], inter[:, s, :], int_hi[:, nb, f, :], ALU.subtract)\
                        .then_inc(ilo_made, 1)
                    if step % (NB * GC) == GC and e + 1 < E:
                        split_weights_lo(e + 1)
                    if f == GC - 1 and (e, nb) != (0, 0):
                        accumulate(*divmod(e * NB + nb - 1, NB))
                accumulate(E - 1, NB - 1)


def program(nc, a, out):
    mid = nc.dram_tensor("x_after_ffn", (B, T, D), F32, kind="Internal").ap()
    encoder_phase(nc, 0, a["x"], a["ctxT"], mid, a["w0"], a["b0"], a["bo0"], None,
                  (a["w1T"], a["w2T"], a["b1"], a["b2"]))
    encoder_phase(nc, 1, mid, a["ctxT"], out, a["w1"], a["b1q"], a["bo1"], a["mask"], None)
    experts_phase(nc, out, a["idx"], a["rw"], a["gu"], a["gub"], a["dw"], a["db"])


def kernel(**inputs):
    import numpy as np
    import concourse.bacc as bacc
    from concourse import mybir as _mybir
    from concourse.bass_utils import run_bass_kernel_spmd

    i = {k: np.asarray(v) for k, v in inputs.items()}
    per_partition = lambda *bs: np.ascontiguousarray(np.stack([b.reshape(KC, P).T for b in bs], 1))
    gu = i["L1_ffn_gate_up_proj"].reshape(E, D, MI, 2).transpose(0, 1, 3, 2).reshape(E, D, 2 * MI)
    gub = i["L1_ffn_gate_up_proj_bias"].reshape(E, MI // P, P, 2).transpose(2, 0, 3, 1)
    arrays = {
        "x": i["x"],
        "ctxT": i["ctx_1024"].transpose(0, 2, 1),
        "mask": i["mask_BxS2_bk0"].reshape(1, B * T),
        "w0": np.stack([i[f"L0_xattn_W_{n}"] for n in "QKVO"]),
        "b0": per_partition(*[i[f"L0_xattn_b_{n}"] for n in "QKV"]),
        "bo0": i["L0_xattn_b_O"],
        "w1T": i["L0_ffn_w1"].T, "b1": i["L0_ffn_b1"],
        "w2T": i["L0_ffn_w2"].T, "b2": i["L0_ffn_b2"],
        "w1": np.stack([i[f"L1_xattn_W{n}"].T for n in "qkvo"]),
        "b1q": per_partition(*[i[f"L1_xattn_b{n}"] for n in "qkv"]),
        "bo1": i["L1_xattn_bo"],
        "idx": i["L1_ffn_router_indices"],
        "rw": i["L1_ffn_routing_weights"],
        "gu": gu, "gub": gub,
        "dw": i["L1_ffn_down_proj"], "db": i["L1_ffn_down_proj_bias"],
    }
    arrays = {k: np.ascontiguousarray(v) for k, v in arrays.items()}
    nc = bacc.Bacc("TRN2", target_bir_lowering=False, num_devices=1, dynamic_dma_scratch_size=1024)
    aps = {k: nc.dram_tensor("in_" + k, v.shape, _mybir.dt.from_np(v.dtype), kind="ExternalInput").ap()
           for k, v in arrays.items()}
    out = nc.dram_tensor("out", (B, T, D), _mybir.dt.float32, kind="ExternalOutput").ap()
    program(nc, aps, out)
    r = run_bass_kernel_spmd(nc, [{"in_" + k: v for k, v in arrays.items()}], core_ids=[0])
    return r.results[0]["out"]
```

```python
from contextlib import ExitStack

import concourse.bass as bass
from concourse import mybir

F32 = mybir.dt.float32
F16 = mybir.dt.float16
BF16 = mybir.dt.bfloat16
U8 = mybir.dt.uint8
I32 = mybir.dt.int32
ALU = mybir.AluOpType
ACT = mybir.ActivationFunctionType
AX = mybir.AxisListType.X

P = 128
D = 512
T = 512
B = 8
H = 16
DK = D // H
KC = D // P
TT = T // P
HG = P // DK
NG = H // HG
F = 2048
FC = F // P
FB = F // 512
E = 8
MT = 1024
MI = 512
UNITS = NG * TT

LN_EPS = 1e-5
RMS_EPS = 1e-5
QUANT_MIN = 1e-5
ROUND = 12582912.0
WS = 16.0
MS = 512.0
MASKED = 32768.0
ROWS_MAX = 3 * DK + 1
ROWS = ROWS_MAX + 2
NSPLIT = 3 * KC
STK = 16 * 3 * HG
MROWS = 16 * (P // 32)


STEPS_ATTENTION = "X0 X1 X2 X3 P3 K0 K1 K2 K3 Q0 Q1 Q2 Q3 V0 V1 V2 V3 M0 O0 M1 O1 M2 O2 M3 O3 M4 M5".split()
STEPS_FFN = ("X0 X1 X2 X3 P3 K0 K1 K2 K3 O0 O1 O2 O3 S0 V0 V1 V2 V3 N0 C0 C1 C2 C3 Q0 R0 R1 R2 R3 U0 Q1 U1 Z0 "
             "Q2 Q3 U2 Z1 G0 U3 Z2 M0 G1 M1 Z3 M2 G2 M3 M4 G3 M5").split()
M_FIRST = 6


def maxima_in_unit(k):
    return range(M_FIRST, M_FIRST + 2) if k == 0 else range(M_FIRST + k + 1, min(M_FIRST + k + 2, UNITS))


def wait(eng, sem, value):
    if isinstance(value, int) and value <= 0:
        return
    eng.wait_ge(sem, value)


def encoder_phase(nc, layer, x_in, ctxT_in, x_out, w_in, bias_in, bo_in, mask_in, ffn_in):
    ffn = layer == 0
    tag = f"L{layer}_"
    sems = []
    with ExitStack() as ctx:
        def sb(name, shape, dt):
            return ctx.enter_context(nc.sbuf_tensor(tag + name, shape, dt))

        def sem(name):
            sems.append(nc.alloc_semaphore(tag + name))
            return sems[-1]

        w_hi = sb("w_hi", [P, 4, KC, D], F16)
        w_lo = sb("w_lo", [P, 4, KC, D], F16)
        qkv_bias = sb("qkv_bias", [P, 3, KC], F32)
        bo_rows = sb("bo_rows", [P, D], F32)
        ctx_raw = sb("ctx_raw", [P, KC, T], F32)
        ctx_hi = sb("ctx_hi", [P, KC, T], F16)
        ctx_lo = sb("ctx_lo", [P, KC, T], F16)
        xz = sb("xz", [P, TT, D], F32)
        xres = sb("xres", [P, TT, D], F32)
        xout = sb("xout", [P, TT, D], F32)
        xT_hi = sb("xT_hi", [P, KC, T], F16)
        xT_lo = sb("xT_lo", [P, KC, T], F16)
        STAGES = 1 if ffn else 2
        stage_hi = sb("stage_hi", [P, STAGES, KC, T], F16)
        stage_lo = sb("stage_lo", [P, STAGES, KC, T], F16)
        v = sb("v", [P, TT, D], F32)
        q_stack = sb("q_stack", [ROWS, H, T], F16)
        k_stack = sb("k_stack", [ROWS, H, T], F16)
        probs = sb("probs", [P, 2, HG, T], F32)
        oT = sb("oT", [P, 2, NG, T], F16)
        o_sb = sb("o_sb", [P, T], F32)
        sum_sb = sb("sum_sb", [P, T], F32)
        ident = sb("ident", [P, P], F32)
        ones = sb("ones", [P, P], F32)
        stats = sb("stats", [P, TT, 6], F32)
        meanvar = sb("meanvar", [P, TT, 2], F32)
        half = sb("half", [P, TT], F32)
        eps = sb("eps", [P, TT], F32)
        var_eps = sb("var_eps", [P, TT], F32)
        rstd = sb("rstd", [P, TT], F32)
        maxima = sb("maxima", [P, 2, HG, TT], F32)
        m_parts = sb("m_parts", [P, 2 * HG * TT], F16)
        m_rows = sb("m_rows", [P, 2 * HG * TT], F16)
        if ffn:
            w1 = sb("w1", [P, KC, F], BF16)
            w2 = sb("w2", [P, FC, D], BF16)
            b1_rows = sb("b1_rows", [P, F], F32)
            b2_rows = sb("b2_rows", [P, D], F32)
            ident_bf = sb("ident_bf", [P, P], BF16)
            gT = sb("gT", [P, 2, FC, P], BF16)
            gq = sb("gq", [P, F], BF16)
            junk = sb("junk", [P, F], BF16)
            wabs = sb("wabs", [P, 2, 4], F32)
            wtot = sb("wtot", [P, 2], F32)
            wmean = sb("wmean", [P, 2], F32)
            wscale = sb("wscale", [P, 2], F32)
            rms = sb("rms", [P, TT], F32)
            zmax = sb("zmax", [P, TT], F32)
            zclip = sb("zclip", [P, TT], F32)
            zrec = sb("zrec", [P, TT], F32)
            zmul = sb("zmul", [P, TT], F32)
            zback = sb("zback", [P, TT], F32)
            gsum = sb("gsum", [P, TT], F32)
            grms = sb("grms", [P, TT], F32)
            inv_f = sb("inv_f", [P, 1], F32)
            gmax = sb("gmax", [P, TT], F32)
            gclip = sb("gclip", [P, TT], F32)
            grec = sb("grec", [P, TT], F32)
            gmul = sb("gmul", [P, TT], F32)
            gback = sb("gback", [P, TT], F32)
            zq = oT[:, 0, :, :].bitcast(BF16)
            qT = oT[:, 1, :, :].bitcast(BF16)
            g = probs[:, :, :, :].rearrange("p s h t -> p s (h t)")
        else:
            mask_u8 = sb("mask_u8", [1, B * T], U8)
            mask_row = sb("mask_row", [1, B * T], F16)
            kept = sb("kept", [1, B], F32)

        bank = [ctx.enter_context(nc.psum_tensor(f"{tag}bank{i}", [P, 512], F32)) for i in range(8)]
        bf_bank = [bank[i][:, :].bitcast(BF16) for i in range(8)]

        w_landed = [sem(f"w_landed{i}") for i in range(2)]
        small_landed = sem("small_landed")
        w_hi_made = sem("w_hi_made")
        w_lo_made = sem("w_lo_made")
        consts = sem("consts")
        consts2 = sem("consts2")
        bias_scaled = sem("bias_scaled")
        abs_made = sem("abs_made")
        mask_step = sem("mask_step")
        tot_made = sem("tot_made")
        tot_psum = sem("tot_psum")
        mean_made = sem("mean_made")
        tern_step = sem("tern_step")
        tern_made = sem("tern_made")
        stage = probs[:, :, :, :].rearrange("p s h t -> p s (h t)")

        jobs = [(w_in[i].rearrange("(c p) n -> p c n", p=P), "split", i) for i in range(4)]
        if ffn:
            w1T, w2T, b1, b2 = ffn_in
            w_views = [
                [w1T.rearrange("(c p) f -> p c f", p=P)[:, :, 512 * q:512 * q + 512] for q in range(4)],
                [w2T.rearrange("(c p) d -> p c d", p=P)[:, 4 * q:4 * q + 4, :] for q in range(4)],
            ]
            for m in range(2):
                jobs += [(w_views[m][q], "abs", (m, q)) for q in range(4)]
            for m in range(2):
                jobs += [(w_views[m][q], "tern", (m, q)) for q in range(4)]
        n_small = 4 if ffn else 3

        with nc.Block() as block:
            @block.sync
            def _(sp):
                sp.dma_start(qkv_bias[:, :, :], bias_in).then_inc(small_landed, 16)
                sp.dma_start(bo_rows[:, :], bo_in.partition_broadcast(P)).then_inc(small_landed, 16)
                if ffn:
                    sp.dma_start(b1_rows[:, :], b1.partition_broadcast(P)).then_inc(small_landed, 16)
                    sp.dma_start(b2_rows[:, :], b2.partition_broadcast(P)).then_inc(small_landed, 16)
                else:
                    sp.dma_start(mask_u8[:, :], mask_in).then_inc(small_landed, 16)
                for n, (src, kind, i) in enumerate(jobs):
                    if n >= 2:
                        _, kind2, i2 = jobs[n - 2]
                        if kind2 == "split":
                            sp.wait_ge(w_lo_made, n - 1)
                        elif kind2 == "abs":
                            sp.wait_ge(abs_made, 4 * i2[0] + i2[1] + 1)
                        else:
                            sp.wait_ge(tern_made, 4 * i2[0] + i2[1] + 1)
                    sp.dma_start(stage[:, n % 2, :].rearrange("p (c n) -> p c n", c=4), src)\
                      .then_inc(w_landed[n % 2], 16)

            @block.gpsimd
            def _(pool):
                nc.gpsimd.memset(ident[:, :], 0.0).then_inc(consts, 1)
                nc.gpsimd.memset(ones[:, :], 1.0).then_inc(consts, 1)
                nc.gpsimd.memset(half[:, :], -0.5).then_inc(consts, 1)
                nc.gpsimd.memset(eps[:, :], LN_EPS).then_inc(consts, 1)
                pool.wait_ge(consts, 4)
                nc.gpsimd.affine_select(out=ident[:, :], in_=ident[:, :], compare_op=ALU.not_equal,
                                        fill=1.0, base=0, pattern=[[-1, P]], channel_multiplier=1)\
                    .then_inc(consts, 1)
                if ffn:
                    pool.wait_ge(consts, 5)
                    nc.gpsimd.tensor_copy(ident_bf[:, :], ident[:, :]).then_inc(consts, 1)
                    nc.gpsimd.memset(inv_f[:, :], 1.0 / F).then_inc(consts, 1)

            @block.scalar
            def _(act):
                for n in range(4):
                    act.wait_ge(w_landed[n % 2], 16 * (n // 2 + 1))
                    nc.scalar.activation(w_hi[:, n, :, :], stage[:, n % 2, :].rearrange("p (c n) -> p c n", c=4),
                                         ACT.Copy, scale=WS).then_inc(w_hi_made, 1)
                act.wait_ge(small_landed, 16 * n_small)
                nc.scalar.activation(qkv_bias[:, :, :], qkv_bias[:, :, :], ACT.Copy, scale=WS)\
                    .then_inc(bias_scaled, 1)

            @block.tensor
            def _(pe):
                if ffn:
                    pe.wait_ge(consts, 5)
                    pe.wait_ge(tot_made, 1)
                    nc.tensor.matmul(bank[0][:, 0:2], ones[:, :], wtot[:, :], start=True, stop=True)\
                        .then_inc(tot_psum, 1)

            @block.vector
            def _(dve):
                nc.vector.memset(q_stack[96:ROWS, :, :], MASKED).then_inc(consts2, 1)
                nc.vector.memset(k_stack[96:ROWS, :, :], -MS).then_inc(consts2, 1)
                if ffn:
                    dve.wait_ge(consts2, 2)
                    nc.vector.memset(k_stack[96:97, :, :], 0.0).then_inc(consts2, 1)
                else:
                    rows = mask_row[:, :].rearrange("o (b t) -> o b t", b=B)
                    dve.wait_ge(small_landed, 16 * n_small)
                    nc.vector.tensor_scalar(mask_row[:, :], mask_u8[:, :], MASKED, -MASKED, ALU.mult, ALU.add)\
                        .then_inc(mask_step, 1)
                    nc.vector.tensor_reduce(kept[:, :], mask_u8[:, :].rearrange("o (b t) -> o b t", b=B), AX, ALU.add)\
                        .then_inc(mask_step, 1)
                    dve.wait_ge(mask_step, 2)
                    nc.vector.reciprocal(kept[:, :], kept[:, :]).then_inc(mask_step, 1)
                    dve.wait_ge(mask_step, 3)
                    nc.vector.tensor_scalar(kept[:, :], kept[:, :], 0.0, None, ALU.mult).then_inc(mask_step, 1)
                    dve.wait_ge(mask_step, 4)
                    nc.vector.tensor_tensor(rows, rows, kept[:, :].unsqueeze(2).to_broadcast([1, B, T]), ALU.add)\
                        .then_inc(mask_step, 1)
                for n, (src, kind, i) in enumerate(jobs):
                    half_n = stage[:, n % 2, :]
                    dve.wait_ge(w_landed[n % 2], 16 * (n // 2 + 1))
                    if kind == "split":
                        dve.wait_ge(w_hi_made, n + 1)
                        nc.vector.scalar_tensor_tensor(
                            w_lo[:, n, :, :].rearrange("p c n -> p (c n)"), half_n, WS,
                            w_hi[:, n, :, :].rearrange("p c n -> p (c n)"), ALU.mult, ALU.subtract)\
                            .then_inc(w_lo_made, 1)
                    elif kind == "abs":
                        m, q = i
                        nc.vector.tensor_reduce(wabs[:, m, q:q + 1], half_n, AX, ALU.add,
                                                apply_absolute_value=True).then_inc(abs_made, 1)
                        if i == (1, 3):
                            dve.wait_ge(abs_made, 8)
                            nc.vector.tensor_reduce(wtot[:, :], wabs[:, :, :], AX, ALU.add)\
                                .then_inc(tot_made, 1)
                            dve.wait_ge(tot_psum, 1)
                            nc.vector.tensor_scalar(wmean[:, :], bank[0][:, 0:2], 1.0 / (D * F), QUANT_MIN,
                                                    ALU.mult, ALU.max).then_inc(mean_made, 1)
                            dve.wait_ge(mean_made, 1)
                            nc.vector.reciprocal(wscale[:, :], wmean[:, :]).then_inc(mean_made, 1)
                            dve.wait_ge(mean_made, 2)
                    else:
                        m, q = i
                        k = 2 * (4 * m + q)
                        nc.vector.tensor_scalar(half_n, half_n, wscale[:, m:m + 1], ROUND, ALU.mult, ALU.add)\
                            .then_inc(tern_step, 1)
                        dve.wait_ge(tern_step, k + 1)
                        nc.vector.tensor_scalar(half_n, half_n, ROUND + 1.0, ROUND - 1.0, ALU.min, ALU.max)\
                            .then_inc(tern_step, 1)
                        dve.wait_ge(tern_step, k + 2)
                        out = w1[:, :, 512 * q:512 * q + 512] if m == 0 else w2[:, 4 * q:4 * q + 4, :]
                        nc.vector.tensor_scalar(out, half_n.rearrange("p (c n) -> p c n", c=4), -ROUND, None,
                                                ALU.add).then_inc(tern_made, 1)

        xz_landed, xres_landed, ctx_landed = sem("xz_landed"), sem("xres_landed"), sem("ctx_landed")
        q_stack_landed, k_stack_landed = sem("q_stack_landed"), sem("k_stack_landed")
        mask_landed, mrows_landed, out_landed = sem("mask_landed"), sem("mrows_landed"), sem("out_landed")
        scores_done, maxmm_done, pv_done = sem("scores_done"), sem("maxmm_done"), sem("pv_done")
        split_job, v_job, o_job = sem("split_job"), sem("v_job"), sem("o_job")
        exp_done, hi_made, v_made, o_copied = sem("exp_done"), sem("hi_made"), sem("v_made"), sem("o_copied")
        max_made, lo_made, z_made, o_normed = sem("max_made"), sem("lo_made"), sem("z_made"), sem("o_normed")
        x1_made, mhi_made, mlo_made, mrows_made = sem("x1_made"), sem("mhi_made"), sem("mlo_made"), sem("mrows_made")
        stats_made, meanvar_made, sum_inverted = sem("stats_made"), sem("meanvar_made"), sem("sum_inverted")
        ve_made, rstd_made, ctxhi_made, ctx_made = sem("ve_made"), sem("rstd_made"), sem("ctxhi_made"), sem("ctx_made")
        ob_made, ohi_made, o_made, xres_made = sem("ob_made"), sem("ohi_made"), sem("o_made"), sem("xres_made")
        if ffn:
            tr_done, f1_done, f2_done = sem("tr_done"), sem("f1_done"), sem("f2_done")
            tr_copied, gelu_made, gsum_made = sem("tr_copied"), sem("gelu_made"), sem("gsum_made")
            stats2_made, meanvar2_made, z2_made = sem("stats2_made"), sem("meanvar2_made"), sem("z2_made")
            zscale_made, zround_made, zq_made = sem("zscale_made"), sem("zround_made"), sem("zq_made")
            u_made, gscale_made, ground_made, gq_made = sem("u_made"), sem("gscale_made"), sem("ground_made"), sem("gq_made")
            x2_made, xout_made = sem("x2_made"), sem("xout_made")
            rms_step, rms_made, grms_step, grms_made = sem("rms_step"), sem("rms_made"), sem("grms_step"), sem("grms_made")

        gated = sem("gated")
        gate = sb("gate", [P, 1], F32)

        x_dst = xres if ffn else xout
        steps = STEPS_FFN if ffn else STEPS_ATTENTION
        PAIR = [st for st in steps if st[0] in "KQV"]
        RING = []
        for st in steps:
            if st[0] in "OR":
                RING.append(st)
            elif st[0] == "U":
                RING += [f"{st}{j}" for j in range(FB)]
            elif st[0] == "G":
                RING += [f"{st}a", f"{st}b", f"D{st[1]}"]
        RING_BANKS = (2, 3, 6, 7)
        ring_bank = lambda name: RING_BANKS[RING.index(name) % 4]
        TR = [name for name in RING if name[0] in "RG"]
        N_TR = len(TR)
        X_BANKS = (2, 3, 4, 5)
        SPLIT = [f"{a}{c}" for a in "XKQ" for c in range(KC)]
        N_ZS, N_GS = 5, 5

        x_view = x_in.rearrange("b (t p) d -> b p t d", p=P)
        out_view = x_out.rearrange("b (t p) d -> b p t d", p=P)
        ctx_view = ctxT_in.rearrange("b (c p) t -> b p c t", p=P)

        def all_batches(eng, prologue, body, epilogue=None):
            prologue()
            body(0, 1)
            with eng.Fori(1, B - 1) as b:
                body(b, b + 1)
            body(B - 1, None)
            if epilogue is not None:
                epilogue()

        with nc.Block() as block:
            @block.sync
            def _(sp):
                def load_for_next(n):
                    if ffn:
                        wait(sp, zq_made, TT * (n - 1))
                    wait(sp, split_job, NSPLIT * (n - 1) + KC)
                    sp.dma_start(xz[:, :, :], x_view[n, :, :, :]).then_inc(xz_landed, 16)
                    wait(sp, ctx_made, KC * n)
                    sp.dma_start(ctx_raw[:, :, :], ctx_view[n, :, :, :]).then_inc(ctx_landed, 16)

                def stacks(n):
                    for stack, landed, at, place in ((k_stack, k_stack_landed, "K3", 0),
                                                     (q_stack, q_stack_landed, "Q3", STAGES - 1)):
                        mid_, end = (stage_hi, stage_lo) if at == "K3" else (stage_lo, stage_hi)
                        sp.wait_ge(lo_made, NSPLIT * n + SPLIT.index(at) + 1)
                        for r, part in enumerate((stage_hi, mid_, end)):
                            for j in range(HG):
                                sp.dma_start(stack[DK * r:DK * r + DK, j:H:HG, :],
                                             part[DK * j:DK * j + DK, place, :, :]).then_inc(landed, 16)
                        if at == "K3" and not ffn:
                            sp.dma_start(k_stack[96:97, :, :], mask_row[0:1, bass.ds(n * T, T)].unsqueeze(1)
                                         .to_broadcast([1, H, T])).then_inc(mask_landed, 16)

                def m_row_dmas(G, g_):
                    sp.wait_ge(mrows_made, G + 1)
                    for q in range(P // 32):
                        dst = q_stack[97:99, HG * g_:HG * g_ + HG, :]\
                            .rearrange("o h (t i) -> o (h t) i", i=P)[:, :, 32 * q:32 * q + 32]
                        sp.dma_start(dst, m_rows[32 * q:32 * q + 32, 0:32]).then_inc(mrows_landed, 16)

                def prologue():
                    load_for_next(0)
                    stacks(0)
                    m_row_dmas(0, 0)

                def store(b):
                    sp.wait_ge(x2_made if ffn else x1_made, TT * (b + 1))
                    sp.dma_start(out_view[b, :, :, :], xout[:, :, :]).then_inc(out_landed, 16)

                def body(b, n):
                    if n is not None:
                        load_for_next(n)
                    if ffn:
                        wait(sp, xout_made, b)
                        wait(sp, z2_made, TT * b)
                    wait(sp, x1_made, TT * b)
                    sp.dma_start(xres[:, :, :], x_view[b, :, :, :]).then_inc(xres_landed, 16)
                    if not (isinstance(b, int) and b == 0):
                        store(b - 1)
                    for g_ in range(1, NG):
                        m_row_dmas(NG * b + g_, g_)
                    if n is not None:
                        stacks(n)
                        m_row_dmas(NG * n, 0)

                def epilogue():
                    store(B - 1)
                    sp.wait_ge(out_landed, 16 * B)

                all_batches(sp, prologue, body, epilogue)

            @block.tensor
            def _(pe):
                tops = []

                def spread():
                    if tops:
                        next(tops[0], None)

                def product(out, lhs_hi, lhs_lo, rhs_hi, rhs_lo):
                    for c in range(KC):
                        spread()
                        nc.tensor.matmul(out, lhs_hi(c), rhs_hi(c), start=(c == 0), stop=False)
                        nc.tensor.matmul(out, lhs_hi(c), rhs_lo(c), start=False, stop=False)
                        last = nc.tensor.matmul(out, lhs_lo(c), rhs_hi(c), start=False, stop=(c == KC - 1))
                    return last

                def wait_pair(n, name):
                    i = PAIR.index(name)
                    before = PAIR[i - 2] if i >= 2 else None
                    if before is None:
                        wait(pe, exp_done, 2 * UNITS * n)
                    elif before[0] == "V":
                        pe.wait_ge(v_made, TT * n + int(before[1]) + 1)
                    else:
                        pe.wait_ge(lo_made, NSPLIT * n + SPLIT.index(before) + 1)
                    return bank[i % 2]

                def wait_read(b, name):
                    kind, t = name[0], int(name[1])
                    if kind == "O":
                        wait(pe, x1_made, TT * b + t + 1)
                    elif kind == "U":
                        wait(pe, u_made, FB * (TT * b + t) + int(name[2]) + 1)
                    elif kind == "D":
                        wait(pe, x2_made, TT * b + t + 1)
                    else:
                        wait(pe, tr_copied, N_TR * b + TR.index(name) + 1)

                def wait_ring(b, name):
                    i = RING.index(name)
                    if i >= 4:
                        wait_read(b, RING[i - 4])
                    return ring_bank(name)

                def transpose_x(n, c):
                    if c == 0:
                        wait(pe, exp_done, 2 * UNITS * n)
                        wait(pe, max_made, HG * UNITS * n)
                        pe.wait_ge(z_made, TT * (n + 1))
                    for t in range(TT):
                        last = nc.tensor.matmul(bank[X_BANKS[c]][:, P * t:P * t + P], xz[:, t, P * c:P * c + P], ident[:, :],
                                                is_transpose=True, start=True, stop=True)
                    last.then_inc(split_job, 1)

                def project(n, name):
                    which, c = "QK".index(name[0]), int(name[1])
                    dst = wait_pair(n, name)
                    if name == "K0":
                        pe.wait_ge(ctx_made, KC * (n + 1))
                    if name == "Q0":
                        pe.wait_ge(lo_made, NSPLIT * n + KC)
                    src_hi, src_lo = (xT_hi, xT_lo) if which == 0 else (ctx_hi, ctx_lo)
                    cols = slice(P * c, P * c + P)
                    product(dst[:, :],
                            lambda k: w_hi[:, which, k, cols], lambda k: w_lo[:, which, k, cols],
                            lambda k: src_hi[:, k, :], lambda k: src_lo[:, k, :]).then_inc(split_job, 1)

                def values(n, s):
                    dst = wait_pair(n, f"V{s}")
                    product(dst[:, :],
                            lambda k: ctx_hi[:, k, P * s:P * s + P], lambda k: ctx_lo[:, k, P * s:P * s + P],
                            lambda k: w_hi[:, 2, k, :], lambda k: w_lo[:, 2, k, :]).then_inc(v_job, 1)

                def max_mms(n, m):
                    g_, t = divmod(m, TT)
                    if m == 0:
                        pe.wait_ge(k_stack_landed, STK * (n + 1))
                        pe.wait_ge(q_stack_landed, STK * (n + 1))
                        if not ffn:
                            pe.wait_ge(mask_landed, 16 * (n + 1))
                    for i in range(HG):
                        h = HG * g_ + i
                        M = UNITS * HG * n + m * HG + i
                        wait(pe, max_made, M - 1)
                        nc.tensor.matmul(bank[4 + i % 2][:, :], q_stack[0:ROWS_MAX, h, P * t:P * t + P],
                                         k_stack[0:ROWS_MAX, h, :], start=True, stop=True).then_inc(maxmm_done, 1)
                        yield

                def scores(b, k):
                    g_, s = divmod(k, TT)
                    if s == 0:
                        pe.wait_ge(mrows_landed, MROWS * (NG * b + g_ + 1))
                    for i in range(HG):
                        h = HG * g_ + i
                        if i % 2 == 0:
                            if k > 0:
                                pe.wait_ge(exp_done, 2 * (UNITS * b + k - 1) + i // 2 + 1)
                            elif i == 0:
                                pe.wait_ge(lo_made, NSPLIT * (b + 1))
                                pe.wait_ge(v_made, TT * (b + 1))
                            else:
                                for name in RING[-4:]:
                                    if ring_bank(name) in (2, 3):
                                        wait_read(b - 1, name)
                        mm = nc.tensor.matmul(bank[i][:, :], k_stack[0:ROWS, h, P * s:P * s + P],
                                              q_stack[0:ROWS, h, :], start=True, stop=True)
                        if i % 2 == 1:
                            mm.then_inc(scores_done, 1)
                            yield

                def weighted_values(b, k):
                    g_, s = divmod(k, TT)
                    pe.wait_ge(exp_done, 2 * (UNITS * b + k) + 2)
                    if s == 0:
                        wait(pe, o_copied, NG * b + g_)
                        if g_ == 0:
                            for name in RING[-4:]:
                                if ring_bank(name) in (6, 7):
                                    wait_read(b - 1, name)
                    for i in range(HG):
                        rows = slice(DK * i, DK * i + DK)
                        h = HG * g_ + i
                        nc.tensor.matmul(bank[6][rows, :], v[:, s, DK * h:DK * h + DK], probs[:, k % 2, i, :],
                                         start=(s == 0), stop=(s == TT - 1))

                def summed_probs(k):
                    s = k % TT
                    for i in range(HG):
                        rows = slice(DK * i, DK * i + DK)
                        last = nc.tensor.matmul(bank[7][rows, :], ones[:, rows], probs[:, k % 2, i, :],
                                                start=(s == 0), stop=(s == TT - 1))
                    last.then_inc(pv_done, 1)

                def project_out(b, t):
                    if t == 0:
                        pe.wait_ge(o_made, NG * (b + 1))
                        pe.wait_ge(o_copied, NG * (b + 1))
                        pe.wait_ge(exp_done, 2 * UNITS * (b + 1))
                    dst = wait_ring(b, f"O{t}")
                    product(bank[dst][:, :],
                            lambda k: oT[:, 0, k, P * t:P * t + P], lambda k: oT[:, 1, k, P * t:P * t + P],
                            lambda k: w_hi[:, 3, k, :], lambda k: w_lo[:, 3, k, :]).then_inc(o_job, 1)

                def transpose_input(b, t):
                    dst = bf_bank[wait_ring(b, f"R{t}")]
                    pe.wait_ge(zq_made, TT * b + t + 1)
                    for c in range(KC):
                        last = nc.tensor.matmul(dst[:, P * c:P * c + P], zq[:, t, P * c:P * c + P], ident_bf[:, :],
                                                is_transpose=True, start=True, stop=True)
                    last.then_inc(tr_done, 1)

                def ffn_up(b, t):
                    pe.wait_ge(tr_copied, N_TR * b + TR.index(f"R{t}") + 1)
                    for j in range(FB):
                        dst = bank[wait_ring(b, f"U{t}{j}")]
                        spread()
                        for c in range(KC):
                            last = nc.tensor.matmul(dst[:, :], qT[:, c, P * t:P * t + P],
                                                    w1[:, c, 512 * j:512 * j + 512], start=(c == 0), stop=(c == KC - 1))
                        last.then_inc(f1_done, 1)

                def ffn_down(b, t):
                    pe.wait_ge(gq_made, TT * b + t + 1)
                    for half_ in "ab":
                        dst = bf_bank[wait_ring(b, f"G{t}{half_}")]
                        first = 0 if half_ == "a" else 8
                        for c in range(8):
                            cols = slice(P * (first + c), P * (first + c) + P)
                            last = nc.tensor.matmul(dst[:, P * c:P * c + P], gq[:, cols], ident_bf[:, :],
                                                    is_transpose=True, start=True, stop=True)
                        last.then_inc(tr_done, 1)
                    dst = bank[wait_ring(b, f"D{t}")]
                    for c in range(FC):
                        if c % 4 == 0:
                            spread()
                        if c % 8 == 0:
                            pe.wait_ge(tr_copied, N_TR * b + TR.index(f"G{t}{'ab'[c // 8]}") + 1)
                        last = nc.tensor.matmul(dst[:, :], gT[:, t % 2, c, :], w2[:, c, :],
                                                start=(c == 0), stop=(c == FC - 1))
                    last.then_inc(f2_done, 1)

                def between(b, n):
                    for st in steps:
                        kind, i = st[0], int(st[1])
                        if n is not None:
                            if kind == "X":
                                transpose_x(n, i)
                            elif kind in "KQ":
                                project(n, st)
                            elif kind == "V":
                                values(n, i)
                            elif kind == "M":
                                finish_tops()
                                tops.append(max_mms(n, i))
                        if b is not None:
                            if kind == "O":
                                project_out(b, i)
                            elif kind == "R":
                                transpose_input(b, i)
                            elif kind == "U":
                                ffn_up(b, i)
                            elif kind == "G":
                                ffn_down(b, i)
                    finish_tops()

                def finish_tops():
                    while tops:
                        for _ in tops.pop():
                            pass

                def prologue():
                    between(None, 0)

                def body(b, n):
                    for _ in scores(b, 0):
                        pass
                    for k in range(UNITS):
                        pairs = scores(b, k + 1) if k + 1 < UNITS else iter(())
                        tops = (mm for m in maxima_in_unit(k) for mm in max_mms(b, m))
                        next(pairs, None)
                        next(tops, None)
                        next(pairs, None)
                        next(tops, None)
                        weighted_values(b, k)
                        next(tops, None)
                        summed_probs(k)
                        for _ in tops:
                            pass
                    between(b, n)

                all_batches(pe, prologue, body)

            @block.scalar
            def _(act):
                def hi_part(n, name):
                    j, c = SPLIT.index(name), int(name[1])
                    act.wait_ge(split_job, NSPLIT * n + j + 1)
                    if name[0] == "X":
                        nc.scalar.activation(xT_hi[:, c, :], bank[X_BANKS[c]][:, :], ACT.Copy).then_inc(hi_made, 1)
                        return
                    which = "QK".index(name[0])
                    place = 0 if name[0] == "K" else STAGES - 1
                    if STAGES == 2:
                        wait(act, k_stack_landed if which else q_stack_landed, STK * n)
                    elif which:
                        wait(act, q_stack_landed, STK * n)
                    else:
                        wait(act, k_stack_landed, STK * (n + 1))
                    nc.scalar.activation(stage_hi[:, place, c, :], bank[PAIR.index(name) % 2][:, :], ACT.Identity,
                                         bias=qkv_bias[:, which, c:c + 1]).then_inc(hi_made, 1)

                def v_copy(n, s):
                    act.wait_ge(v_job, TT * n + s + 1)
                    nc.scalar.activation(v[:, s, :], bank[PAIR.index(f"V{s}") % 2][:, :], ACT.Copy).then_inc(v_made, 1)

                def o_copies(b, g_):
                    act.wait_ge(pv_done, UNITS * b + TT * (g_ + 1))
                    wait(act, o_made, NG * b + g_)
                    nc.scalar.activation(sum_sb[:, :], bank[7][:, :], ACT.Copy)
                    nc.scalar.activation(o_sb[:, :], bank[6][:, :], ACT.Copy).then_inc(o_copied, 1)

                def body(b, n):
                    if ffn:
                        wait(act, gq_made, TT * b)
                    for k in range(UNITS):
                        g_, s = divmod(k, TT)
                        wait(act, pv_done, UNITS * b + k - 1)
                        for pair in range(2):
                            act.wait_ge(scores_done, 2 * (UNITS * b + k) + pair + 1)
                            for i in (2 * pair, 2 * pair + 1):
                                e = nc.scalar.activation(probs[:, k % 2, i, :], bank[i][:, :], ACT.Exp,
                                                         scale=float(DK) ** -0.5 / WS ** 2)
                            e.then_inc(exp_done, 1)
                        if s == 0 and g_ > 0:
                            o_copies(b, g_ - 1)
                    o_copies(b, NG - 1)
                    between(b, n)

                def copy_transposed(b, name):
                    t = int(name[1])
                    act.wait_ge(tr_done, N_TR * b + TR.index(name) + 1)
                    src = bf_bank[ring_bank(name)]
                    if name[0] == "R":
                        dst = qT[:, :, P * t:P * t + P]
                        src = src[:, 0:KC * P]
                    else:
                        wait(act, f2_done, TT * b + t - 1)
                        dst = gT[:, t % 2, 0:8, :] if name[2] == "a" else gT[:, t % 2, 8:16, :]
                    nc.scalar.activation(dst, src.rearrange("p (c t) -> p c t", t=P), ACT.Copy)\
                        .then_inc(tr_copied, 1)

                def gelu(b, t):
                    act.wait_ge(u_made, FB * (TT * b + t + 1))
                    nc.scalar.activation(g[:, t % 2, :], g[:, t % 2, :], ACT.Gelu).then_inc(gelu_made, 1)
                    act.wait_ge(gelu_made, TT * b + t + 1)
                    wait(act, gsum_made, TT * b + t)
                    nc.scalar.activation(junk[:, :], g[:, t % 2, :], ACT.Square,
                                         accum_out=gsum[:, t:t + 1]).then_inc(gsum_made, 1)

                def between(b, n):
                    for st in steps:
                        kind, i = st[0], int(st[1])
                        if n is not None:
                            if kind in "XKQ":
                                hi_part(n, st)
                            elif kind == "V":
                                v_copy(n, i)
                        if b is not None:
                            if kind == "R":
                                copy_transposed(b, st)
                            elif kind == "Z":
                                gelu(b, i)
                            elif kind == "G":
                                copy_transposed(b, f"{st}a")
                                copy_transposed(b, f"{st}b")

                def prologue():
                    between(None, 0)

                all_batches(act, prologue, body)

            @block.vector
            def _(dve):
                def aggregate_gate(done):
                    wait(dve, gated, done)
                    nc.vector.memset(gate[:, :], 0.0).then_inc(gated, 1)

                def ln_stats(n, t):
                    dve.wait_ge(xz_landed, 16 * (n + 1))
                    nc.vector.bn_stats(stats[:, t, :], xz[:, t, :]).then_inc(stats_made, 1)
                    if t < TT - 1:
                        return
                    wait(dve, rstd_made, n)
                    wait(dve, z_made, TT * n)
                    dve.wait_ge(stats_made, TT * (n + 1))
                    if ffn:
                        wait(dve, z2_made, TT * (n - 1))
                        wait(dve, rms_made, n - 1)
                    aggregate_gate(2 * n - 1 if ffn else n)
                    for t in range(TT):
                        nc.vector.bn_aggr(meanvar[:, t, :], stats[:, t, :]).then_inc(meanvar_made, 1)

                def ln_apply(n, t):
                    dve.wait_ge(rstd_made, n + 1)
                    dve.wait_ge(meanvar_made, TT * (n + 1))
                    nc.vector.tensor_scalar(xz[:, t, :], xz[:, t, :], meanvar[:, t, 0:1], rstd[:, t:t + 1],
                                            ALU.subtract, ALU.mult).then_inc(z_made, 1)

                def lo_part(n, name):
                    j, c = SPLIT.index(name), int(name[1])
                    dve.wait_ge(hi_made, NSPLIT * n + j + 1)
                    if name[0] == "X":
                        nc.vector.tensor_tensor(xT_lo[:, c, :], bank[X_BANKS[c]][:, :], xT_hi[:, c, :], ALU.subtract)\
                            .then_inc(lo_made, 1)
                        return
                    which = "QK".index(name[0])
                    place = 0 if name[0] == "K" else STAGES - 1
                    nc.vector.scalar_tensor_tensor(stage_lo[:, place, c, :], bank[PAIR.index(name) % 2][:, :],
                                                   qkv_bias[:, which, c:c + 1], stage_hi[:, place, c, :],
                                                   ALU.add, ALU.subtract).then_inc(lo_made, 1)

                def maxima_of(n, m):
                    g_, t = divmod(m, TT)
                    if t == 0:
                        wait(dve, mlo_made, NG * n + g_ - 1)
                    for i in range(HG):
                        M = UNITS * HG * n + m * HG + i
                        dve.wait_ge(maxmm_done, M + 1)
                        nc.vector.tensor_reduce(maxima[:, g_ % 2, i, t:t + 1], bank[4 + i % 2][:, :], AX, ALU.max)\
                            .then_inc(max_made, 1)
                    if t == TT - 1:
                        max_rows(n, g_)

                def max_rows(n, g_):
                    G = NG * n + g_
                    half_n = HG * TT
                    dve.wait_ge(max_made, HG * TT * (G + 1))
                    wait(dve, mrows_made, G)
                    src = maxima[:, g_ % 2, :, :].rearrange("p h t -> p (h t)")
                    nc.vector.tensor_scalar(m_parts[:, 0:half_n], src, 1.0 / MS, None, ALU.mult).then_inc(mhi_made, 1)
                    dve.wait_ge(mhi_made, G + 1)
                    nc.vector.scalar_tensor_tensor(m_parts[:, half_n:2 * half_n], src, 1.0 / MS, m_parts[:, 0:half_n],
                                                   ALU.mult, ALU.subtract).then_inc(mlo_made, 1)
                    dve.wait_ge(mlo_made, G + 1)
                    wait(dve, mrows_landed, MROWS * G)
                    nc.vector.transpose(m_rows[:, :], m_parts[:, :]).then_inc(mrows_made, 1)

                def normalise(b, g_, quarter):
                    G = NG * b + g_
                    if quarter == 0:
                        dve.wait_ge(o_copied, G + 1)
                    cols = slice(P * quarter, P * quarter + P)
                    nc.vector.reciprocal(sum_sb[:, cols], sum_sb[:, cols]).then_inc(sum_inverted, 1)
                    dve.wait_ge(sum_inverted, TT * G + quarter + 1)
                    nc.vector.tensor_tensor(o_sb[:, cols], o_sb[:, cols], sum_sb[:, cols], ALU.mult)\
                        .then_inc(o_normed, 1)

                def residual(b, t):
                    if t == 0:
                        dve.wait_ge(xres_made, b + 1)
                        if not ffn:
                            wait(dve, out_landed, 16 * b)
                    dve.wait_ge(o_job, TT * b + t + 1)
                    nc.vector.scalar_tensor_tensor(x_dst[:, t, :], bank[ring_bank(f"O{t}")][:, :], 1.0 / WS ** 2,
                                                   xres[:, t, :], ALU.mult, ALU.add).then_inc(x1_made, 1)

                def input_stats(b, n):
                    dve.wait_ge(x1_made, TT * (b + 1))
                    for t in range(TT):
                        nc.vector.bn_stats(stats[:, t, :], xres[:, t, :]).then_inc(stats2_made, 1)
                    dve.wait_ge(stats2_made, TT * (b + 1))
                    dve.wait_ge(z_made, TT * (b + 1 if n is None else n + 1))
                    aggregate_gate(2 * b + 1 if n is None else 2 * b + 2)
                    for t in range(TT):
                        nc.vector.bn_aggr(meanvar[:, t, :], stats[:, t, :]).then_inc(meanvar2_made, 1)

                def normalise_input(b, n):
                    dve.wait_ge(split_job, NSPLIT * (b + 1) if n is None else NSPLIT * n + KC)
                    dve.wait_ge(rms_step, 5 * b + 2)
                    dve.wait_ge(meanvar2_made, TT * (b + 1))
                    for t in range(TT):
                        nc.vector.tensor_scalar(xz[:, t, :], xres[:, t, :], meanvar[:, t, 0:1], rstd[:, t:t + 1],
                                                ALU.subtract, ALU.mult).then_inc(z2_made, 1)
                    dve.wait_ge(z2_made, TT * (b + 1))
                    zs = N_ZS * b
                    wait(dve, u_made, FB * TT * b)
                    nc.vector.tensor_reduce(zmax[:, :], xz[:, :, :], AX, ALU.max, apply_absolute_value=True)\
                        .then_inc(zscale_made, 1)
                    dve.wait_ge(rms_made, b + 1)
                    dve.wait_ge(zscale_made, zs + 1)
                    nc.vector.tensor_tensor(zclip[:, :], zmax[:, :], rms[:, :], ALU.mult).then_inc(zscale_made, 1)
                    dve.wait_ge(zscale_made, zs + 2)
                    nc.vector.tensor_scalar(zclip[:, :], zclip[:, :], QUANT_MIN, None, ALU.max).then_inc(zscale_made, 1)
                    dve.wait_ge(zscale_made, zs + 3)
                    nc.vector.reciprocal(zrec[:, :], zclip[:, :]).then_inc(zscale_made, 1)
                    nc.vector.tensor_scalar(zback[:, :], zclip[:, :], 1.0 / 127.0, wmean[:, 0:1], ALU.mult, ALU.mult)\
                        .then_inc(zscale_made, 1)
                    dve.wait_ge(zscale_made, zs + 5)
                    nc.vector.scalar_tensor_tensor(zmul[:, :], zrec[:, :], 127.0, rms[:, :], ALU.mult, ALU.mult)\
                        .then_inc(zround_made, 1)

                def quantise_input(b, t):
                    dve.wait_ge(zround_made, 5 * b + 1)
                    nc.vector.tensor_scalar(xz[:, t, :], xz[:, t, :], zmul[:, t:t + 1], ROUND, ALU.mult, ALU.add)\
                        .then_inc(zround_made, 1)
                    dve.wait_ge(zround_made, 5 * b + t + 2)
                    nc.vector.tensor_scalar(zq[:, t, :], xz[:, t, :], ROUND + 127.0, -ROUND, ALU.min, ALU.add)\
                        .then_inc(zq_made, 1)

                def ffn_hidden(b, t):
                    for j in range(FB):
                        dve.wait_ge(f1_done, FB * (TT * b + t) + j + 1)
                        if j == 0:
                            if t >= 2:
                                dve.wait_ge(gq_made, TT * b + t - 1)
                            else:
                                dve.wait_ge(pv_done, UNITS * (b + 1))
                        nc.vector.scalar_tensor_tensor(g[:, t % 2, 512 * j:512 * j + 512],
                                                       bank[ring_bank(f"U{t}{j}")][:, :],
                                                       zback[:, t:t + 1], b1_rows[:, 512 * j:512 * j + 512],
                                                       ALU.mult, ALU.add).then_inc(u_made, 1)

                def quantise_g(b, t):
                    gs = N_GS * (TT * b + t)
                    col = slice(t, t + 1)
                    dve.wait_ge(gelu_made, TT * b + t + 1)
                    if t == 0:
                        wait(dve, x2_made, TT * b)
                    nc.vector.tensor_reduce(gmax[:, col], g[:, t % 2, :], AX, ALU.max, apply_absolute_value=True)\
                        .then_inc(gscale_made, 1)
                    dve.wait_ge(grms_made, TT * b + t + 1)
                    dve.wait_ge(gscale_made, gs + 1)
                    nc.vector.tensor_tensor(gclip[:, col], gmax[:, col], grms[:, col], ALU.mult).then_inc(gscale_made, 1)
                    dve.wait_ge(gscale_made, gs + 2)
                    nc.vector.tensor_scalar(gclip[:, col], gclip[:, col], QUANT_MIN, None, ALU.max).then_inc(gscale_made, 1)
                    dve.wait_ge(gscale_made, gs + 3)
                    nc.vector.reciprocal(grec[:, col], gclip[:, col]).then_inc(gscale_made, 1)
                    nc.vector.tensor_scalar(gback[:, col], gclip[:, col], 1.0 / 127.0, wmean[:, 1:2], ALU.mult, ALU.mult)\
                        .then_inc(gscale_made, 1)
                    dve.wait_ge(gscale_made, gs + 5)
                    nc.vector.scalar_tensor_tensor(gmul[:, col], grec[:, col], 127.0, grms[:, col], ALU.mult, ALU.mult)\
                        .then_inc(ground_made, 1)
                    dve.wait_ge(ground_made, 2 * (TT * b + t) + 1)
                    dve.wait_ge(gsum_made, TT * b + t + 1)
                    nc.vector.tensor_scalar(g[:, t % 2, :], g[:, t % 2, :], gmul[:, col], ROUND, ALU.mult, ALU.add)\
                        .then_inc(ground_made, 1)
                    dve.wait_ge(ground_made, 2 * (TT * b + t) + 2)
                    if t > 0:
                        dve.wait_ge(tr_done, N_TR * b + TR.index(f"G{t - 1}b") + 1)
                    nc.vector.tensor_scalar(gq[:, :], g[:, t % 2, :], ROUND + 127.0, -ROUND, ALU.min, ALU.add)\
                        .then_inc(gq_made, 1)

                def ffn_residual(b, t):
                    if t == 0:
                        dve.wait_ge(xout_made, b + 1)
                    dve.wait_ge(f2_done, TT * b + t + 1)
                    nc.vector.scalar_tensor_tensor(xout[:, t, :], bank[ring_bank(f"D{t}")][:, :], gback[:, t:t + 1],
                                                   xout[:, t, :], ALU.mult, ALU.add).then_inc(x2_made, 1)

                def body(b, n):
                    for k in range(UNITS):
                        g_, s = divmod(k, TT)
                        for m in maxima_in_unit(k):
                            maxima_of(b, m)
                        if g_ > 0:
                            for quarter in ((), (0, 1), (2, 3), ())[s]:
                                normalise(b, g_ - 1, quarter)
                        if n is not None:
                            if k < TT:
                                ln_stats(n, k)
                            if k >= UNITS - TT:
                                ln_apply(n, k - (UNITS - TT))
                    between(b, n)

                def between(b, n):
                    for st in steps:
                        kind, i = st[0], int(st[1])
                        if n is not None:
                            if kind in "XKQ":
                                lo_part(n, st)
                            elif kind == "M":
                                maxima_of(n, i)
                        if b is not None:
                            if kind == "P":
                                for quarter in range(TT):
                                    normalise(b, i, quarter)
                            elif kind == "O":
                                residual(b, i)
                            elif kind == "S":
                                input_stats(b, n)
                            elif kind == "N":
                                normalise_input(b, n)
                            elif kind == "C":
                                quantise_input(b, i)
                            elif kind == "U":
                                ffn_hidden(b, i)
                            elif kind == "Z":
                                quantise_g(b, i)
                            elif kind == "G":
                                ffn_residual(b, i)

                def prologue():
                    for t in range(TT):
                        ln_stats(0, t)
                    for t in range(TT):
                        ln_apply(0, t)
                    between(None, 0)

                all_batches(dve, prologue, body)

            @block.gpsimd
            def _(pool):
                def inverse_std(n):
                    pool.wait_ge(meanvar_made, TT * (n + 1))
                    if ffn:
                        wait(pool, z2_made, TT * (n - 1))
                    wait(pool, z_made, TT * n)
                    nc.gpsimd.tensor_tensor(var_eps[:, :], meanvar[:, :, 1], eps[:, :], ALU.add).then_inc(ve_made, 1)
                    pool.wait_ge(ve_made, n + 1)
                    nc.gpsimd.tensor_tensor(rstd[:, :], var_eps[:, :], half[:, :], ALU.pow).then_inc(rstd_made, 1)

                def split_context(n):
                    pool.wait_ge(ctx_landed, 16 * (n + 1))
                    wait(pool, v_job, TT * n)
                    for c in range(KC):
                        nc.gpsimd.tensor_tensor(ctx_hi[:, c, :], ctx_raw[:, c, :], ones[:, 0:1].to_broadcast([P, T]),
                                                ALU.mult).then_inc(ctxhi_made, 1)
                        pool.wait_ge(ctxhi_made, KC * n + c + 1)
                        nc.gpsimd.tensor_tensor(ctx_lo[:, c, :], ctx_raw[:, c, :], ctx_hi[:, c, :], ALU.subtract)\
                            .then_inc(ctx_made, 1)

                def split_output(b, g_):
                    G = NG * b + g_
                    pool.wait_ge(o_normed, TT * (G + 1))
                    if g_ == 0:
                        wait(pool, o_job, TT * b)
                        if ffn:
                            wait(pool, f1_done, FB * TT * b)
                    nc.gpsimd.tensor_tensor(o_sb[:, :], o_sb[:, :], qkv_bias[:, 2, g_:g_ + 1].to_broadcast([P, T]),
                                            ALU.add).then_inc(ob_made, 1)
                    pool.wait_ge(ob_made, G + 1)
                    nc.gpsimd.tensor_tensor(oT[:, 0, g_, :], o_sb[:, :], ones[:, 0:1].to_broadcast([P, T]),
                                            ALU.mult).then_inc(ohi_made, 1)
                    pool.wait_ge(ohi_made, G + 1)
                    nc.gpsimd.tensor_tensor(oT[:, 1, g_, :], o_sb[:, :], oT[:, 0, g_, :], ALU.subtract)\
                        .then_inc(o_made, 1)

                def residual_bias(b):
                    pool.wait_ge(xres_landed, 16 * (b + 1))
                    nc.gpsimd.tensor_tensor(xres[:, :, :], xres[:, :, :],
                                            bo_rows[:, :].unsqueeze(1).to_broadcast([P, TT, D]), ALU.add)\
                        .then_inc(xres_made, 1)

                def ffn_norms(b):
                    k = 5 * b
                    wait(pool, zround_made, 5 * (b - 1) + 1)
                    pool.wait_ge(meanvar2_made, TT * (b + 1))
                    var = meanvar[:, :, 1]
                    nc.gpsimd.tensor_tensor(var_eps[:, :], var, eps[:, :], ALU.add).then_inc(rms_step, 1)
                    pool.wait_ge(rms_step, k + 1)
                    nc.gpsimd.tensor_tensor(rstd[:, :], var_eps[:, :], half[:, :], ALU.pow).then_inc(rms_step, 1)
                    pool.wait_ge(rms_step, k + 2)
                    nc.gpsimd.tensor_tensor(rms[:, :], var, rstd[:, :], ALU.mult).then_inc(rms_step, 1)
                    pool.wait_ge(rms_step, k + 3)
                    nc.gpsimd.tensor_tensor(rms[:, :], rms[:, :], rstd[:, :], ALU.mult).then_inc(rms_step, 1)
                    pool.wait_ge(rms_step, k + 4)
                    nc.gpsimd.tensor_tensor(rms[:, :], rms[:, :], eps[:, :], ALU.add).then_inc(rms_step, 1)
                    pool.wait_ge(rms_step, k + 5)
                    nc.gpsimd.tensor_tensor(rms[:, :], rms[:, :], half[:, :], ALU.pow).then_inc(rms_made, 1)
                    wait(pool, out_landed, 16 * b)
                    pool.wait_ge(x1_made, TT * (b + 1))
                    nc.gpsimd.tensor_tensor(xout[:, :, :], xres[:, :, :],
                                            b2_rows[:, :].unsqueeze(1).to_broadcast([P, TT, D]), ALU.add)\
                        .then_inc(xout_made, 1)
                    for t in range(TT):
                        col = slice(t, t + 1)
                        pool.wait_ge(gsum_made, TT * b + t + 1)
                        wait(pool, ground_made, 2 * (TT * b + t - 3) - 1)
                        nc.gpsimd.tensor_tensor(grms[:, col], gsum[:, col], inv_f[:, :], ALU.mult).then_inc(grms_step, 1)
                        pool.wait_ge(grms_step, 2 * (TT * b + t) + 1)
                        nc.gpsimd.tensor_tensor(grms[:, col], grms[:, col], eps[:, col], ALU.add).then_inc(grms_step, 1)
                        pool.wait_ge(grms_step, 2 * (TT * b + t) + 2)
                        nc.gpsimd.tensor_tensor(grms[:, col], grms[:, col], half[:, col], ALU.pow).then_inc(grms_made, 1)

                def body(b, n):
                    residual_bias(b)
                    if n is not None:
                        split_context(n)
                        inverse_std(n)
                    for g_ in range(NG):
                        split_output(b, g_)
                    if ffn:
                        ffn_norms(b)

                def prologue():
                    inverse_std(0)
                    split_context(0)

                all_batches(pool, prologue, body)

        nc.clear_and_free_semaphores(sems)
        nc.all_engine_barrier()


def experts_phase(nc, x_io, idx_in, rw_in, gu_in, gub_in, dw_in, db_in):
    tag = "M_"
    sems = []
    NT = MT // P
    NB = MT // T
    GC = MI // P
    with ExitStack() as ctx:
        def sb(name, shape, dt):
            return ctx.enter_context(nc.sbuf_tensor(tag + name, shape, dt))

        def sem(name):
            sems.append(nc.alloc_semaphore(tag + name))
            return sems[-1]

        acc = sb("acc", [P, NT, D], F32)
        z = sb("z", [P, NT, D], F32)
        xT_hi = sb("xT_hi", [P, KC, MT], F16)
        xT_lo = sb("xT_lo", [P, KC, MT], F16)
        gu_raw = sb("gu_raw", [P, KC, 2 * MI], F32)
        dw_raw = sb("dw_raw", [P, GC, D], F32)
        gu_hi = sb("gu_hi", [P, 2, KC, 2 * MI], F16)
        gu_lo = sb("gu_lo", [P, 2, KC, 2 * MI], F16)
        dw_hi = sb("dw_hi", [P, 2, GC, D], F16)
        dw_lo = sb("dw_lo", [P, 2, GC, D], F16)
        gub = sb("gub", [P, E, 2, GC], F32)
        db = sb("db", [E, D], F32)
        gate = sb("gate", [P, 2, T], F32)
        up = sb("up", [P, 2, T], F32)
        inter = sb("inter", [P, 2, T], F32)
        int_hi = sb("int_hi", [P, 2, GC, T], F16)
        int_lo = sb("int_lo", [P, 2, GC, T], F16)
        idx_i = sb("idx_i", [P, NT, 2], I32)
        idx_f = sb("idx_f", [P, NT, 2], F32)
        rw = sb("rw", [P, NT, E], F32)
        number = sb("number", [P, E], F32)
        named = sb("named", [P, NT, E], F32)
        cw = sb("cw", [P, NT, E], F32)
        cws = sb("cws", [P, NT, E], F32)
        cwT = sb("cwT", [E, MT], F32)
        ident = sb("ident", [P, P], F32)
        half = sb("half", [P, NT], F32)
        eps = sb("eps", [P, NT], F32)
        stats = sb("stats", [P, NT, 6], F32)
        meanvar = sb("meanvar", [P, NT, 2], F32)
        rstd = sb("rstd", [P, NT], F32)
        bank = [ctx.enter_context(nc.psum_tensor(f"{tag}bank{i}", [P, 512], F32)) for i in range(8)]

        x_landed, small_landed = sem("x_landed"), sem("small_landed")
        gu_landed, dw_landed, out_landed = sem("gu_landed"), sem("dw_landed"), sem("out_landed")
        consts, stats_made, meanvar_made, z_made = sem("consts"), sem("stats_made"), sem("meanvar_made"), sem("z_made")
        rstd_step = sem("rstd_step")
        xT_job, xhi_made, xlo_made = sem("xT_job"), sem("xhi_made"), sem("xlo_made")
        cw_step, cwT_job, cwT_made, bias_job, acc_made = sem("cw_step"), sem("cwT_job"), sem("cwT_made"), sem("bias_job"), sem("acc_made")
        guhi_made, gulo_made, dwhi_made, dwlo_made = sem("guhi_made"), sem("gulo_made"), sem("dwhi_made"), sem("dwlo_made")
        gu_job, down_job = sem("gu_job"), sem("down_job")
        gate_made, glu_made, upa_made, up_made = sem("gate_made"), sem("glu_made"), sem("upa_made"), sem("up_made")
        inter_made, ihi_made, ilo_made, gub_made = sem("inter_made"), sem("ihi_made"), sem("ilo_made"), sem("gub_made")
        x_view = x_io[0:NB, :, :].rearrange("b (t p) d -> p (b t) d", p=P)
        STEPS = E * NB * GC

        with nc.Block() as block:
            @block.sync
            def _(sp):
                sp.dma_start(acc[:, :, :], x_view).then_inc(x_landed, 16)
                sp.dma_start(idx_i[:, :, :], idx_in.rearrange("(t p) k -> p t k", p=P)).then_inc(small_landed, 16)
                sp.dma_start(rw[:, :, :], rw_in.rearrange("(t p) e -> p t e", p=P)).then_inc(small_landed, 16)
                sp.dma_start(gub[:, :, :, :], gub_in).then_inc(small_landed, 16)
                sp.dma_start(db[:, :], db_in).then_inc(small_landed, 16)
                for e in range(E):
                    wait(sp, gulo_made, e)
                    sp.dma_start(gu_raw[:, :, :], gu_in[e].rearrange("(c p) n -> p c n", p=P)).then_inc(gu_landed, 16)
                    wait(sp, dwlo_made, e)
                    sp.dma_start(dw_raw[:, :, :], dw_in[e].rearrange("(c p) n -> p c n", p=P)).then_inc(dw_landed, 16)
                for t in range(NT):
                    sp.wait_ge(acc_made, NT + NT * (E - 1) + t + 1)
                    sp.dma_start(x_view[:, t, :], acc[:, t, :]).then_inc(out_landed, 16)
                sp.wait_ge(out_landed, 16 * NT)

            @block.gpsimd
            def _(pool):
                nc.gpsimd.memset(ident[:, :], 0.0).then_inc(consts, 1)
                nc.gpsimd.memset(half[:, :], -0.5).then_inc(consts, 1)
                nc.gpsimd.memset(eps[:, :], LN_EPS).then_inc(consts, 1)
                for e in range(E):
                    nc.gpsimd.memset(number[:, e:e + 1], float(e)).then_inc(consts, 1)
                pool.wait_ge(consts, 3 + E)
                nc.gpsimd.affine_select(out=ident[:, :], in_=ident[:, :], compare_op=ALU.not_equal, fill=1.0, base=0,
                                        pattern=[[-1, P]], channel_multiplier=1).then_inc(consts, 1)
                pool.wait_ge(meanvar_made, NT)
                nc.gpsimd.tensor_tensor(rstd[:, :], meanvar[:, :, 1], eps[:, :], ALU.add).then_inc(rstd_step, 1)
                pool.wait_ge(rstd_step, 1)
                nc.gpsimd.tensor_tensor(rstd[:, :], rstd[:, :], half[:, :], ALU.pow).then_inc(rstd_step, 1)

            @block.tensor
            def _(pe):
                pe.wait_ge(consts, 4 + E)
                for j in range(NB * KC):
                    nb, c = divmod(j, KC)
                    pe.wait_ge(z_made, TT * (nb + 1))
                    wait(pe, xlo_made, j - 3)
                    for t in range(TT):
                        last = nc.tensor.matmul(bank[j % 4][:, P * t:P * t + P], z[:, TT * nb + t, P * c:P * c + P],
                                                ident[:, :], is_transpose=True, start=True, stop=True)
                    last.then_inc(xT_job, 1)
                pe.wait_ge(cw_step, 5)
                for t in range(NT):
                    last = nc.tensor.matmul(bank[4 + t // 4][0:E, P * (t % 4):P * (t % 4) + P], cw[:, t, :], ident[:, :],
                                            is_transpose=True, start=True, stop=True)
                last.then_inc(cwT_job, 1)
                pe.wait_ge(cwT_made, 2)
                for t in range(NT):
                    wait(pe, acc_made, t - 1)
                    nc.tensor.matmul(bank[6 + t % 2][:, :], cwT[:, P * t:P * t + P], db[:, :], start=True, stop=True)\
                        .then_inc(bias_job, 1)

                def product(out, lhs_hi, lhs_lo, rhs_hi, rhs_lo):
                    for c in range(KC):
                        nc.tensor.matmul(out, lhs_hi(c), rhs_hi(c), start=(c == 0), stop=False)
                        nc.tensor.matmul(out, lhs_hi(c), rhs_lo(c), start=False, stop=False)
                        last = nc.tensor.matmul(out, lhs_lo(c), rhs_hi(c), start=False, stop=(c == KC - 1))
                    return last

                def down(e, nb):
                    pe.wait_ge(ilo_made, (e * NB + nb + 1) * GC)
                    pe.wait_ge(dwlo_made, e + 1)
                    for t in range(TT):
                        job = (e * NB + nb) * TT + t
                        pe.wait_ge(acc_made, NT + job - 1)
                        product(bank[6 + t % 2][:, :],
                                lambda k: int_hi[:, nb, k, P * t:P * t + P], lambda k: int_lo[:, nb, k, P * t:P * t + P],
                                lambda k: dw_hi[:, e % 2, k, :], lambda k: dw_lo[:, e % 2, k, :]).then_inc(down_job, 1)

                pe.wait_ge(xlo_made, NB * KC)
                for e in range(E):
                    pe.wait_ge(gulo_made, e + 1)
                    for nb in range(NB):
                        for f in range(GC):
                            step = (e * NB + nb) * GC + f
                            for u in range(2):
                                if u == 0:
                                    wait(pe, gate_made, step - 1)
                                else:
                                    wait(pe, upa_made, step - 1)
                                cols = slice(MI * u + P * f, MI * u + P * f + P)
                                toks = slice(T * nb, T * nb + T)
                                product(bank[2 * (step % 2) + u][:, :],
                                        lambda k: gu_hi[:, e % 2, k, cols], lambda k: gu_lo[:, e % 2, k, cols],
                                        lambda k: xT_hi[:, k, toks], lambda k: xT_lo[:, k, toks]).then_inc(gu_job, 1)
                        if (e, nb) != (0, 0):
                            down(*divmod(e * NB + nb - 1, NB))
                down(E - 1, NB - 1)

            def split_weights_hi(e):
                wait(nc.scalar, down_job, NT * (e - 1))
                nc.scalar.wait_ge(gu_landed, 16 * (e + 1))
                nc.scalar.activation(gu_hi[:, e % 2, :, :], gu_raw[:, :, :], ACT.Copy, scale=WS).then_inc(guhi_made, 1)
                nc.scalar.wait_ge(dw_landed, 16 * (e + 1))
                nc.scalar.activation(dw_hi[:, e % 2, :, :], dw_raw[:, :, :], ACT.Copy, scale=WS).then_inc(dwhi_made, 1)

            @block.scalar
            def _(act):
                for j in range(NB * KC):
                    nb, c = divmod(j, KC)
                    act.wait_ge(xT_job, j + 1)
                    nc.scalar.activation(xT_hi[:, c, T * nb:T * nb + T], bank[j % 4][:, :], ACT.Copy).then_inc(xhi_made, 1)
                act.wait_ge(small_landed, 64)
                nc.scalar.activation(gub[:, :, :, :], gub[:, :, :, :], ACT.Copy, scale=WS).then_inc(gub_made, 1)
                split_weights_hi(0)
                act.wait_ge(cwT_job, 1)
                for i in range(2):
                    nc.scalar.activation(cwT[:, T * i:T * i + T], bank[4 + i][0:E, :], ACT.Copy).then_inc(cwT_made, 1)
                for step in range(STEPS):
                    e, r = divmod(step, NB * GC)
                    nb, f = divmod(r, GC)
                    act.wait_ge(gate_made, step + 1)
                    nc.scalar.activation(gate[:, step % 2, :], gate[:, step % 2, :], ACT.Gelu_apprx_sigmoid,
                                         scale=1.0 / WS).then_inc(glu_made, 1)
                    if step % (NB * GC) == GC and e + 1 < E:
                        split_weights_hi(e + 1)
                    act.wait_ge(inter_made, step + 1)
                    if f == 0:
                        wait(act, down_job, TT * (e * NB + nb - 1))
                    nc.scalar.activation(int_hi[:, nb, f, :], inter[:, step % 2, :], ACT.Copy).then_inc(ihi_made, 1)

            @block.vector
            def _(dve):
                dve.wait_ge(x_landed, 16)
                for t in range(NT):
                    nc.vector.bn_stats(stats[:, t, :], acc[:, t, :]).then_inc(stats_made, 1)
                dve.wait_ge(stats_made, NT)
                for t in range(NT):
                    nc.vector.bn_aggr(meanvar[:, t, :], stats[:, t, :]).then_inc(meanvar_made, 1)
                dve.wait_ge(meanvar_made, NT)
                dve.wait_ge(rstd_step, 2)
                for t in range(NT):
                    nc.vector.tensor_scalar(z[:, t, :], acc[:, t, :], meanvar[:, t, 0:1], rstd[:, t:t + 1],
                                            ALU.subtract, ALU.mult).then_inc(z_made, 1)
                for j in range(NB * KC):
                    nb, c = divmod(j, KC)
                    dve.wait_ge(xhi_made, j + 1)
                    nc.vector.tensor_tensor(xT_lo[:, c, T * nb:T * nb + T], bank[j % 4][:, :],
                                            xT_hi[:, c, T * nb:T * nb + T], ALU.subtract).then_inc(xlo_made, 1)
                dve.wait_ge(small_landed, 64)
                dve.wait_ge(consts, 3 + E)
                nc.vector.tensor_copy(idx_f[:, :, :], idx_i[:, :, :]).then_inc(cw_step, 1)
                dve.wait_ge(cw_step, 1)
                every = number[:, :].unsqueeze(1).to_broadcast([P, NT, E])
                nc.vector.tensor_tensor(named[:, :, :], every, idx_f[:, :, 0:1].to_broadcast([P, NT, E]), ALU.is_equal)\
                    .then_inc(cw_step, 1)
                nc.vector.tensor_tensor(cw[:, :, :], every, idx_f[:, :, 1:2].to_broadcast([P, NT, E]), ALU.is_equal)\
                    .then_inc(cw_step, 1)
                dve.wait_ge(cw_step, 3)
                nc.vector.tensor_tensor(named[:, :, :], named[:, :, :], cw[:, :, :], ALU.add).then_inc(cw_step, 1)
                dve.wait_ge(cw_step, 4)
                nc.vector.tensor_tensor(cw[:, :, :], named[:, :, :], rw[:, :, :], ALU.mult).then_inc(cw_step, 1)
                dve.wait_ge(cw_step, 5)
                nc.vector.tensor_scalar(cws[:, :, :], cw[:, :, :], 1.0 / WS ** 2, None, ALU.mult).then_inc(cw_step, 1)
                dve.wait_ge(cw_step, 6)

                def split_weights_lo(e):
                    dve.wait_ge(guhi_made, e + 1)
                    nc.vector.scalar_tensor_tensor(gu_lo[:, e % 2, :, :].rearrange("p c n -> p (c n)"),
                                                   gu_raw[:, :, :].rearrange("p c n -> p (c n)"), WS,
                                                   gu_hi[:, e % 2, :, :].rearrange("p c n -> p (c n)"),
                                                   ALU.mult, ALU.subtract).then_inc(gulo_made, 1)
                    dve.wait_ge(dwhi_made, e + 1)
                    nc.vector.scalar_tensor_tensor(dw_lo[:, e % 2, :, :].rearrange("p c n -> p (c n)"),
                                                   dw_raw[:, :, :].rearrange("p c n -> p (c n)"), WS,
                                                   dw_hi[:, e % 2, :, :].rearrange("p c n -> p (c n)"),
                                                   ALU.mult, ALU.subtract).then_inc(dwlo_made, 1)

                split_weights_lo(0)
                for t in range(NT):
                    dve.wait_ge(bias_job, t + 1)
                    nc.vector.tensor_tensor(acc[:, t, :], bank[6 + t % 2][:, :], acc[:, t, :], ALU.add)\
                        .then_inc(acc_made, 1)
                dve.wait_ge(gub_made, 1)

                def accumulate(e, nb):
                    for t in range(TT):
                        job = (e * NB + nb) * TT + t
                        tile = TT * nb + t
                        dve.wait_ge(down_job, job + 1)
                        dve.wait_ge(acc_made, NT + job - NT + 1)
                        nc.vector.scalar_tensor_tensor(acc[:, tile, :], bank[6 + t % 2][:, :], cws[:, tile, e:e + 1],
                                                       acc[:, tile, :], ALU.mult, ALU.add).then_inc(acc_made, 1)

                for step in range(STEPS):
                    e, r = divmod(step, NB * GC)
                    nb, f = divmod(r, GC)
                    s = step % 2
                    dve.wait_ge(gu_job, 2 * step + 1)
                    wait(dve, inter_made, step - 1)
                    nc.vector.tensor_scalar(gate[:, s, :], bank[2 * s][:, :], gub[:, e, 0, f:f + 1], 7.0 * WS,
                                            ALU.add, ALU.min).then_inc(gate_made, 1)
                    dve.wait_ge(gu_job, 2 * step + 2)
                    nc.vector.tensor_scalar(up[:, s, :], bank[2 * s + 1][:, :], gub[:, e, 1, f:f + 1], 7.0 * WS,
                                            ALU.add, ALU.min).then_inc(upa_made, 1)
                    dve.wait_ge(upa_made, step + 1)
                    nc.vector.tensor_scalar(up[:, s, :], up[:, s, :], -7.0 * WS, WS, ALU.max, ALU.add)\
                        .then_inc(up_made, 1)
                    dve.wait_ge(up_made, step + 1)
                    dve.wait_ge(glu_made, step + 1)
                    wait(dve, ihi_made, step - 1)
                    wait(dve, ilo_made, step - 1)
                    nc.vector.tensor_tensor(inter[:, s, :], up[:, s, :], gate[:, s, :], ALU.mult).then_inc(inter_made, 1)
                    dve.wait_ge(ihi_made, step + 1)
                    nc.vector.tensor_tensor(int_lo[:, nb, f, :], inter[:, s, :], int_hi[:, nb, f, :], ALU.subtract)\
                        .then_inc(ilo_made, 1)
                    if step % (NB * GC) == GC and e + 1 < E:
                        split_weights_lo(e + 1)
                    if f == GC - 1 and (e, nb) != (0, 0):
                        accumulate(*divmod(e * NB + nb - 1, NB))
                accumulate(E - 1, NB - 1)


def program(nc, a, out):
    mid = nc.dram_tensor("x_after_ffn", (B, T, D), F32, kind="Internal").ap()
    encoder_phase(nc, 0, a["x"], a["ctxT"], mid, a["w0"], a["b0"], a["bo0"], None,
                  (a["w1T"], a["w2T"], a["b1"], a["b2"]))
    encoder_phase(nc, 1, mid, a["ctxT"], out, a["w1"], a["b1q"], a["bo1"], a["mask"], None)
    experts_phase(nc, out, a["idx"], a["rw"], a["gu"], a["gub"], a["dw"], a["db"])


def kernel(**inputs):
    import numpy as np
    import concourse.bacc as bacc
    from concourse import mybir as _mybir
    from concourse.bass_utils import run_bass_kernel_spmd

    i = {k: np.asarray(v) for k, v in inputs.items()}
    per_partition = lambda *bs: np.ascontiguousarray(np.stack([b.reshape(KC, P).T for b in bs], 1))
    gu = i["L1_ffn_gate_up_proj"].reshape(E, D, MI, 2).transpose(0, 1, 3, 2).reshape(E, D, 2 * MI)
    gub = i["L1_ffn_gate_up_proj_bias"].reshape(E, MI // P, P, 2).transpose(2, 0, 3, 1)
    arrays = {
        "x": i["x"],
        "ctxT": i["ctx_1024"].transpose(0, 2, 1),
        "mask": i["mask_BxS2_bk0"].reshape(1, B * T),
        "w0": np.stack([i[f"L0_xattn_W_{n}"] for n in "QKVO"]),
        "b0": per_partition(*[i[f"L0_xattn_b_{n}"] for n in "QKV"]),
        "bo0": i["L0_xattn_b_O"],
        "w1T": i["L0_ffn_w1"].T, "b1": i["L0_ffn_b1"],
        "w2T": i["L0_ffn_w2"].T, "b2": i["L0_ffn_b2"],
        "w1": np.stack([i[f"L1_xattn_W{n}"].T for n in "qkvo"]),
        "b1q": per_partition(*[i[f"L1_xattn_b{n}"] for n in "qkv"]),
        "bo1": i["L1_xattn_bo"],
        "idx": i["L1_ffn_router_indices"],
        "rw": i["L1_ffn_routing_weights"],
        "gu": gu, "gub": gub,
        "dw": i["L1_ffn_down_proj"], "db": i["L1_ffn_down_proj_bias"],
    }
    arrays = {k: np.ascontiguousarray(v) for k, v in arrays.items()}
    nc = bacc.Bacc("TRN2", target_bir_lowering=False, num_devices=1, dynamic_dma_scratch_size=1024)
    aps = {k: nc.dram_tensor("in_" + k, v.shape, _mybir.dt.from_np(v.dtype), kind="ExternalInput").ap()
           for k, v in arrays.items()}
    out = nc.dram_tensor("out", (B, T, D), _mybir.dt.float32, kind="ExternalOutput").ap()
    program(nc, aps, out)
    r = run_bass_kernel_spmd(nc, [{"in_" + k: v for k, v in arrays.items()}], core_ids=[0])
    return r.results[0]["out"]
```

```python
from contextlib import ExitStack

import concourse.bass as bass
from concourse import mybir

F32 = mybir.dt.float32
F16 = mybir.dt.float16
BF16 = mybir.dt.bfloat16
U8 = mybir.dt.uint8
I32 = mybir.dt.int32
ALU = mybir.AluOpType
ACT = mybir.ActivationFunctionType
AX = mybir.AxisListType.X

P = 128
D = 512
T = 512
B = 8
H = 16
DK = D // H
KC = D // P
TT = T // P
HG = P // DK
NG = H // HG
F = 2048
FC = F // P
FB = F // 512
E = 8
MT = 1024
MI = 512
UNITS = NG * TT

LN_EPS = 1e-5
RMS_EPS = 1e-5
QUANT_MIN = 1e-5
ROUND = 12582912.0
WS = 16.0
MS = 512.0
MASKED = 32768.0
ROWS_MAX = 3 * DK + 1
ROWS = ROWS_MAX + 2
NSPLIT = 3 * KC
STK = 16 * 3 * KC
MROWS = 16 * (P // 32)


STEPS_ATTENTION = (
    "P0 X0 P1 X1 X2 X3 K0 P2 P3 K1 K2 K3 Q0 Q1 Q2 Q3 O0 V0 M0 V1 M1 O1 M2 O2 M3 V2 M4 V3 M5 "
    "O3"
).split()
STEPS_FFN = (
    "P0 X0 P1 X1 P2 X2 X3 K0 K1 P3 K2 K3 O0 O1 O2 O3 S0 V0 V1 V2 V3 N0 C0 C1 Q0 C2 R0 R1 C3 "
    "U0 Q1 U1 A0 Q2 R2 Z0 Q3 U2 A1 Z1 R3 G0 U3 A2 Z2 G1 M0 M1 A3 Z3 M2 G2 M3 M4 G3 M5"
).split()
M_UNITS = 9


def maxima_in_unit(steps, k):
    first = sum(st[0] == "M" for st in steps)
    twice = UNITS - first - M_UNITS
    if k >= M_UNITS:
        return range(0)
    return range(first + 2 * k, first + 2 * k + 2) if k < twice else range(first + twice + k, first + twice + k + 1)


def wait(eng, sem, value):
    if isinstance(value, int) and value <= 0:
        return
    eng.wait_ge(sem, value)


def encoder_phase(nc, layer, x_in, ctxT_in, x_out, w_in, bias_in, bo_in, mask_in, ffn_in, load_ahead=None):
    ffn = layer == 0
    tag = f"L{layer}_"
    sems = []
    with ExitStack() as ctx:
        def sb(name, shape, dt):
            return ctx.enter_context(nc.sbuf_tensor(tag + name, shape, dt))

        def sem(name):
            sems.append(nc.alloc_semaphore(tag + name))
            return sems[-1]

        w_hi = sb("w_hi", [P, 4, KC, D], F16)
        w_lo = sb("w_lo", [P, 4, KC, D], F16)
        qkv_bias = sb("qkv_bias", [P, 3, KC], F32)
        bo_rows = sb("bo_rows", [P, D], F32)
        ctx_raw = sb("ctx_raw", [P, KC, T], F32)
        ctx_hi = sb("ctx_hi", [P, KC, T], F16)
        ctx_lo = sb("ctx_lo", [P, KC, T], F16)
        xz = sb("xz", [P, TT, D], F32)
        xres = sb("xres", [P, TT, D], F32)
        xout = sb("xout", [P, TT, D], F32)
        xT_hi = sb("xT_hi", [P, KC, T], F16)
        xT_lo = sb("xT_lo", [P, KC, T], F16)
        STAGES = 1 if ffn else 2
        stage_hi = sb("stage_hi", [P, STAGES, KC, T], F16)
        stage_lo = sb("stage_lo", [P, STAGES, KC, T], F16)
        v = sb("v", [P, TT, D], F32)
        q_stack = sb("q_stack", [ROWS, H, T], F16)
        k_stack = sb("k_stack", [ROWS, H, T], F16)
        probs = sb("probs", [P, 2, HG, T], F32)
        oT = sb("oT", [P, 2, NG, T], F16)
        o_sb = sb("o_sb", [P, T], F32)
        sum_sb = sb("sum_sb", [P, T], F32)
        ident = sb("ident", [P, P], F32)
        ones = sb("ones", [P, P], F32)
        stats = sb("stats", [P, TT, 6], F32)
        meanvar = sb("meanvar", [P, TT, 2], F32)
        half = sb("half", [P, TT], F32)
        eps = sb("eps", [P, TT], F32)
        var_eps = sb("var_eps", [P, TT], F32)
        rstd = sb("rstd", [P, TT], F32)
        maxima = sb("maxima", [P, 2, HG, TT], F32)
        m_parts = sb("m_parts", [P, 2 * HG * TT], F16)
        m_rows = sb("m_rows", [P, 2 * HG * TT], F16)
        row_const = sb("row_const", [1, 3, T], F16)
        if ffn:
            w1 = sb("w1", [P, KC, F], BF16)
            w2 = sb("w2", [P, FC, D], BF16)
            b1_rows = sb("b1_rows", [P, F], F32)
            b2_rows = sb("b2_rows", [P, D], F32)
            ident_bf = sb("ident_bf", [P, P], BF16)
            gT = sb("gT", [P, 2, FC, P], BF16)
            gq = sb("gq", [P, F], BF16)
            junk = sb("junk", [P, F], BF16)
            wabs = sb("wabs", [P, 2, 4], F32)
            wtot = sb("wtot", [P, 2], F32)
            wmean = sb("wmean", [P, 2], F32)
            wscale = sb("wscale", [P, 2], F32)
            rms = sb("rms", [P, TT], F32)
            zmax = sb("zmax", [P, TT], F32)
            zclip = sb("zclip", [P, TT], F32)
            zrec = sb("zrec", [P, TT], F32)
            zmul = sb("zmul", [P, TT], F32)
            zback = sb("zback", [P, TT], F32)
            gsum = sb("gsum", [P, TT], F32)
            grms = sb("grms", [P, TT], F32)
            inv_f = sb("inv_f", [P, 1], F32)
            gmax = sb("gmax", [P, TT], F32)
            gclip = sb("gclip", [P, TT], F32)
            grec = sb("grec", [P, TT], F32)
            gmul = sb("gmul", [P, TT], F32)
            gback = sb("gback", [P, TT], F32)
            zq = oT[:, 0, :, :].bitcast(BF16)
            qT = oT[:, 1, :, :].bitcast(BF16)
            g = probs[:, :, :, :].rearrange("p s h t -> p s (h t)")
        else:
            mask_u8 = sb("mask_u8", [1, B * T], U8)
            mask_row = sb("mask_row", [1, B * T], F16)
            kept = sb("kept", [1, B], F32)

        bank = [ctx.enter_context(nc.psum_tensor(f"{tag}bank{i}", [P, 512], F32)) for i in range(8)]
        bf_bank = [bank[i][:, :].bitcast(BF16) for i in range(8)]

        w_landed = [sem(f"w_landed{i}") for i in range(2)]
        small_landed, rows_landed = sem("small_landed"), sem("rows_landed")
        w_hi_made, w_lo_made = sem("w_hi_made"), sem("w_lo_made")
        consts, row_consts, bias_scaled = sem("consts"), sem("row_consts"), sem("bias_scaled")
        N_CONSTS = 7 if ffn else 5
        W_ORDER = (1, 0, 2, 3)
        w_stage = probs[:, :, :, :].rearrange("p s h t -> p s (h t)")
        N_SMALL = 4 if ffn else 3
        if ffn:
            f_landed = [sem(f"f_landed{i}") for i in range(2)]
            abs_made, tot_made, tot_psum, mean_made = sem("abs_made"), sem("tot_made"), sem("tot_psum"), sem("mean_made")
            tern_step, tern_made = sem("tern_step"), sem("tern_made")
            w1T, w2T, b1, b2 = ffn_in
            f_quarters = [w1T.rearrange("(c p) f -> p c f", p=P)[:, :, 512 * q:512 * q + 512] for q in range(4)] \
                + [w2T.rearrange("(c p) d -> p c d", p=P)[:, 4 * q:4 * q + 4, :] for q in range(4)]
            f_stage = (xout[:, :, :], gT[:, :, :, :].bitcast(F32).rearrange("p s c t -> p (s c t)")
                       .rearrange("p (c n) -> p c n", c=4))
            N_F = len(f_quarters)
        else:
            mask_step = sem("mask_step")

        xz_landed, xres_landed, ctx_landed = sem("xz_landed"), sem("xres_landed"), sem("ctx_landed")
        q_stack_landed, k_stack_landed = sem("q_stack_landed"), sem("k_stack_landed")
        mask_landed, mrows_landed, out_landed = sem("mask_landed"), sem("mrows_landed"), sem("out_landed")
        scores_done, maxmm_done, pv_done = sem("scores_done"), sem("maxmm_done"), sem("pv_done")
        split_job, v_job, o_job = sem("split_job"), sem("v_job"), sem("o_job")
        exp_done, hi_made, v_made, o_copied = sem("exp_done"), sem("hi_made"), sem("v_made"), sem("o_copied")
        max_made, lo_made, z_made, o_normed = sem("max_made"), sem("lo_made"), sem("z_made"), sem("o_normed")
        x1_made, mhi_made, mlo_made, mrows_made = sem("x1_made"), sem("mhi_made"), sem("mlo_made"), sem("mrows_made")
        stats_made, meanvar_made, sum_inverted = sem("stats_made"), sem("meanvar_made"), sem("sum_inverted")
        ve_made, rstd_made, ctxhi_made, ctx_made = sem("ve_made"), sem("rstd_made"), sem("ctxhi_made"), sem("ctx_made")
        ob_made, ohi_made, o_made, xres_made = sem("ob_made"), sem("ohi_made"), sem("o_made"), sem("xres_made")
        if ffn:
            tr_done, f1_done, f2_done = sem("tr_done"), sem("f1_done"), sem("f2_done")
            tr_copied, gelu_made, gsum_made = sem("tr_copied"), sem("gelu_made"), sem("gsum_made")
            stats2_made, meanvar2_made, z2_made = sem("stats2_made"), sem("meanvar2_made"), sem("z2_made")
            zscale_made, zround_made, zq_made = sem("zscale_made"), sem("zround_made"), sem("zq_made")
            u_made, gscale_made, ground_made, gq_made = sem("u_made"), sem("gscale_made"), sem("ground_made"), sem("gq_made")
            x2_made, xout_made = sem("x2_made"), sem("xout_made")
            gmax_made = sem("gmax_made")
            rms_step, rms_made, grms_step, grms_made = sem("rms_step"), sem("rms_made"), sem("grms_step"), sem("grms_made")

        gated = sem("gated")
        gate = sb("gate", [P, 1], F32)

        x_dst = xres if ffn else xout
        steps = STEPS_FFN if ffn else STEPS_ATTENTION
        PAIR = [st for st in steps if st[0] in "KQV"]
        RING = []
        for st in steps:
            if st[0] in "OR":
                RING.append(st)
            elif st[0] == "U":
                RING += [f"{st}{j}" for j in range(FB)]
            elif st[0] == "G":
                RING += [f"{st}a", f"{st}b", f"D{st[1]}"]
        RING_BANKS = (2, 3, 6, 7)
        ring_bank = lambda name: RING_BANKS[RING.index(name) % 4]
        TR = [name for name in RING if name[0] in "RG"]
        N_TR = len(TR)
        X_BANKS = (2, 3, 4, 5)
        SPLIT = [f"{a}{c}" for a in "XKQ" for c in range(KC)]
        N_ZS, N_GS = 5, 3

        x_view = x_in.rearrange("b (t p) d -> b p t d", p=P)
        out_view = x_out.rearrange("b (t p) d -> b p t d", p=P)
        ctx_view = ctxT_in.rearrange("b (c p) t -> b p c t", p=P)

        def all_batches(eng, prologue, body, epilogue=None):
            prologue()
            body(0, 1)
            with eng.Fori(1, B - 1) as b:
                body(b, b + 1)
            body(B - 1, None)
            if epilogue is not None:
                epilogue()

        with nc.Block() as block:
            @block.sync
            def _(sp):
                def load_start():
                    load_for_next(0)
                    for n, i in enumerate(W_ORDER):
                        wait(sp, w_lo_made, n - 1)
                        sp.dma_start(w_stage[:, n % 2, :].rearrange("p (c n) -> p c n", c=KC),
                                     w_in[i].rearrange("(c p) n -> p c n", p=P)).then_inc(w_landed[n % 2], 16)
                        if n == 0:
                            sp.dma_start(qkv_bias[:, :, :], bias_in).then_inc(small_landed, 16)
                            sp.dma_start(bo_rows[:, :], bo_in.partition_broadcast(P)).then_inc(small_landed, 16)
                            if ffn:
                                sp.dma_start(b1_rows[:, :], b1.partition_broadcast(P)).then_inc(small_landed, 16)
                                sp.dma_start(b2_rows[:, :], b2.partition_broadcast(P)).then_inc(small_landed, 16)
                            else:
                                sp.dma_start(mask_u8[:, :], mask_in).then_inc(small_landed, 16)
                            sp.wait_ge(row_consts, 3)
                            for stack, row, value in ((q_stack, 96, 0), (k_stack, 97, 1), (k_stack, 98, 1)) + \
                                    (((k_stack, 96, 2),) if ffn else ()):
                                sp.dma_start(stack[row:row + 1, :, :], row_const[:, value:value + 1, :]
                                             .to_broadcast([1, H, T])).then_inc(rows_landed, 16)

                def load_quarter(j):
                    if j >= 2:
                        if j - 2 < N_F:
                            sp.wait_ge(abs_made, j - 1)
                        else:
                            sp.wait_ge(tern_made, j - 1 - N_F)
                    sp.dma_start(f_stage[j % 2], f_quarters[j % N_F]).then_inc(f_landed[j % 2], 16)

                def load_for_next(n):
                    if ffn:
                        wait(sp, zq_made, TT * (n - 1))
                    wait(sp, split_job, NSPLIT * (n - 1) + KC)
                    sp.dma_start(xz[:, :, :], x_view[n, :, :, :]).then_inc(xz_landed, 16)
                    wait(sp, ctx_made, KC * n)
                    sp.dma_start(ctx_raw[:, :, :], ctx_view[n, :, :, :]).then_inc(ctx_landed, 16)

                def stacks(n):
                    for stack, landed, at, place in ((k_stack, k_stack_landed, "K", 0),
                                                     (q_stack, q_stack_landed, "Q", STAGES - 1)):
                        middle, end = (stage_hi, stage_lo) if at == "K" else (stage_lo, stage_hi)
                        if ffn and isinstance(n, int) and n == 0:
                            for j in range(0, 2) if at == "K" else range(6, N_F):
                                load_quarter(j)
                        for c in range(KC):
                            sp.wait_ge(lo_made, NSPLIT * n + SPLIT.index(f"{at}{c}") + 1)
                            for r, part in enumerate((stage_hi, middle, end)):
                                sp.dma_start(stack[DK * r:DK * r + DK, HG * c:HG * c + HG, :],
                                             part[:, place, c, :]).then_inc(landed, 16)
                            if ffn and isinstance(n, int) and n == 0 and at == "K":
                                load_quarter(2 + c)
                        if at == "K" and not ffn:
                            if isinstance(n, int) and n == 0:
                                sp.wait_ge(mask_step, 5)
                            sp.dma_start(k_stack[96:97, :, :], mask_row[0:1, bass.ds(n * T, T)].unsqueeze(1)
                                         .to_broadcast([1, H, T])).then_inc(mask_landed, 16)

                def m_row_dmas(G, g_):
                    sp.wait_ge(mrows_made, G + 1)
                    for q in range(P // 32):
                        dst = q_stack[97:99, HG * g_:HG * g_ + HG, :]\
                            .rearrange("o h (t i) -> o (h t) i", i=P)[:, :, 32 * q:32 * q + 32]
                        sp.dma_start(dst, m_rows[32 * q:32 * q + 32, 0:32]).then_inc(mrows_landed, 16)

                def prologue():
                    load_start()
                    stacks(0)
                    m_row_dmas(0, 0)

                def store(b):
                    sp.wait_ge(x2_made if ffn else x1_made, TT * (b + 1))
                    sp.dma_start(out_view[b, :, :, :], xout[:, :, :]).then_inc(out_landed, 16)

                def body(b, n):
                    if n is not None:
                        load_for_next(n)
                    if ffn:
                        wait(sp, xout_made, b)
                        wait(sp, z2_made, TT * b)
                    wait(sp, x1_made, TT * b)
                    sp.dma_start(xres[:, :, :], x_view[b, :, :, :]).then_inc(xres_landed, 16)
                    if not (isinstance(b, int) and b == 0):
                        store(b - 1)
                    for g_ in range(1, NG):
                        m_row_dmas(NG * b + g_, g_)
                    if n is None and load_ahead is not None:
                        sp.wait_ge(out_landed, 16 * (B - 1))
                        load_ahead(sp)
                    if ffn and isinstance(b, int) and b == 0:
                        for j in range(N_F, 2 * N_F):
                            load_quarter(j)
                    if n is not None:
                        stacks(n)
                        m_row_dmas(NG * n, 0)

                def epilogue():
                    store(B - 1)
                    sp.wait_ge(out_landed, 16 * B)

                all_batches(sp, prologue, body, epilogue)

            @block.tensor
            def _(pe):
                tops = []

                def spread():
                    if tops:
                        next(tops[0], None)

                def product(out, lhs_hi, lhs_lo, rhs_hi, rhs_lo):
                    for c in range(KC):
                        spread()
                        nc.tensor.matmul(out, lhs_hi(c), rhs_hi(c), start=(c == 0), stop=False)
                        nc.tensor.matmul(out, lhs_hi(c), rhs_lo(c), start=False, stop=False)
                        last = nc.tensor.matmul(out, lhs_lo(c), rhs_hi(c), start=False, stop=(c == KC - 1))
                    return last

                def wait_pair(n, name):
                    i = PAIR.index(name)
                    before = PAIR[i - 2] if i >= 2 else None
                    if before is None:
                        wait(pe, exp_done, 2 * UNITS * n)
                    elif before[0] == "V":
                        pe.wait_ge(v_made, TT * n + int(before[1]) + 1)
                    else:
                        pe.wait_ge(lo_made, NSPLIT * n + SPLIT.index(before) + 1)
                    return bank[i % 2]

                def wait_read(b, name):
                    kind, t = name[0], int(name[1])
                    if kind == "O":
                        wait(pe, x1_made, TT * b + t + 1)
                    elif kind == "U":
                        wait(pe, u_made, FB * (TT * b + t) + int(name[2]) + 1)
                    elif kind == "D":
                        wait(pe, x2_made, TT * b + t + 1)
                    else:
                        wait(pe, tr_copied, N_TR * b + TR.index(name) + 1)

                def wait_ring(b, name):
                    i = RING.index(name)
                    if i >= 4:
                        wait_read(b, RING[i - 4])
                    return ring_bank(name)

                def transpose_x(n, c):
                    if c == 0:
                        pe.wait_ge(consts, N_CONSTS)
                        wait(pe, exp_done, 2 * UNITS * n)
                        wait(pe, max_made, HG * UNITS * n)
                        pe.wait_ge(z_made, TT * (n + 1))
                    for t in range(TT):
                        last = nc.tensor.matmul(bank[X_BANKS[c]][:, P * t:P * t + P], xz[:, t, P * c:P * c + P], ident[:, :],
                                                is_transpose=True, start=True, stop=True)
                    last.then_inc(split_job, 1)

                def project(n, name):
                    which, c = "QK".index(name[0]), int(name[1])
                    dst = wait_pair(n, name)
                    if c == 0:
                        pe.wait_ge(w_lo_made, W_ORDER.index(which) + 1)
                    if name == "K0":
                        pe.wait_ge(ctx_made, KC * (n + 1))
                    if name == "Q0":
                        pe.wait_ge(lo_made, NSPLIT * n + KC)
                    src_hi, src_lo = (xT_hi, xT_lo) if which == 0 else (ctx_hi, ctx_lo)
                    cols = slice(P * c, P * c + P)
                    product(dst[:, :],
                            lambda k: w_hi[:, which, k, cols], lambda k: w_lo[:, which, k, cols],
                            lambda k: src_hi[:, k, :], lambda k: src_lo[:, k, :]).then_inc(split_job, 1)

                def values(n, s):
                    dst = wait_pair(n, f"V{s}")
                    pe.wait_ge(w_lo_made, W_ORDER.index(2) + 1)
                    product(dst[:, :],
                            lambda k: ctx_hi[:, k, P * s:P * s + P], lambda k: ctx_lo[:, k, P * s:P * s + P],
                            lambda k: w_hi[:, 2, k, :], lambda k: w_lo[:, 2, k, :]).then_inc(v_job, 1)

                def max_mms(n, m):
                    g_, t = divmod(m, TT)
                    if m == 0:
                        pe.wait_ge(rows_landed, 64 if ffn else 48)
                        pe.wait_ge(k_stack_landed, STK * (n + 1))
                        pe.wait_ge(q_stack_landed, STK * (n + 1))
                        if not ffn:
                            pe.wait_ge(mask_landed, 16 * (n + 1))
                    for i in range(HG):
                        h = HG * g_ + i
                        M = UNITS * HG * n + m * HG + i
                        wait(pe, max_made, M - 1)
                        nc.tensor.matmul(bank[4 + i % 2][:, :], q_stack[0:ROWS_MAX, h, P * t:P * t + P],
                                         k_stack[0:ROWS_MAX, h, :], start=True, stop=True).then_inc(maxmm_done, 1)
                        yield

                def scores(b, k):
                    g_, s = divmod(k, TT)
                    if s == 0:
                        pe.wait_ge(mrows_landed, MROWS * (NG * b + g_ + 1))
                    for i in range(HG):
                        h = HG * g_ + i
                        if i % 2 == 0:
                            if k > 0:
                                pe.wait_ge(exp_done, 2 * (UNITS * b + k - 1) + i // 2 + 1)
                            elif i == 0:
                                pe.wait_ge(lo_made, NSPLIT * (b + 1))
                                pe.wait_ge(v_made, TT * (b + 1))
                            else:
                                for name in RING[-4:]:
                                    if ring_bank(name) in (2, 3):
                                        wait_read(b - 1, name)
                        mm = nc.tensor.matmul(bank[i][:, :], k_stack[0:ROWS, h, P * s:P * s + P],
                                              q_stack[0:ROWS, h, :], start=True, stop=True)
                        if i % 2 == 1:
                            mm.then_inc(scores_done, 1)
                            yield

                def weighted_values(b, k):
                    g_, s = divmod(k, TT)
                    pe.wait_ge(exp_done, 2 * (UNITS * b + k) + 2)
                    if s == 0:
                        wait(pe, o_copied, NG * b + g_)
                        if g_ == 0:
                            for name in RING[-4:]:
                                if ring_bank(name) in (6, 7):
                                    wait_read(b - 1, name)
                    for i in range(HG):
                        rows = slice(DK * i, DK * i + DK)
                        h = HG * g_ + i
                        nc.tensor.matmul(bank[6][rows, :], v[:, s, DK * h:DK * h + DK], probs[:, k % 2, i, :],
                                         start=(s == 0), stop=(s == TT - 1))

                def summed_probs(k):
                    s = k % TT
                    for i in range(HG):
                        rows = slice(DK * i, DK * i + DK)
                        last = nc.tensor.matmul(bank[7][rows, :], ones[:, rows], probs[:, k % 2, i, :],
                                                start=(s == 0), stop=(s == TT - 1))
                    last.then_inc(pv_done, 1)

                def project_out(b, t):
                    if t == 0:
                        pe.wait_ge(w_lo_made, 4)
                        pe.wait_ge(o_made, 2 * NG * (b + 1))
                        pe.wait_ge(o_copied, NG * (b + 1))
                        pe.wait_ge(exp_done, 2 * UNITS * (b + 1))
                    dst = wait_ring(b, f"O{t}")
                    product(bank[dst][:, :],
                            lambda k: oT[:, 0, k, P * t:P * t + P], lambda k: oT[:, 1, k, P * t:P * t + P],
                            lambda k: w_hi[:, 3, k, :], lambda k: w_lo[:, 3, k, :]).then_inc(o_job, 1)

                def transpose_input(b, t):
                    dst = bf_bank[wait_ring(b, f"R{t}")]
                    pe.wait_ge(zq_made, TT * b + t + 1)
                    for c in range(KC):
                        last = nc.tensor.matmul(dst[:, P * c:P * c + P], zq[:, t, P * c:P * c + P], ident_bf[:, :],
                                                is_transpose=True, start=True, stop=True)
                    last.then_inc(tr_done, 1)

                def ffn_up(b, t):
                    pe.wait_ge(tern_made, N_F)
                    pe.wait_ge(tr_copied, N_TR * b + TR.index(f"R{t}") + 1)
                    for j in range(FB):
                        dst = bank[wait_ring(b, f"U{t}{j}")]
                        spread()
                        for c in range(KC):
                            last = nc.tensor.matmul(dst[:, :], qT[:, c, P * t:P * t + P],
                                                    w1[:, c, 512 * j:512 * j + 512], start=(c == 0), stop=(c == KC - 1))
                        last.then_inc(f1_done, 1)

                def ffn_down(b, t):
                    pe.wait_ge(gq_made, TT * b + t + 1)
                    for half_ in "ab":
                        dst = bf_bank[wait_ring(b, f"G{t}{half_}")]
                        first = 0 if half_ == "a" else 8
                        for c in range(8):
                            cols = slice(P * (first + c), P * (first + c) + P)
                            last = nc.tensor.matmul(dst[:, P * c:P * c + P], gq[:, cols], ident_bf[:, :],
                                                    is_transpose=True, start=True, stop=True)
                        last.then_inc(tr_done, 1)
                    dst = bank[wait_ring(b, f"D{t}")]
                    for c in range(FC):
                        if c % 4 == 0:
                            spread()
                        if c % 8 == 0:
                            pe.wait_ge(tr_copied, N_TR * b + TR.index(f"G{t}{'ab'[c // 8]}") + 1)
                        last = nc.tensor.matmul(dst[:, :], gT[:, t % 2, c, :], w2[:, c, :],
                                                start=(c == 0), stop=(c == FC - 1))
                    last.then_inc(f2_done, 1)

                def between(b, n):
                    for st in steps:
                        kind, i = st[0], int(st[1])
                        if n is not None:
                            if kind == "X":
                                transpose_x(n, i)
                            elif kind in "KQ":
                                project(n, st)
                            elif kind == "V":
                                values(n, i)
                            elif kind == "M":
                                if ffn and b is None and i == 0:
                                    pe.wait_ge(tot_made, 1)
                                    nc.tensor.matmul(bank[6][:, 0:2], ones[:, :], wtot[:, :], start=True, stop=True)\
                                        .then_inc(tot_psum, 1)
                                finish_tops()
                                tops.append(max_mms(n, i))
                        if b is not None:
                            if kind == "O":
                                project_out(b, i)
                            elif kind == "R":
                                transpose_input(b, i)
                            elif kind == "U":
                                ffn_up(b, i)
                            elif kind == "G":
                                ffn_down(b, i)
                    finish_tops()

                def finish_tops():
                    while tops:
                        for _ in tops.pop():
                            pass

                def prologue():
                    between(None, 0)

                def body(b, n):
                    for _ in scores(b, 0):
                        pass
                    for k in range(UNITS):
                        pairs = scores(b, k + 1) if k + 1 < UNITS else iter(())
                        tops = (mm for m in maxima_in_unit(steps, k) for mm in max_mms(b, m))
                        next(tops, None)
                        next(pairs, None)
                        next(tops, None)
                        next(pairs, None)
                        next(tops, None)
                        weighted_values(b, k)
                        next(tops, None)
                        summed_probs(k)
                        for _ in tops:
                            pass
                    between(b, n)

                all_batches(pe, prologue, body)

            @block.scalar
            def _(act):
                def split_weights_hi(k):
                    act.wait_ge(w_landed[k % 2], 16 * (k // 2 + 1))
                    nc.scalar.activation(w_hi[:, W_ORDER[k], :, :], w_stage[:, k % 2, :].rearrange("p (c n) -> p c n", c=KC),
                                         ACT.Copy, scale=WS).then_inc(w_hi_made, 1)

                def hi_part(n, name):
                    j, c = SPLIT.index(name), int(name[1])
                    act.wait_ge(split_job, NSPLIT * n + j + 1)
                    if name[0] == "X":
                        nc.scalar.activation(xT_hi[:, c, :], bank[X_BANKS[c]][:, :], ACT.Copy).then_inc(hi_made, 1)
                        return
                    which = "QK".index(name[0])
                    place = 0 if name[0] == "K" else STAGES - 1
                    if STAGES == 2:
                        wait(act, k_stack_landed if which else q_stack_landed, STK * n)
                    elif which:
                        wait(act, q_stack_landed, STK * n)
                    else:
                        wait(act, k_stack_landed, STK * (n + 1))
                    nc.scalar.activation(stage_hi[:, place, c, :], bank[PAIR.index(name) % 2][:, :], ACT.Identity,
                                         bias=qkv_bias[:, which, c:c + 1]).then_inc(hi_made, 1)

                def v_copy(n, s):
                    act.wait_ge(v_job, TT * n + s + 1)
                    nc.scalar.activation(v[:, s, :], bank[PAIR.index(f"V{s}") % 2][:, :], ACT.Copy).then_inc(v_made, 1)

                def o_copies(b, g_):
                    act.wait_ge(pv_done, UNITS * b + TT * (g_ + 1))
                    wait(act, o_made, 2 * (NG * b + g_))
                    nc.scalar.activation(sum_sb[:, :], bank[7][:, :], ACT.Copy)
                    nc.scalar.activation(o_sb[:, :], bank[6][:, :], ACT.Copy).then_inc(o_copied, 1)

                def body(b, n):
                    if ffn:
                        wait(act, gq_made, TT * b)
                    for k in range(UNITS):
                        g_, s = divmod(k, TT)
                        wait(act, pv_done, UNITS * b + k - 1)
                        for pair in range(2):
                            act.wait_ge(scores_done, 2 * (UNITS * b + k) + pair + 1)
                            for i in (2 * pair, 2 * pair + 1):
                                e = nc.scalar.activation(probs[:, k % 2, i, :], bank[i][:, :], ACT.Exp,
                                                         scale=float(DK) ** -0.5 / WS ** 2)
                            e.then_inc(exp_done, 1)
                        if s == 0 and g_ > 0:
                            o_copies(b, g_ - 1)
                    o_copies(b, NG - 1)
                    between(b, n)

                def copy_transposed(b, name):
                    t = int(name[1])
                    act.wait_ge(tr_done, N_TR * b + TR.index(name) + 1)
                    src = bf_bank[ring_bank(name)]
                    if name[0] == "R":
                        dst = qT[:, :, P * t:P * t + P]
                        src = src[:, 0:KC * P]
                    else:
                        wait(act, f2_done, TT * b + t - 1)
                        dst = gT[:, t % 2, 0:8, :] if name[2] == "a" else gT[:, t % 2, 8:16, :]
                    nc.scalar.activation(dst, src.rearrange("p (c t) -> p c t", t=P), ACT.Copy)\
                        .then_inc(tr_copied, 1)

                def gelu(b, t):
                    act.wait_ge(u_made, FB * (TT * b + t + 1))
                    nc.scalar.activation(g[:, t % 2, :], g[:, t % 2, :], ACT.Gelu).then_inc(gelu_made, 1)
                    act.wait_ge(gelu_made, TT * b + t + 1)
                    wait(act, gsum_made, TT * b + t)
                    nc.scalar.activation(junk[:, :], g[:, t % 2, :], ACT.Square,
                                         accum_out=gsum[:, t:t + 1]).then_inc(gsum_made, 1)

                def between(b, n):
                    for st in steps:
                        kind, i = st[0], int(st[1])
                        if n is not None:
                            if kind in "XKQ":
                                if b is None and i == 0:
                                    for k in {"X": (0, 1), "K": (2,), "Q": (3,)}[kind]:
                                        split_weights_hi(k)
                                if b is None and st == "K0":
                                    act.wait_ge(small_landed, 16 * N_SMALL)
                                    nc.scalar.activation(qkv_bias[:, :, :], qkv_bias[:, :, :], ACT.Copy, scale=WS)\
                                        .then_inc(bias_scaled, 1)
                                    act.wait_ge(bias_scaled, 1)
                                hi_part(n, st)
                            elif kind == "V":
                                v_copy(n, i)
                        if b is not None:
                            if kind == "R":
                                copy_transposed(b, st)
                            elif kind == "A":
                                gelu(b, i)
                            elif kind == "G":
                                copy_transposed(b, f"{st}a")
                                copy_transposed(b, f"{st}b")

                def prologue():
                    between(None, 0)

                all_batches(act, prologue, body)

            @block.vector
            def _(dve):
                def aggregate_gate(done):
                    wait(dve, gated, done)
                    nc.vector.memset(gate[:, :], 0.0).then_inc(gated, 1)

                def ln_stats(n, t):
                    dve.wait_ge(xz_landed, 16 * (n + 1))
                    nc.vector.bn_stats(stats[:, t, :], xz[:, t, :]).then_inc(stats_made, 1)
                    if t < TT - 1:
                        return
                    wait(dve, rstd_made, n)
                    wait(dve, z_made, TT * n)
                    dve.wait_ge(stats_made, TT * (n + 1))
                    if ffn:
                        wait(dve, z2_made, TT * (n - 1))
                        wait(dve, rms_made, n - 1)
                    aggregate_gate(2 * n - 1 if ffn else n)
                    for t in range(TT):
                        nc.vector.bn_aggr(meanvar[:, t, :], stats[:, t, :]).then_inc(meanvar_made, 1)

                def ln_apply(n, t):
                    dve.wait_ge(rstd_made, n + 1)
                    dve.wait_ge(meanvar_made, TT * (n + 1))
                    nc.vector.tensor_scalar(xz[:, t, :], xz[:, t, :], meanvar[:, t, 0:1], rstd[:, t:t + 1],
                                            ALU.subtract, ALU.mult).then_inc(z_made, 1)

                def split_weights_lo(k):
                    dve.wait_ge(w_hi_made, k + 1)
                    nc.vector.scalar_tensor_tensor(
                        w_lo[:, W_ORDER[k], :, :].rearrange("p c n -> p (c n)"), w_stage[:, k % 2, :], WS,
                        w_hi[:, W_ORDER[k], :, :].rearrange("p c n -> p (c n)"), ALU.mult, ALU.subtract)\
                        .then_inc(w_lo_made, 1)

                def mask_rows():
                    rows = mask_row[:, :].rearrange("o (b t) -> o b t", b=B)
                    dve.wait_ge(small_landed, 16 * N_SMALL)
                    nc.vector.tensor_scalar(mask_row[:, :], mask_u8[:, :], MASKED, -MASKED, ALU.mult, ALU.add)\
                        .then_inc(mask_step, 1)
                    nc.vector.tensor_reduce(kept[:, :], mask_u8[:, :].rearrange("o (b t) -> o b t", b=B), AX, ALU.add)\
                        .then_inc(mask_step, 1)
                    dve.wait_ge(mask_step, 2)
                    nc.vector.reciprocal(kept[:, :], kept[:, :]).then_inc(mask_step, 1)
                    dve.wait_ge(mask_step, 3)
                    nc.vector.tensor_scalar(kept[:, :], kept[:, :], 0.0, None, ALU.mult).then_inc(mask_step, 1)
                    dve.wait_ge(mask_step, 4)
                    nc.vector.tensor_tensor(rows, rows, kept[:, :].unsqueeze(2).to_broadcast([1, B, T]), ALU.add)\
                        .then_inc(mask_step, 1)

                def quarter_landed(j):
                    dve.wait_ge(f_landed[j % 2], 16 * (j // 2 + 1))

                def absolute_sum(j):
                    quarter_landed(j)
                    nc.vector.tensor_reduce(wabs[:, j // 4, j % 4:j % 4 + 1], f_stage[j % 2].rearrange("p c n -> p (c n)"),
                                            AX, ALU.add, apply_absolute_value=True).then_inc(abs_made, 1)
                    if j == N_F - 1:
                        dve.wait_ge(abs_made, N_F)
                        nc.vector.tensor_reduce(wtot[:, :], wabs[:, :, :], AX, ALU.add).then_inc(tot_made, 1)

                def weight_means():
                    dve.wait_ge(tot_psum, 1)
                    nc.vector.tensor_scalar(wmean[:, :], bank[6][:, 0:2], 1.0 / (D * F), QUANT_MIN,
                                            ALU.mult, ALU.max).then_inc(mean_made, 1)
                    dve.wait_ge(mean_made, 1)
                    nc.vector.reciprocal(wscale[:, :], wmean[:, :]).then_inc(mean_made, 1)

                def ternary(j):
                    m, q = divmod(j, 4)
                    part = f_stage[j % 2]
                    quarter_landed(N_F + j)
                    dve.wait_ge(mean_made, 2)
                    nc.vector.tensor_scalar(part, part, wscale[:, m:m + 1], ROUND, ALU.mult, ALU.add)\
                        .then_inc(tern_step, 1)
                    dve.wait_ge(tern_step, 2 * j + 1)
                    nc.vector.tensor_scalar(part, part, ROUND + 1.0, ROUND - 1.0, ALU.min, ALU.max)\
                        .then_inc(tern_step, 1)
                    dve.wait_ge(tern_step, 2 * j + 2)
                    out = w1[:, :, 512 * q:512 * q + 512] if m == 0 else w2[:, 4 * q:4 * q + 4, :]
                    nc.vector.tensor_scalar(out, part, -ROUND, None, ALU.add).then_inc(tern_made, 1)

                def lo_part(n, name):
                    j, c = SPLIT.index(name), int(name[1])
                    dve.wait_ge(hi_made, NSPLIT * n + j + 1)
                    if name[0] == "X":
                        nc.vector.tensor_tensor(xT_lo[:, c, :], bank[X_BANKS[c]][:, :], xT_hi[:, c, :], ALU.subtract)\
                            .then_inc(lo_made, 1)
                        return
                    which = "QK".index(name[0])
                    place = 0 if name[0] == "K" else STAGES - 1
                    nc.vector.scalar_tensor_tensor(stage_lo[:, place, c, :], bank[PAIR.index(name) % 2][:, :],
                                                   qkv_bias[:, which, c:c + 1], stage_hi[:, place, c, :],
                                                   ALU.add, ALU.subtract).then_inc(lo_made, 1)

                def maxima_of(n, m):
                    g_, t = divmod(m, TT)
                    if t == 0:
                        wait(dve, mlo_made, NG * n + g_ - 1)
                    for i in range(HG):
                        M = UNITS * HG * n + m * HG + i
                        dve.wait_ge(maxmm_done, M + 1)
                        nc.vector.tensor_reduce(maxima[:, g_ % 2, i, t:t + 1], bank[4 + i % 2][:, :], AX, ALU.max)\
                            .then_inc(max_made, 1)
                    if t == TT - 1:
                        max_rows(n, g_)

                def max_rows(n, g_):
                    G = NG * n + g_
                    half_n = HG * TT
                    dve.wait_ge(max_made, HG * TT * (G + 1))
                    wait(dve, mrows_made, G)
                    src = maxima[:, g_ % 2, :, :].rearrange("p h t -> p (h t)")
                    nc.vector.tensor_scalar(m_parts[:, 0:half_n], src, 1.0 / MS, None, ALU.mult).then_inc(mhi_made, 1)
                    dve.wait_ge(mhi_made, G + 1)
                    nc.vector.scalar_tensor_tensor(m_parts[:, half_n:2 * half_n], src, 1.0 / MS, m_parts[:, 0:half_n],
                                                   ALU.mult, ALU.subtract).then_inc(mlo_made, 1)
                    dve.wait_ge(mlo_made, G + 1)
                    wait(dve, mrows_landed, MROWS * G)
                    nc.vector.transpose(m_rows[:, :], m_parts[:, :]).then_inc(mrows_made, 1)

                def invert_sums(b, g_, quarter):
                    G = NG * b + g_
                    if quarter == 0:
                        dve.wait_ge(o_copied, G + 1)
                    cols = slice(P * quarter, P * quarter + P)
                    nc.vector.reciprocal(sum_sb[:, cols], sum_sb[:, cols]).then_inc(sum_inverted, 1)

                def residual(b, t):
                    if t == 0:
                        dve.wait_ge(xres_made, b + 1)
                        if not ffn:
                            wait(dve, out_landed, 16 * b)
                    dve.wait_ge(o_job, TT * b + t + 1)
                    nc.vector.scalar_tensor_tensor(x_dst[:, t, :], bank[ring_bank(f"O{t}")][:, :], 1.0 / WS ** 2,
                                                   xres[:, t, :], ALU.mult, ALU.add).then_inc(x1_made, 1)

                def input_stats(b, n):
                    dve.wait_ge(x1_made, TT * (b + 1))
                    for t in range(TT):
                        nc.vector.bn_stats(stats[:, t, :], xres[:, t, :]).then_inc(stats2_made, 1)
                    dve.wait_ge(stats2_made, TT * (b + 1))
                    dve.wait_ge(z_made, TT * (b + 1 if n is None else n + 1))
                    aggregate_gate(2 * b + 1 if n is None else 2 * b + 2)
                    for t in range(TT):
                        nc.vector.bn_aggr(meanvar[:, t, :], stats[:, t, :]).then_inc(meanvar2_made, 1)

                def normalise_input(b, n):
                    dve.wait_ge(split_job, NSPLIT * (b + 1) if n is None else NSPLIT * n + KC)
                    dve.wait_ge(rms_step, 5 * b + 2)
                    dve.wait_ge(meanvar2_made, TT * (b + 1))
                    for t in range(TT):
                        nc.vector.tensor_scalar(xz[:, t, :], xres[:, t, :], meanvar[:, t, 0:1], rstd[:, t:t + 1],
                                                ALU.subtract, ALU.mult).then_inc(z2_made, 1)
                    dve.wait_ge(z2_made, TT * (b + 1))
                    zs = N_ZS * b
                    wait(dve, u_made, FB * TT * b)
                    nc.vector.tensor_reduce(zmax[:, :], xz[:, :, :], AX, ALU.max, apply_absolute_value=True)\
                        .then_inc(zscale_made, 1)
                    dve.wait_ge(rms_made, b + 1)
                    dve.wait_ge(zscale_made, zs + 1)
                    nc.vector.tensor_tensor(zclip[:, :], zmax[:, :], rms[:, :], ALU.mult).then_inc(zscale_made, 1)
                    dve.wait_ge(zscale_made, zs + 2)
                    nc.vector.tensor_scalar(zclip[:, :], zclip[:, :], QUANT_MIN, None, ALU.max).then_inc(zscale_made, 1)
                    dve.wait_ge(zscale_made, zs + 3)
                    nc.vector.reciprocal(zrec[:, :], zclip[:, :]).then_inc(zscale_made, 1)
                    nc.vector.tensor_scalar(zback[:, :], zclip[:, :], 1.0 / 127.0, wmean[:, 0:1], ALU.mult, ALU.mult)\
                        .then_inc(zscale_made, 1)
                    dve.wait_ge(zscale_made, zs + 5)
                    nc.vector.scalar_tensor_tensor(zmul[:, :], zrec[:, :], 127.0, rms[:, :], ALU.mult, ALU.mult)\
                        .then_inc(zround_made, 1)

                def quantise_input(b, t):
                    dve.wait_ge(zround_made, 5 * b + 1)
                    nc.vector.tensor_scalar(xz[:, t, :], xz[:, t, :], zmul[:, t:t + 1], ROUND, ALU.mult, ALU.add)\
                        .then_inc(zround_made, 1)
                    dve.wait_ge(zround_made, 5 * b + t + 2)
                    nc.vector.tensor_scalar(zq[:, t, :], xz[:, t, :], ROUND + 127.0, -ROUND, ALU.min, ALU.add)\
                        .then_inc(zq_made, 1)

                def ffn_hidden(b, t):
                    for j in range(FB):
                        dve.wait_ge(f1_done, FB * (TT * b + t) + j + 1)
                        if j == 0:
                            if t >= 2:
                                dve.wait_ge(gq_made, TT * b + t - 1)
                            else:
                                dve.wait_ge(pv_done, UNITS * (b + 1))
                        nc.vector.scalar_tensor_tensor(g[:, t % 2, 512 * j:512 * j + 512],
                                                       bank[ring_bank(f"U{t}{j}")][:, :],
                                                       zback[:, t:t + 1], b1_rows[:, 512 * j:512 * j + 512],
                                                       ALU.mult, ALU.add).then_inc(u_made, 1)

                def largest_g(b, t):
                    col = slice(t, t + 1)
                    dve.wait_ge(gelu_made, TT * b + t + 1)
                    if t == 0:
                        wait(dve, x2_made, TT * b)
                    nc.vector.tensor_reduce(gmax[:, col], g[:, t % 2, :], AX, ALU.max, apply_absolute_value=True)\
                        .then_inc(gmax_made, 1)

                def quantise_g(b, t):
                    gs = N_GS * (TT * b + t)
                    col = slice(t, t + 1)
                    dve.wait_ge(gmax_made, TT * b + t + 1)
                    dve.wait_ge(grms_made, TT * b + t + 1)
                    nc.vector.tensor_scalar(gclip[:, col], gmax[:, col], grms[:, col], QUANT_MIN, ALU.mult, ALU.max)\
                        .then_inc(gscale_made, 1)
                    dve.wait_ge(gscale_made, gs + 1)
                    nc.vector.reciprocal(grec[:, col], gclip[:, col]).then_inc(gscale_made, 1)
                    nc.vector.tensor_scalar(gback[:, col], gclip[:, col], 1.0 / 127.0, wmean[:, 1:2], ALU.mult, ALU.mult)\
                        .then_inc(gscale_made, 1)
                    dve.wait_ge(gscale_made, gs + 3)
                    nc.vector.scalar_tensor_tensor(gmul[:, col], grec[:, col], 127.0, grms[:, col], ALU.mult, ALU.mult)\
                        .then_inc(ground_made, 1)
                    dve.wait_ge(ground_made, 2 * (TT * b + t) + 1)
                    dve.wait_ge(gsum_made, TT * b + t + 1)
                    nc.vector.tensor_scalar(g[:, t % 2, :], g[:, t % 2, :], gmul[:, col], ROUND, ALU.mult, ALU.add)\
                        .then_inc(ground_made, 1)
                    dve.wait_ge(ground_made, 2 * (TT * b + t) + 2)
                    if t > 0:
                        dve.wait_ge(tr_done, N_TR * b + TR.index(f"G{t - 1}b") + 1)
                    nc.vector.tensor_scalar(gq[:, :], g[:, t % 2, :], ROUND + 127.0, -ROUND, ALU.min, ALU.add)\
                        .then_inc(gq_made, 1)

                def ffn_residual(b, t):
                    if t == 0:
                        dve.wait_ge(xout_made, b + 1)
                    dve.wait_ge(f2_done, TT * b + t + 1)
                    nc.vector.scalar_tensor_tensor(xout[:, t, :], bank[ring_bank(f"D{t}")][:, :], gback[:, t:t + 1],
                                                   xout[:, t, :], ALU.mult, ALU.add).then_inc(x2_made, 1)

                def body(b, n):
                    for k in range(UNITS):
                        g_, s = divmod(k, TT)
                        for m in maxima_in_unit(steps, k):
                            maxima_of(b, m)
                        if g_ > 0:
                            for quarter in ((), (0, 1), (2, 3), ())[s]:
                                invert_sums(b, g_ - 1, quarter)
                        if n is not None:
                            if k < TT:
                                ln_stats(n, k)
                            if k >= UNITS - TT:
                                ln_apply(n, k - (UNITS - TT))
                        if ffn and isinstance(b, int) and b == 0 and 9 <= k < 15:
                            ternary(k - 9)
                    between(b, n)

                def between(b, n):
                    for st in steps:
                        kind, i = st[0], int(st[1])
                        if n is not None:
                            if kind in "XKQ":
                                if b is None and i == 0:
                                    for k in {"X": (0, 1), "K": (2,), "Q": (3,)}[kind]:
                                        split_weights_lo(k)
                                if b is None and st == "K0":
                                    dve.wait_ge(bias_scaled, 1)
                                    if not ffn:
                                        mask_rows()
                                lo_part(n, st)
                                if ffn and b is None and kind in "KQ":
                                    absolute_sum(4 * "KQ".index(kind) + i)
                            elif kind == "M":
                                if ffn and b is None and i == 0:
                                    weight_means()
                                maxima_of(n, i)
                        if b is not None:
                            if kind == "P":
                                invert_sums(b, NG - 1, i)
                            elif kind == "O":
                                residual(b, i)
                            elif kind == "S":
                                if isinstance(b, int) and b == 0:
                                    ternary(6)
                                    ternary(7)
                                input_stats(b, n)
                            elif kind == "N":
                                normalise_input(b, n)
                            elif kind == "C":
                                quantise_input(b, i)
                            elif kind == "U":
                                ffn_hidden(b, i)
                            elif kind == "A":
                                largest_g(b, i)
                            elif kind == "Z":
                                quantise_g(b, i)
                            elif kind == "G":
                                ffn_residual(b, i)

                def prologue():
                    for t in range(TT):
                        ln_stats(0, t)
                    for t in range(TT):
                        ln_apply(0, t)
                    between(None, 0)

                all_batches(dve, prologue, body)

            @block.gpsimd
            def _(pool):
                def inverse_std(n):
                    pool.wait_ge(meanvar_made, TT * (n + 1))
                    if ffn:
                        wait(pool, z2_made, TT * (n - 1))
                    wait(pool, z_made, TT * n)
                    nc.gpsimd.tensor_tensor(var_eps[:, :], meanvar[:, :, 1], eps[:, :], ALU.add).then_inc(ve_made, 1)
                    pool.wait_ge(ve_made, n + 1)
                    nc.gpsimd.tensor_tensor(rstd[:, :], var_eps[:, :], half[:, :], ALU.pow).then_inc(rstd_made, 1)

                def split_context(n):
                    pool.wait_ge(ctx_landed, 16 * (n + 1))
                    wait(pool, v_job, TT * n)
                    for c in range(KC):
                        nc.gpsimd.tensor_tensor(ctx_hi[:, c, :], ctx_raw[:, c, :], ones[:, 0:1].to_broadcast([P, T]),
                                                ALU.mult).then_inc(ctxhi_made, 1)
                        pool.wait_ge(ctxhi_made, KC * n + c + 1)
                        nc.gpsimd.tensor_tensor(ctx_lo[:, c, :], ctx_raw[:, c, :], ctx_hi[:, c, :], ALU.subtract)\
                            .then_inc(ctx_made, 1)

                def split_output(b, g_):
                    G = NG * b + g_
                    pool.wait_ge(o_copied, G + 1)
                    if g_ == 0:
                        wait(pool, o_job, TT * b)
                        if ffn:
                            wait(pool, f1_done, FB * TT * b)
                    for part in range(2):
                        n_done = 2 * G + part + 1
                        cols = slice(T // 2 * part, T // 2 * (part + 1))
                        pool.wait_ge(sum_inverted, 2 * n_done)
                        nc.gpsimd.tensor_tensor(o_sb[:, cols], o_sb[:, cols], sum_sb[:, cols], ALU.mult)\
                            .then_inc(o_normed, 1)
                        pool.wait_ge(o_normed, n_done)
                        nc.gpsimd.tensor_tensor(o_sb[:, cols], o_sb[:, cols],
                                                qkv_bias[:, 2, g_:g_ + 1].to_broadcast([P, T // 2]), ALU.add)\
                            .then_inc(ob_made, 1)
                        pool.wait_ge(ob_made, n_done)
                        nc.gpsimd.tensor_tensor(oT[:, 0, g_, cols], o_sb[:, cols], ones[:, 0:1].to_broadcast([P, T // 2]),
                                                ALU.mult).then_inc(ohi_made, 1)
                        pool.wait_ge(ohi_made, n_done)
                        nc.gpsimd.tensor_tensor(oT[:, 1, g_, cols], o_sb[:, cols], oT[:, 0, g_, cols], ALU.subtract)\
                            .then_inc(o_made, 1)

                def residual_bias(b):
                    pool.wait_ge(xres_landed, 16 * (b + 1))
                    nc.gpsimd.tensor_tensor(xres[:, :, :], xres[:, :, :],
                                            bo_rows[:, :].unsqueeze(1).to_broadcast([P, TT, D]), ALU.add)\
                        .then_inc(xres_made, 1)

                def ffn_norms(b):
                    k = 5 * b
                    wait(pool, zround_made, 5 * (b - 1) + 1)
                    pool.wait_ge(meanvar2_made, TT * (b + 1))
                    var = meanvar[:, :, 1]
                    nc.gpsimd.tensor_tensor(var_eps[:, :], var, eps[:, :], ALU.add).then_inc(rms_step, 1)
                    pool.wait_ge(rms_step, k + 1)
                    nc.gpsimd.tensor_tensor(rstd[:, :], var_eps[:, :], half[:, :], ALU.pow).then_inc(rms_step, 1)
                    pool.wait_ge(rms_step, k + 2)
                    nc.gpsimd.tensor_tensor(rms[:, :], var, rstd[:, :], ALU.mult).then_inc(rms_step, 1)
                    pool.wait_ge(rms_step, k + 3)
                    nc.gpsimd.tensor_tensor(rms[:, :], rms[:, :], rstd[:, :], ALU.mult).then_inc(rms_step, 1)
                    pool.wait_ge(rms_step, k + 4)
                    nc.gpsimd.tensor_tensor(rms[:, :], rms[:, :], eps[:, :], ALU.add).then_inc(rms_step, 1)
                    pool.wait_ge(rms_step, k + 5)
                    nc.gpsimd.tensor_tensor(rms[:, :], rms[:, :], half[:, :], ALU.pow).then_inc(rms_made, 1)
                    pool.wait_ge(tern_made, N_F)
                    wait(pool, out_landed, 16 * b)
                    pool.wait_ge(x1_made, TT * (b + 1))
                    nc.gpsimd.tensor_tensor(xout[:, :, :], xres[:, :, :],
                                            b2_rows[:, :].unsqueeze(1).to_broadcast([P, TT, D]), ALU.add)\
                        .then_inc(xout_made, 1)
                    for t in range(TT):
                        col = slice(t, t + 1)
                        pool.wait_ge(gsum_made, TT * b + t + 1)
                        wait(pool, ground_made, 2 * (TT * b + t - 3) - 1)
                        nc.gpsimd.tensor_tensor(grms[:, col], gsum[:, col], inv_f[:, :], ALU.mult).then_inc(grms_step, 1)
                        pool.wait_ge(grms_step, 2 * (TT * b + t) + 1)
                        nc.gpsimd.tensor_tensor(grms[:, col], grms[:, col], eps[:, col], ALU.add).then_inc(grms_step, 1)
                        pool.wait_ge(grms_step, 2 * (TT * b + t) + 2)
                        nc.gpsimd.tensor_tensor(grms[:, col], grms[:, col], half[:, col], ALU.pow).then_inc(grms_made, 1)

                def body(b, n):
                    residual_bias(b)
                    if n is not None:
                        split_context(n)
                        inverse_std(n)
                    for g_ in range(NG):
                        split_output(b, g_)
                    if ffn:
                        ffn_norms(b)

                def prologue():
                    for i, value in enumerate((MASKED, -MS, 0.0)):
                        nc.gpsimd.memset(row_const[:, i, :], value).then_inc(row_consts, 1)
                    nc.gpsimd.memset(ident[:, :], 0.0).then_inc(consts, 1)
                    nc.gpsimd.memset(ones[:, :], 1.0).then_inc(consts, 1)
                    nc.gpsimd.memset(half[:, :], -0.5).then_inc(consts, 1)
                    nc.gpsimd.memset(eps[:, :], LN_EPS).then_inc(consts, 1)
                    pool.wait_ge(consts, 4)
                    nc.gpsimd.affine_select(out=ident[:, :], in_=ident[:, :], compare_op=ALU.not_equal,
                                            fill=1.0, base=0, pattern=[[-1, P]], channel_multiplier=1)\
                        .then_inc(consts, 1)
                    if ffn:
                        pool.wait_ge(consts, 5)
                        nc.gpsimd.tensor_copy(ident_bf[:, :], ident[:, :]).then_inc(consts, 1)
                        nc.gpsimd.memset(inv_f[:, :], 1.0 / F).then_inc(consts, 1)
                        pool.wait_ge(consts, 7)
                    inverse_std(0)
                    split_context(0)
                    pool.wait_ge(small_landed, 16 * N_SMALL)
                    pool.wait_ge(bias_scaled, 1)

                all_batches(pool, prologue, body)

        nc.clear_and_free_semaphores(sems)
        nc.all_engine_barrier()


def experts_phase(nc, x_io, idx_in, rw_in, gu_in, gub_in, dw_in, db_in, acc, gu_raw, x_landed, gu_landed):
    tag = "M_"
    sems = []
    NT = MT // P
    NB = MT // T
    GC = MI // P
    with ExitStack() as ctx:
        def sb(name, shape, dt):
            return ctx.enter_context(nc.sbuf_tensor(tag + name, shape, dt))

        def sem(name):
            sems.append(nc.alloc_semaphore(tag + name))
            return sems[-1]

        z = sb("z", [P, NT, D], F32)
        xT_hi = sb("xT_hi", [P, KC, MT], F16)
        xT_lo = sb("xT_lo", [P, KC, MT], F16)
        dw_raw = sb("dw_raw", [P, GC, D], F32)
        gu_hi = sb("gu_hi", [P, 2, KC, 2 * MI], F16)
        gu_lo = sb("gu_lo", [P, 2, KC, 2 * MI], F16)
        dw_hi = sb("dw_hi", [P, 2, GC, D], F16)
        dw_lo = sb("dw_lo", [P, 2, GC, D], F16)
        gub = sb("gub", [P, E, 2, GC], F32)
        db = sb("db", [E, D], F32)
        gate = sb("gate", [P, 2, T], F32)
        up = sb("up", [P, 2, T], F32)
        inter = sb("inter", [P, 2, T], F32)
        int_hi = sb("int_hi", [P, 2, GC, T], F16)
        int_lo = sb("int_lo", [P, 2, GC, T], F16)
        idx_i = sb("idx_i", [P, NT, 2], I32)
        idx_f = sb("idx_f", [P, NT, 2], F32)
        rw = sb("rw", [P, NT, E], F32)
        number = sb("number", [P, E], F32)
        named = sb("named", [P, NT, E], F32)
        cw = sb("cw", [P, NT, E], F32)
        cws = sb("cws", [P, NT, E], F32)
        cwT = sb("cwT", [E, MT], F32)
        ident = sb("ident", [P, P], F32)
        half = sb("half", [P, NT], F32)
        eps = sb("eps", [P, NT], F32)
        stats = sb("stats", [P, NT, 6], F32)
        meanvar = sb("meanvar", [P, NT, 2], F32)
        rstd = sb("rstd", [P, NT], F32)
        bank = [ctx.enter_context(nc.psum_tensor(f"{tag}bank{i}", [P, 512], F32)) for i in range(8)]

        small_landed, dw_landed, out_landed = sem("small_landed"), sem("dw_landed"), sem("out_landed")
        consts, stats_made, meanvar_made, z_made = sem("consts"), sem("stats_made"), sem("meanvar_made"), sem("z_made")
        rstd_step = sem("rstd_step")
        xT_job, xhi_made, xlo_made = sem("xT_job"), sem("xhi_made"), sem("xlo_made")
        cw_step, cwT_job, cwT_made, bias_job, acc_made = sem("cw_step"), sem("cwT_job"), sem("cwT_made"), sem("bias_job"), sem("acc_made")
        guhi_made, gulo_made, dwhi_made, dwlo_made = sem("guhi_made"), sem("gulo_made"), sem("dwhi_made"), sem("dwlo_made")
        gu_job, down_job = sem("gu_job"), sem("down_job")
        gate_made, glu_made, upa_made, up_made = sem("gate_made"), sem("glu_made"), sem("upa_made"), sem("up_made")
        inter_made, ihi_made, ilo_made, gub_made = sem("inter_made"), sem("ihi_made"), sem("ilo_made"), sem("gub_made")
        x_view = x_io[0:NB, :, :].rearrange("b (t p) d -> p (b t) d", p=P)
        STEPS = E * NB * GC

        with nc.Block() as block:
            @block.sync
            def _(sp):
                for e in range(E):
                    if e > 0:
                        sp.wait_ge(gulo_made, e)
                        sp.dma_start(gu_raw[:, :, :], gu_in[e].rearrange("(c p) n -> p c n", p=P))\
                          .then_inc(gu_landed, 16)
                    if e == 0:
                        sp.dma_start(idx_i[:, :, :], idx_in.rearrange("(t p) k -> p t k", p=P)).then_inc(small_landed, 16)
                        sp.dma_start(rw[:, :, :], rw_in.rearrange("(t p) e -> p t e", p=P)).then_inc(small_landed, 16)
                        sp.dma_start(gub[:, :, :, :], gub_in).then_inc(small_landed, 16)
                        sp.dma_start(db[:, :], db_in).then_inc(small_landed, 16)
                    wait(sp, dwlo_made, e)
                    sp.dma_start(dw_raw[:, :, :], dw_in[e].rearrange("(c p) n -> p c n", p=P)).then_inc(dw_landed, 16)
                for t in range(NT):
                    sp.wait_ge(acc_made, NT + NT * (E - 1) + t + 1)
                    sp.dma_start(x_view[:, t, :], acc[:, t, :]).then_inc(out_landed, 16)
                sp.wait_ge(out_landed, 16 * NT)

            @block.gpsimd
            def _(pool):
                nc.gpsimd.memset(ident[:, :], 0.0).then_inc(consts, 1)
                nc.gpsimd.memset(half[:, :], -0.5).then_inc(consts, 1)
                nc.gpsimd.memset(eps[:, :], LN_EPS).then_inc(consts, 1)
                for e in range(E):
                    nc.gpsimd.memset(number[:, e:e + 1], float(e)).then_inc(consts, 1)
                pool.wait_ge(consts, 3 + E)
                nc.gpsimd.affine_select(out=ident[:, :], in_=ident[:, :], compare_op=ALU.not_equal, fill=1.0, base=0,
                                        pattern=[[-1, P]], channel_multiplier=1).then_inc(consts, 1)
                for nb in range(NB):
                    tiles = slice(TT * nb, TT * nb + TT)
                    pool.wait_ge(meanvar_made, TT * (nb + 1))
                    nc.gpsimd.tensor_tensor(rstd[:, tiles], meanvar[:, tiles, 1], eps[:, tiles], ALU.add)\
                        .then_inc(rstd_step, 1)
                    pool.wait_ge(rstd_step, 2 * nb + 1)
                    nc.gpsimd.tensor_tensor(rstd[:, tiles], rstd[:, tiles], half[:, tiles], ALU.pow)\
                        .then_inc(rstd_step, 1)

            @block.tensor
            def _(pe):
                pe.wait_ge(consts, 4 + E)

                def transpose_x(nb):
                    pe.wait_ge(z_made, TT * (nb + 1))
                    for j in range(KC * nb, KC * nb + KC):
                        c = j % KC
                        for t in range(TT):
                            last = nc.tensor.matmul(bank[j][:, P * t:P * t + P], z[:, TT * nb + t, P * c:P * c + P],
                                                    ident[:, :], is_transpose=True, start=True, stop=True)
                        last.then_inc(xT_job, 1)

                def transpose_weights():
                    pe.wait_ge(xlo_made, NB * KC)
                    pe.wait_ge(cw_step, 5)
                    for t in range(NT):
                        last = nc.tensor.matmul(bank[4 + t // 4][0:E, P * (t % 4):P * (t % 4) + P], cw[:, t, :],
                                                ident[:, :], is_transpose=True, start=True, stop=True)
                    last.then_inc(cwT_job, 1)

                def output_biases():
                    pe.wait_ge(cwT_made, 2)
                    for t in range(NT):
                        wait(pe, acc_made, t - 1)
                        nc.tensor.matmul(bank[6 + t % 2][:, :], cwT[:, P * t:P * t + P], db[:, :], start=True, stop=True)\
                            .then_inc(bias_job, 1)

                def product(out, lhs_hi, lhs_lo, rhs_hi, rhs_lo):
                    for c in range(KC):
                        nc.tensor.matmul(out, lhs_hi(c), rhs_hi(c), start=(c == 0), stop=False)
                        nc.tensor.matmul(out, lhs_hi(c), rhs_lo(c), start=False, stop=False)
                        last = nc.tensor.matmul(out, lhs_lo(c), rhs_hi(c), start=False, stop=(c == KC - 1))
                    return last

                def down(e, nb):
                    pe.wait_ge(ilo_made, (e * NB + nb + 1) * GC)
                    pe.wait_ge(dwlo_made, e + 1)
                    for t in range(TT):
                        job = (e * NB + nb) * TT + t
                        pe.wait_ge(acc_made, NT + job - 1)
                        product(bank[6 + t % 2][:, :],
                                lambda k: int_hi[:, nb, k, P * t:P * t + P], lambda k: int_lo[:, nb, k, P * t:P * t + P],
                                lambda k: dw_hi[:, e % 2, k, :], lambda k: dw_lo[:, e % 2, k, :]).then_inc(down_job, 1)

                transpose_x(0)
                for e in range(E):
                    pe.wait_ge(gulo_made, e + 1)
                    for nb in range(NB):
                        if e == 0:
                            pe.wait_ge(xlo_made, KC * (nb + 1))
                        for f in range(GC):
                            step = (e * NB + nb) * GC + f
                            if step == 1:
                                transpose_x(1)
                            if step == 2:
                                transpose_weights()
                            if step == 3:
                                output_biases()
                            for u in range(2):
                                if u == 0:
                                    wait(pe, gate_made, step - 1)
                                else:
                                    wait(pe, upa_made, step - 1)
                                cols = slice(MI * u + P * f, MI * u + P * f + P)
                                toks = slice(T * nb, T * nb + T)
                                product(bank[2 * (step % 2) + u][:, :],
                                        lambda k: gu_hi[:, e % 2, k, cols], lambda k: gu_lo[:, e % 2, k, cols],
                                        lambda k: xT_hi[:, k, toks], lambda k: xT_lo[:, k, toks]).then_inc(gu_job, 1)
                        if (e, nb) != (0, 0):
                            down(*divmod(e * NB + nb - 1, NB))
                down(E - 1, NB - 1)

            def split_gu_hi(e):
                wait(nc.scalar, down_job, NT * (e - 1))
                nc.scalar.wait_ge(gu_landed, 16 * (e + 1))
                nc.scalar.activation(gu_hi[:, e % 2, :, :], gu_raw[:, :, :], ACT.Copy, scale=WS).then_inc(guhi_made, 1)

            def split_dw_hi(e):
                wait(nc.scalar, down_job, NT * (e - 1))
                nc.scalar.wait_ge(dw_landed, 16 * (e + 1))
                nc.scalar.activation(dw_hi[:, e % 2, :, :], dw_raw[:, :, :], ACT.Copy, scale=WS).then_inc(dwhi_made, 1)

            @block.scalar
            def _(act):
                def hi_parts(nb):
                    for j in range(KC * nb, KC * nb + KC):
                        act.wait_ge(xT_job, j + 1)
                        nc.scalar.activation(xT_hi[:, j % KC, T * nb:T * nb + T], bank[j][:, :], ACT.Copy)\
                            .then_inc(xhi_made, 1)

                split_gu_hi(0)
                hi_parts(0)
                act.wait_ge(small_landed, 64)
                nc.scalar.activation(gub[:, :, :, :], gub[:, :, :, :], ACT.Copy, scale=WS).then_inc(gub_made, 1)
                for step in range(STEPS):
                    e, r = divmod(step, NB * GC)
                    nb, f = divmod(r, GC)
                    if step == 1:
                        hi_parts(1)
                    if step == 2:
                        act.wait_ge(cwT_job, 1)
                        for i in range(2):
                            nc.scalar.activation(cwT[:, T * i:T * i + T], bank[4 + i][0:E, :], ACT.Copy)\
                                .then_inc(cwT_made, 1)
                    if step == 3:
                        split_dw_hi(0)
                    act.wait_ge(gate_made, step + 1)
                    nc.scalar.activation(gate[:, step % 2, :], gate[:, step % 2, :], ACT.Gelu_apprx_sigmoid,
                                         scale=1.0 / WS).then_inc(glu_made, 1)
                    act.wait_ge(inter_made, step + 1)
                    if f == 0:
                        wait(act, down_job, TT * (e * NB + nb - 1))
                    nc.scalar.activation(int_hi[:, nb, f, :], inter[:, step % 2, :], ACT.Copy).then_inc(ihi_made, 1)
                    if nb == 1 and f == 0 and e + 1 < E:
                        split_gu_hi(e + 1)
                    if nb == 0 and f == 0 and e > 0:
                        split_dw_hi(e)

            @block.vector
            def _(dve):
                def normalise(nb):
                    dve.wait_ge(x_landed[nb], 16)
                    tiles = range(TT * nb, TT * nb + TT)
                    for t in tiles:
                        nc.vector.bn_stats(stats[:, t, :], acc[:, t, :]).then_inc(stats_made, 1)
                    dve.wait_ge(stats_made, TT * (nb + 1))
                    for t in tiles:
                        nc.vector.bn_aggr(meanvar[:, t, :], stats[:, t, :]).then_inc(meanvar_made, 1)
                    dve.wait_ge(meanvar_made, TT * (nb + 1))
                    dve.wait_ge(rstd_step, 2 * (nb + 1))
                    for t in tiles:
                        nc.vector.tensor_scalar(z[:, t, :], acc[:, t, :], meanvar[:, t, 0:1], rstd[:, t:t + 1],
                                                ALU.subtract, ALU.mult).then_inc(z_made, 1)

                def lo_parts(nb):
                    for j in range(KC * nb, KC * nb + KC):
                        c = j % KC
                        dve.wait_ge(xhi_made, j + 1)
                        nc.vector.tensor_tensor(xT_lo[:, c, T * nb:T * nb + T], bank[j][:, :],
                                                xT_hi[:, c, T * nb:T * nb + T], ALU.subtract).then_inc(xlo_made, 1)

                def split_gu_lo(e):
                    dve.wait_ge(guhi_made, e + 1)
                    nc.vector.scalar_tensor_tensor(gu_lo[:, e % 2, :, :].rearrange("p c n -> p (c n)"),
                                                   gu_raw[:, :, :].rearrange("p c n -> p (c n)"), WS,
                                                   gu_hi[:, e % 2, :, :].rearrange("p c n -> p (c n)"),
                                                   ALU.mult, ALU.subtract).then_inc(gulo_made, 1)

                def split_dw_lo(e):
                    dve.wait_ge(dwhi_made, e + 1)
                    nc.vector.scalar_tensor_tensor(dw_lo[:, e % 2, :, :].rearrange("p c n -> p (c n)"),
                                                   dw_raw[:, :, :].rearrange("p c n -> p (c n)"), WS,
                                                   dw_hi[:, e % 2, :, :].rearrange("p c n -> p (c n)"),
                                                   ALU.mult, ALU.subtract).then_inc(dwlo_made, 1)

                normalise(0)
                split_gu_lo(0)
                lo_parts(0)
                normalise(1)
                dve.wait_ge(small_landed, 64)
                dve.wait_ge(consts, 3 + E)
                nc.vector.tensor_copy(idx_f[:, :, :], idx_i[:, :, :]).then_inc(cw_step, 1)
                dve.wait_ge(cw_step, 1)
                every = number[:, :].unsqueeze(1).to_broadcast([P, NT, E])
                nc.vector.tensor_tensor(named[:, :, :], every, idx_f[:, :, 0:1].to_broadcast([P, NT, E]), ALU.is_equal)\
                    .then_inc(cw_step, 1)
                nc.vector.tensor_tensor(cw[:, :, :], every, idx_f[:, :, 1:2].to_broadcast([P, NT, E]), ALU.is_equal)\
                    .then_inc(cw_step, 1)
                dve.wait_ge(cw_step, 3)
                nc.vector.tensor_tensor(named[:, :, :], named[:, :, :], cw[:, :, :], ALU.add).then_inc(cw_step, 1)
                dve.wait_ge(cw_step, 4)
                nc.vector.tensor_tensor(cw[:, :, :], named[:, :, :], rw[:, :, :], ALU.mult).then_inc(cw_step, 1)
                dve.wait_ge(cw_step, 5)
                nc.vector.tensor_scalar(cws[:, :, :], cw[:, :, :], 1.0 / WS ** 2, None, ALU.mult).then_inc(cw_step, 1)
                dve.wait_ge(cw_step, 6)

                dve.wait_ge(gub_made, 1)

                def accumulate(e, nb):
                    for t in range(TT):
                        job = (e * NB + nb) * TT + t
                        tile = TT * nb + t
                        dve.wait_ge(down_job, job + 1)
                        dve.wait_ge(acc_made, NT + job - NT + 1)
                        nc.vector.scalar_tensor_tensor(acc[:, tile, :], bank[6 + t % 2][:, :], cws[:, tile, e:e + 1],
                                                       acc[:, tile, :], ALU.mult, ALU.add).then_inc(acc_made, 1)

                for step in range(STEPS):
                    e, r = divmod(step, NB * GC)
                    nb, f = divmod(r, GC)
                    s = step % 2
                    if step == 1:
                        lo_parts(1)
                    if step == 3:
                        for t in range(NT):
                            dve.wait_ge(bias_job, t + 1)
                            nc.vector.tensor_tensor(acc[:, t, :], bank[6 + t % 2][:, :], acc[:, t, :], ALU.add)\
                                .then_inc(acc_made, 1)
                        split_dw_lo(0)
                    dve.wait_ge(gu_job, 2 * step + 1)
                    wait(dve, inter_made, step - 1)
                    nc.vector.tensor_scalar(gate[:, s, :], bank[2 * s][:, :], gub[:, e, 0, f:f + 1], 7.0 * WS,
                                            ALU.add, ALU.min).then_inc(gate_made, 1)
                    dve.wait_ge(gu_job, 2 * step + 2)
                    nc.vector.tensor_scalar(up[:, s, :], bank[2 * s + 1][:, :], gub[:, e, 1, f:f + 1], 7.0 * WS,
                                            ALU.add, ALU.min).then_inc(upa_made, 1)
                    dve.wait_ge(upa_made, step + 1)
                    nc.vector.tensor_scalar(up[:, s, :], up[:, s, :], -7.0 * WS, WS, ALU.max, ALU.add)\
                        .then_inc(up_made, 1)
                    dve.wait_ge(up_made, step + 1)
                    dve.wait_ge(glu_made, step + 1)
                    wait(dve, ihi_made, step - 1)
                    wait(dve, ilo_made, step - 1)
                    nc.vector.tensor_tensor(inter[:, s, :], up[:, s, :], gate[:, s, :], ALU.mult).then_inc(inter_made, 1)
                    dve.wait_ge(ihi_made, step + 1)
                    nc.vector.tensor_tensor(int_lo[:, nb, f, :], inter[:, s, :], int_hi[:, nb, f, :], ALU.subtract)\
                        .then_inc(ilo_made, 1)
                    if nb == 1 and f == 1 and e + 1 < E:
                        split_gu_lo(e + 1)
                    if nb == 0 and f == 1 and e > 0:
                        split_dw_lo(e)
                    if f == GC - 1 and (e, nb) != (0, 0):
                        accumulate(*divmod(e * NB + nb - 1, NB))
                accumulate(E - 1, NB - 1)


def program(nc, a, out):
    mid = nc.dram_tensor("x_after_ffn", (B, T, D), F32, kind="Internal").ap()
    encoder_phase(nc, 0, a["x"], a["ctxT"], mid, a["w0"], a["b0"], a["bo0"], None,
                  (a["w1T"], a["w2T"], a["b1"], a["b2"]))
    with ExitStack() as ctx:
        acc = ctx.enter_context(nc.sbuf_tensor("acc", [P, MT // P, D], F32))
        gu_raw = ctx.enter_context(nc.sbuf_tensor("gu_raw", [P, KC, 2 * MI], F32))
        x_landed = [nc.alloc_semaphore(f"x_landed{nb}") for nb in range(MT // T)]
        gu_landed = nc.alloc_semaphore("gu_landed")

        def load_ahead(sp):
            for nb in range(MT // T):
                sp.dma_start(acc[:, TT * nb:TT * nb + TT, :], out[nb].rearrange("(t p) d -> p t d", p=P))\
                  .then_inc(x_landed[nb], 16)
                if nb == 0:
                    sp.dma_start(gu_raw[:, :, :], a["gu"][0].rearrange("(c p) n -> p c n", p=P)).then_inc(gu_landed, 16)

        encoder_phase(nc, 1, mid, a["ctxT"], out, a["w1"], a["b1q"], a["bo1"], a["mask"], None, load_ahead)
        experts_phase(nc, out, a["idx"], a["rw"], a["gu"], a["gub"], a["dw"], a["db"], acc, gu_raw, x_landed, gu_landed)


def kernel(**inputs):
    import numpy as np
    import concourse.bacc as bacc
    from concourse import mybir as _mybir
    from concourse.bass_utils import run_bass_kernel_spmd

    i = {k: np.asarray(v) for k, v in inputs.items()}
    by_feature = lambda w: w.reshape(w.shape[:-1] + (KC, HG, DK)).swapaxes(-1, -2).reshape(w.shape)
    per_partition = lambda *bs: np.ascontiguousarray(np.stack([b.reshape(KC, P).T for b in bs], 1))
    gu = i["L1_ffn_gate_up_proj"].reshape(E, D, MI, 2).transpose(0, 1, 3, 2).reshape(E, D, 2 * MI)
    gub = i["L1_ffn_gate_up_proj_bias"].reshape(E, MI // P, P, 2).transpose(2, 0, 3, 1)
    arrays = {
        "x": i["x"],
        "ctxT": i["ctx_1024"].transpose(0, 2, 1),
        "mask": i["mask_BxS2_bk0"].reshape(1, B * T),
        "w0": np.stack([by_feature(i[f"L0_xattn_W_{n}"]) for n in "QK"] + [i[f"L0_xattn_W_{n}"] for n in "VO"]),
        "b0": per_partition(*[by_feature(i[f"L0_xattn_b_{n}"]) for n in "QK"], i["L0_xattn_b_V"]),
        "bo0": i["L0_xattn_b_O"],
        "w1T": i["L0_ffn_w1"].T, "b1": i["L0_ffn_b1"],
        "w2T": i["L0_ffn_w2"].T, "b2": i["L0_ffn_b2"],
        "w1": np.stack([by_feature(i[f"L1_xattn_W{n}"].T) for n in "qk"] + [i[f"L1_xattn_W{n}"].T for n in "vo"]),
        "b1q": per_partition(*[by_feature(i[f"L1_xattn_b{n}"]) for n in "qk"], i["L1_xattn_bv"]),
        "bo1": i["L1_xattn_bo"],
        "idx": i["L1_ffn_router_indices"],
        "rw": i["L1_ffn_routing_weights"],
        "gu": gu, "gub": gub,
        "dw": i["L1_ffn_down_proj"], "db": i["L1_ffn_down_proj_bias"],
    }
    arrays = {k: np.ascontiguousarray(v) for k, v in arrays.items()}
    nc = bacc.Bacc("TRN2", target_bir_lowering=False, num_devices=1, dynamic_dma_scratch_size=1024)
    aps = {k: nc.dram_tensor("in_" + k, v.shape, _mybir.dt.from_np(v.dtype), kind="ExternalInput").ap()
           for k, v in arrays.items()}
    out = nc.dram_tensor("out", (B, T, D), _mybir.dt.float32, kind="ExternalOutput").ap()
    program(nc, aps, out)
    r = run_bass_kernel_spmd(nc, [{"in_" + k: v for k, v in arrays.items()}], core_ids=[0])
    return r.results[0]["out"]
```
